# Optimizing a Trainium2 kernel written in Bass

```python
import numpy as np
import jax
import jax.numpy as jnp

def _softmax(x, axis=-1):
    return jax.nn.softmax(x, axis=axis)

def _gelu(x):
    return jax.nn.gelu(x, approximate=True)

def _silu(x):
    return jax.nn.silu(x)

def _sigmoid(x):
    return jax.nn.sigmoid(x)

def _layernorm(x, axis=-1, eps=1e-05):
    m = jnp.mean(x, axis=axis, keepdims=True)
    v = jnp.var(x, axis=axis, keepdims=True)
    return (x - m) / jnp.sqrt(v + eps)

def _scatter_add(tgt, idx, src, axis=0):
    return tgt.at[idx].add(src)

def _segment_sum(src, seg, n):
    return jax.ops.segment_sum(src, seg, n)
kernel_name = 'mk_macaron_d4_jaxref_r8_188735'

def setup_inputs(seed: int=0):
    np.random.seed(seed)
    _w = jnp.asarray

    def _L0_attn_setup():
        import jax, jax.numpy as jnp
        import numpy as np
        EPS = 1e-08

        def rmsnorm(x, w):
            norm = jax.lax.rsqrt(jnp.mean(x * x, axis=-1, keepdims=True) + EPS)
            return x * norm * w
        key = jax.random.key(seed)
        ks = jax.random.split(key, 10)
        B, L, D, S = (8, 512, 128, 32)
        sD = 1.0 / np.sqrt(D)
        sS = 1.0 / np.sqrt(S)
        return {'x': jax.random.normal(ks[0], (B, L, D), jnp.float32), 'w_norm': jnp.ones((D,), jnp.float32), 'W_in': jax.random.normal(ks[1], (D, 3 * S), jnp.float32) * sD, 'b_in': jnp.zeros((3 * S,), jnp.float32), 'W_x': jax.random.normal(ks[2], (S, S), jnp.float32) * sS, 'b_x': jnp.zeros((S,), jnp.float32), 'W_dt': jax.random.normal(ks[3], (S, S), jnp.float32) * sS, 'b_dt': jnp.zeros((S,), jnp.float32), 'W_out': jax.random.normal(ks[4], (S, D), jnp.float32) * sS, 'b_out': jnp.zeros((D,), jnp.float32)}
    _L0_attn_in = _L0_attn_setup()

    def _L0_ffn_setup():
        import jax, jax.numpy as jnp
        import numpy as np
        DIM = 128

        def _reference_tuple_inner(x, W_r, W_k, W_v, mu_r, mu_k):
            B, T, C = x.shape
            x_prev = jnp.concatenate([jnp.zeros((B, 1, C), x.dtype), x[:, :-1, :]], axis=1)
            xr = mu_r * x + (1.0 - mu_r) * x_prev
            xk = mu_k * x + (1.0 - mu_k) * x_prev
            r = jax.nn.sigmoid(jnp.einsum('btc,dc->btd', xr, W_r))
            k = jnp.einsum('btc,dc->btd', xk, W_k)
            k_act = jnp.square(jax.nn.relu(k))
            out = r * jnp.einsum('btc,dc->btd', k_act, W_v)
            new_state = x[:, -1, :]
            return (out, new_state)
        key = jax.random.key(seed)
        ks = jax.random.split(key, 6)
        B, T, C = (8, 256, DIM)
        x = jax.random.normal(ks[0], (B, T, C), dtype=jnp.float32)
        s = 1.0 / np.sqrt(C)
        W_r = jax.random.uniform(ks[1], (C, C), jnp.float32, -s, s)
        W_k = jax.random.uniform(ks[2], (C, C), jnp.float32, -s, s)
        W_v = jax.random.uniform(ks[3], (C, C), jnp.float32, -s, s)
        mu_r = jax.random.uniform(ks[4], (C,), jnp.float32)
        mu_k = jax.random.uniform(ks[5], (C,), jnp.float32)
        return {'x': x, 'W_r': W_r, 'W_k': W_k, 'W_v': W_v, 'mu_r': mu_r, 'mu_k': mu_k}
    _L0_ffn_in = _L0_ffn_setup()

    def _L1_attn_setup():
        import jax, jax.numpy as jnp
        import numpy as np
        D_MODEL = 128
        D_INNER = 256
        D_STATE = 16
        D_CONV = 4
        DT_RANK = 64
        BATCH = 2
        SEQ = 128
        LN_EPS = 1e-05

        def _mk_layer(key):
            k = jax.random.split(key, 5)
            return {'in_proj': jax.random.normal(k[0], (2 * D_INNER, D_MODEL)) * 0.02, 'conv_w': jax.random.normal(k[1], (D_INNER, 1, D_CONV)) * 0.2, 'conv_b': jnp.zeros((D_INNER,)), 'x_proj': jax.random.normal(k[2], (DT_RANK + 2 * D_STATE, D_INNER)) * 0.02, 'dt_w': jax.random.normal(k[3], (D_INNER, DT_RANK)) * 0.02, 'dt_b': jnp.full((D_INNER,), -4.6), 'A_log': jnp.log(jnp.tile(jnp.arange(1.0, D_STATE + 1.0), (D_INNER, 1))), 'D': jnp.ones((D_INNER,)), 'out_proj': jax.random.normal(k[4], (D_MODEL, D_INNER)) * 0.02}

        def _mamba(x, in_proj, conv_w, conv_b, x_proj, dt_w, dt_b, A_log, Dp, out_proj):
            Bb, L, _ = x.shape
            xz = jnp.einsum('bld,ed->ble', x, in_proj)
            xi, z = jnp.split(xz, 2, axis=-1)
            xc = jnp.transpose(xi, (0, 2, 1))
            xc = jax.lax.conv_general_dilated(xc, conv_w, (1,), [(D_CONV - 1, 0)], dimension_numbers=('NCH', 'OIH', 'NCH'), feature_group_count=D_INNER)
            xc = xc + conv_b[None, :, None]
            xi = jax.nn.silu(jnp.transpose(xc, (0, 2, 1)))
            dbc = jnp.einsum('bld,ed->ble', xi, x_proj)
            dt, Bm, Cm = jnp.split(dbc, [DT_RANK, DT_RANK + D_STATE], axis=-1)
            dt = jax.nn.softplus(jnp.einsum('blr,dr->bld', dt, dt_w) + dt_b)
            A = -jnp.exp(A_log)
            dA = jnp.exp(dt[..., None] * A)
            dBx = (dt * xi)[..., None] * Bm[:, :, None, :]

            def step(h, inp):
                a, bx, c = inp
                h = a * h + bx
                return (h, jnp.einsum('bds,bs->bd', h, c))
            h0 = jnp.zeros((Bb, D_INNER, D_STATE), x.dtype)
            _, ys = jax.lax.scan(step, h0, (jnp.moveaxis(dA, 1, 0), jnp.moveaxis(dBx, 1, 0), jnp.moveaxis(Cm, 1, 0)))
            y = jnp.moveaxis(ys, 0, 1) + xi * Dp
            y = y * jax.nn.silu(z)
            return jnp.einsum('ble,de->bld', y, out_proj)
        key = jax.random.key(seed)
        kx, kf, kb = jax.random.split(key, 3)
        inp = {'x': jax.random.normal(kx, (BATCH, SEQ, D_MODEL), jnp.float32)}
        for pref, kk in (('f_', kf), ('b_', kb)):
            for name, v in _mk_layer(kk).items():
                inp[pref + name] = v
        inp['ln_g'] = jnp.ones((D_MODEL,))
        inp['ln_b'] = jnp.zeros((D_MODEL,))
        return inp
    _L1_attn_in = _L1_attn_setup()

    def _L1_ffn_setup():
        import jax, jax.numpy as jnp
        import numpy as np
        B, S, D = (4, 256, 128)
        E = 8
        CF = 1
        key = jax.random.key(seed)
        k_x, k_g, k_w, k_b = jax.random.split(key, 4)
        x = jax.random.normal(k_x, (B, S, D), dtype=jnp.float32)
        Wg = jax.random.normal(k_g, (D, E), dtype=jnp.float32) * (1.0 / np.sqrt(D))
        We = jax.random.normal(k_w, (D, D), dtype=jnp.float32) * (1.0 / np.sqrt(D))
        be = jax.random.normal(k_b, (D,), dtype=jnp.float32) * 0.01
        return {'x': x, 'Wg': Wg, 'We': We, 'be': be}
    _L1_ffn_in = _L1_ffn_setup()

    def _L2_attn_setup():
        import jax, jax.numpy as jnp
        import numpy as np
        HEADS = 16
        EPS = 1e-08

        def _attention(x, Wq, Wkv, Wo, heads=HEADS, causal=True, eps=EPS):
            B, N, D = x.shape
            dh = D // heads
            q = x @ Wq.T
            k, v = jnp.split(x @ Wkv.T, 2, axis=-1)

            def split_heads(t):
                return t.reshape(B, N, heads, dh).transpose(0, 2, 1, 3)
            q, k, v = map(split_heads, (q, k, v))
            q = q * dh ** (-0.5)
            sim = jnp.einsum('bhid,bhjd->bhij', q, k)
            mask_value = -jnp.finfo(sim.dtype).max
            if causal:
                causal_mask = jnp.triu(jnp.ones((N, N), dtype=bool), 1)
                sim = jnp.where(causal_mask, mask_value, sim)
            m = jax.lax.stop_gradient(jnp.max(sim, axis=-1, keepdims=True))
            e = jnp.exp(sim - m)
            num = jnp.einsum('bhij,bhjd->bhid', e, v)
            den = jnp.sum(e, axis=-1, keepdims=True) + eps
            out = num / den
            out = out.transpose(0, 2, 1, 3).reshape(B, N, D)
            return out @ Wo.T
        key = jax.random.key(seed)
        k0, k1, k2, k3 = jax.random.split(key, 4)
        B, N, D = (2, 256, 128)
        x = jax.random.normal(k0, (B, N, D), jnp.float32)
        Wq = jax.random.normal(k1, (D, D), jnp.float32) * 0.02
        Wkv = jax.random.normal(k2, (2 * D, D), jnp.float32) * 0.02
        Wo = jax.random.normal(k3, (D, D), jnp.float32) * 0.02
        return {'x': x, 'Wq': Wq, 'Wkv': Wkv, 'Wo': Wo}
    _L2_attn_in = _L2_attn_setup()

    def _L2_ffn_setup():
        import jax, jax.numpy as jnp
        import numpy as np
        B, S, D = (2, 256, 128)
        E, K, F = (16, 2, 64)
        FS = 128
        key = jax.random.key(seed)
        ks = jax.random.split(key, 8)

        def w(k, shape, fan_in):
            return jax.random.normal(k, shape, jnp.float32) / np.sqrt(fan_in).astype(np.float32)
        return {'x': jax.random.normal(ks[0], (B, S, D), jnp.float32), 'Wr': w(ks[1], (D, E), D), 'Wg': w(ks[2], (E, D, F), D), 'Wu': w(ks[3], (E, D, F), D), 'Wd': w(ks[4], (E, F, D), F), 'Sg': w(ks[5], (D, FS), D), 'Su': w(ks[6], (D, FS), D), 'Sd': w(ks[7], (FS, D), FS)}
    _L2_ffn_in = _L2_ffn_setup()

    def _L3_attn_setup():
        import jax, jax.numpy as jnp
        import numpy as np
        D_MODEL = 128
        N_HEADS = 16
        D_HEAD = D_MODEL // N_HEADS

        def _rmsnorm(x, w):
            xf = x.astype(jnp.float32)
            rms = jnp.mean(xf * xf, axis=-1, keepdims=True)
            return (xf / jnp.sqrt(rms + 1e-06) * w.astype(jnp.float32)).astype(x.dtype)
        key = jax.random.key(seed)
        ks = jax.random.split(key, 7)
        x = jax.random.normal(ks[0], (1, 512, D_MODEL), dtype=jnp.float32)
        Wqkv = jax.random.normal(ks[1], (3 * D_MODEL, D_MODEL), dtype=jnp.float32) * (1.0 / np.sqrt(D_MODEL))
        bqkv = jax.random.normal(ks[2], (3 * D_MODEL,), dtype=jnp.float32) * 0.01
        Wo = jax.random.normal(ks[3], (D_MODEL, D_MODEL), dtype=jnp.float32) * (1.0 / np.sqrt(D_MODEL))
        bo = jax.random.normal(ks[4], (D_MODEL,), dtype=jnp.float32) * 0.01
        wq = jnp.ones((D_HEAD,), dtype=jnp.float32)
        wk = jnp.ones((D_HEAD,), dtype=jnp.float32)
        return {'x': x, 'Wqkv': Wqkv, 'bqkv': bqkv, 'Wo': Wo, 'bo': bo, 'wq': wq, 'wk': wk}
    _L3_attn_in = _L3_attn_setup()

    def _L3_ffn_setup():
        import jax, jax.numpy as jnp
        import numpy as np
        B, S, D, E, K = (4, 256, 128, 8, 2)
        EPS, W_THRES, TEMP = (0.0001, 0.1, 1.0)
        key = jax.random.key(seed)
        k1, k2, k3, k4, k5 = jax.random.split(key, 5)
        x = jax.random.normal(k1, (B, S, D), dtype=jnp.float32)
        gate_W = jax.random.normal(k2, (D, E), dtype=jnp.float32) * 0.02
        gate_b = jnp.zeros((E,), dtype=jnp.float32)
        expert_W = jax.random.normal(k3, (E, D, D), dtype=jnp.float32) * 0.02
        expert_b = jnp.zeros((E, D), dtype=jnp.float32)
        return {'x': x, 'gate_W': gate_W, 'gate_b': gate_b, 'expert_W': expert_W, 'expert_b': expert_b}
    _L3_ffn_in = _L3_ffn_setup()
    _d = {'L0_attn_x': _L0_attn_in['x'], 'L0_attn_w_norm': _L0_attn_in['w_norm'], 'L0_attn_W_in': _L0_attn_in['W_in'], 'L0_attn_b_in': _L0_attn_in['b_in'], 'L0_attn_W_x': _L0_attn_in['W_x'], 'L0_attn_b_x': _L0_attn_in['b_x'], 'L0_attn_W_dt': _L0_attn_in['W_dt'], 'L0_attn_b_dt': _L0_attn_in['b_dt'], 'L0_attn_W_out': _L0_attn_in['W_out'], 'L0_attn_b_out': _L0_attn_in['b_out'], 'L0_ffn_W_r': _L0_ffn_in['W_r'], 'L0_ffn_W_k': _L0_ffn_in['W_k'], 'L0_ffn_W_v': _L0_ffn_in['W_v'], 'L0_ffn_mu_r': _L0_ffn_in['mu_r'], 'L0_ffn_mu_k': _L0_ffn_in['mu_k'], 'L1_attn_f_in_proj': _L1_attn_in['f_in_proj'], 'L1_attn_f_conv_w': _L1_attn_in['f_conv_w'], 'L1_attn_f_conv_b': _L1_attn_in['f_conv_b'], 'L1_attn_f_x_proj': _L1_attn_in['f_x_proj'], 'L1_attn_f_dt_w': _L1_attn_in['f_dt_w'], 'L1_attn_f_dt_b': _L1_attn_in['f_dt_b'], 'L1_attn_f_A_log': _L1_attn_in['f_A_log'], 'L1_attn_f_D': _L1_attn_in['f_D'], 'L1_attn_f_out_proj': _L1_attn_in['f_out_proj'], 'L1_attn_b_in_proj': _L1_attn_in['b_in_proj'], 'L1_attn_b_conv_w': _L1_attn_in['b_conv_w'], 'L1_attn_b_conv_b': _L1_attn_in['b_conv_b'], 'L1_attn_b_x_proj': _L1_attn_in['b_x_proj'], 'L1_attn_b_dt_w': _L1_attn_in['b_dt_w'], 'L1_attn_b_dt_b': _L1_attn_in['b_dt_b'], 'L1_attn_b_A_log': _L1_attn_in['b_A_log'], 'L1_attn_b_D': _L1_attn_in['b_D'], 'L1_attn_b_out_proj': _L1_attn_in['b_out_proj'], 'L1_attn_ln_g': _L1_attn_in['ln_g'], 'L1_attn_ln_b': _L1_attn_in['ln_b'], 'L1_ffn_Wg': _L1_ffn_in['Wg'], 'L1_ffn_We': _L1_ffn_in['We'], 'L1_ffn_be': _L1_ffn_in['be'], 'L2_attn_Wq': _L2_attn_in['Wq'], 'L2_attn_Wkv': _L2_attn_in['Wkv'], 'L2_attn_Wo': _L2_attn_in['Wo'], 'L2_ffn_Wr': _L2_ffn_in['Wr'], 'L2_ffn_Wg': _L2_ffn_in['Wg'], 'L2_ffn_Wu': _L2_ffn_in['Wu'], 'L2_ffn_Wd': _L2_ffn_in['Wd'], 'L2_ffn_Sg': _L2_ffn_in['Sg'], 'L2_ffn_Su': _L2_ffn_in['Su'], 'L2_ffn_Sd': _L2_ffn_in['Sd'], 'L3_attn_Wqkv': _L3_attn_in['Wqkv'], 'L3_attn_bqkv': _L3_attn_in['bqkv'], 'L3_attn_Wo': _L3_attn_in['Wo'], 'L3_attn_bo': _L3_attn_in['bo'], 'L3_attn_wq': _L3_attn_in['wq'], 'L3_attn_wk': _L3_attn_in['wk'], 'L3_ffn_gate_W': _L3_ffn_in['gate_W'], 'L3_ffn_gate_b': _L3_ffn_in['gate_b'], 'L3_ffn_expert_W': _L3_ffn_in['expert_W'], 'L3_ffn_expert_b': _L3_ffn_in['expert_b']}
    _x0 = _d['L0_attn_x']
    _d['L0_attn_x'] = jax.random.normal(jax.random.fold_in(jax.random.key(seed), 1), (8, 512, 128), dtype=_x0.dtype)
    del _x0
    return _d

def reference(L0_attn_x, L0_attn_w_norm, L0_attn_W_in, L0_attn_b_in, L0_attn_W_x, L0_attn_b_x, L0_attn_W_dt, L0_attn_b_dt, L0_attn_W_out, L0_attn_b_out, L0_ffn_W_r, L0_ffn_W_k, L0_ffn_W_v, L0_ffn_mu_r, L0_ffn_mu_k, L1_attn_f_in_proj, L1_attn_f_conv_w, L1_attn_f_conv_b, L1_attn_f_x_proj, L1_attn_f_dt_w, L1_attn_f_dt_b, L1_attn_f_A_log, L1_attn_f_D, L1_attn_f_out_proj, L1_attn_b_in_proj, L1_attn_b_conv_w, L1_attn_b_conv_b, L1_attn_b_x_proj, L1_attn_b_dt_w, L1_attn_b_dt_b, L1_attn_b_A_log, L1_attn_b_D, L1_attn_b_out_proj, L1_attn_ln_g, L1_attn_ln_b, L1_ffn_Wg, L1_ffn_We, L1_ffn_be, L2_attn_Wq, L2_attn_Wkv, L2_attn_Wo, L2_ffn_Wr, L2_ffn_Wg, L2_ffn_Wu, L2_ffn_Wd, L2_ffn_Sg, L2_ffn_Su, L2_ffn_Sd, L3_attn_Wqkv, L3_attn_bqkv, L3_attn_Wo, L3_attn_bo, L3_attn_wq, L3_attn_wk, L3_ffn_gate_W, L3_ffn_gate_b, L3_ffn_expert_W, L3_ffn_expert_b):

    def _L0_attn_ref(x, w_norm, W_in, b_in, W_x, b_x, W_dt, b_dt, W_out, b_out):
        import jax, jax.numpy as jnp
        import numpy as np
        EPS = 1e-08

        def rmsnorm(x, w):
            norm = jax.lax.rsqrt(jnp.mean(x * x, axis=-1, keepdims=True) + EPS)
            return x * norm * w
        residual = x
        xn = rmsnorm(x, w_norm)
        uzg = xn @ W_in + b_in
        S = uzg.shape[-1] // 3
        u, z, g = (uzg[..., :S], uzg[..., S:2 * S], uzg[..., 2 * S:])
        ut = jnp.tanh(u @ W_x + b_x)
        dt = jax.nn.sigmoid(z @ W_dt + b_dt)

        def step(h, inp):
            u_t, dt_t = inp
            h = (1.0 - dt_t) * h + dt_t * u_t
            return (h, h)
        h0 = jnp.zeros(ut.shape[::2][::-1][:0] + (ut.shape[0], ut.shape[2]), ut.dtype)
        _, hs = jax.lax.scan(step, h0, (ut.transpose(1, 0, 2), dt.transpose(1, 0, 2)))
        hs = hs.transpose(1, 0, 2)
        y = hs * jax.nn.sigmoid(g)
        y = y @ W_out + b_out
        return residual + y

    def _L0_ffn_ref(x, W_r, W_k, W_v, mu_r, mu_k):
        import jax, jax.numpy as jnp
        import numpy as np
        DIM = 128

        def _reference_tuple_inner(x, W_r, W_k, W_v, mu_r, mu_k):
            B, T, C = x.shape
            x_prev = jnp.concatenate([jnp.zeros((B, 1, C), x.dtype), x[:, :-1, :]], axis=1)
            xr = mu_r * x + (1.0 - mu_r) * x_prev
            xk = mu_k * x + (1.0 - mu_k) * x_prev
            r = jax.nn.sigmoid(jnp.einsum('btc,dc->btd', xr, W_r))
            k = jnp.einsum('btc,dc->btd', xk, W_k)
            k_act = jnp.square(jax.nn.relu(k))
            out = r * jnp.einsum('btc,dc->btd', k_act, W_v)
            new_state = x[:, -1, :]
            return (out, new_state)
        return _reference_tuple_inner(x, W_r, W_k, W_v, mu_r, mu_k)[0]

    def _L1_attn_ref(x, f_in_proj, f_conv_w, f_conv_b, f_x_proj, f_dt_w, f_dt_b, f_A_log, f_D, f_out_proj, b_in_proj, b_conv_w, b_conv_b, b_x_proj, b_dt_w, b_dt_b, b_A_log, b_D, b_out_proj, ln_g, ln_b):
        import jax, jax.numpy as jnp
        import numpy as np
        D_MODEL = 128
        D_INNER = 256
        D_STATE = 16
        D_CONV = 4
        DT_RANK = 64
        BATCH = 2
        SEQ = 128
        LN_EPS = 1e-05

        def _mk_layer(key):
            k = jax.random.split(key, 5)
            return {'in_proj': jax.random.normal(k[0], (2 * D_INNER, D_MODEL)) * 0.02, 'conv_w': jax.random.normal(k[1], (D_INNER, 1, D_CONV)) * 0.2, 'conv_b': jnp.zeros((D_INNER,)), 'x_proj': jax.random.normal(k[2], (DT_RANK + 2 * D_STATE, D_INNER)) * 0.02, 'dt_w': jax.random.normal(k[3], (D_INNER, DT_RANK)) * 0.02, 'dt_b': jnp.full((D_INNER,), -4.6), 'A_log': jnp.log(jnp.tile(jnp.arange(1.0, D_STATE + 1.0), (D_INNER, 1))), 'D': jnp.ones((D_INNER,)), 'out_proj': jax.random.normal(k[4], (D_MODEL, D_INNER)) * 0.02}

        def _mamba(x, in_proj, conv_w, conv_b, x_proj, dt_w, dt_b, A_log, Dp, out_proj):
            Bb, L, _ = x.shape
            xz = jnp.einsum('bld,ed->ble', x, in_proj)
            xi, z = jnp.split(xz, 2, axis=-1)
            xc = jnp.transpose(xi, (0, 2, 1))
            xc = jax.lax.conv_general_dilated(xc, conv_w, (1,), [(D_CONV - 1, 0)], dimension_numbers=('NCH', 'OIH', 'NCH'), feature_group_count=D_INNER)
            xc = xc + conv_b[None, :, None]
            xi = jax.nn.silu(jnp.transpose(xc, (0, 2, 1)))
            dbc = jnp.einsum('bld,ed->ble', xi, x_proj)
            dt, Bm, Cm = jnp.split(dbc, [DT_RANK, DT_RANK + D_STATE], axis=-1)
            dt = jax.nn.softplus(jnp.einsum('blr,dr->bld', dt, dt_w) + dt_b)
            A = -jnp.exp(A_log)
            dA = jnp.exp(dt[..., None] * A)
            dBx = (dt * xi)[..., None] * Bm[:, :, None, :]

            def step(h, inp):
                a, bx, c = inp
                h = a * h + bx
                return (h, jnp.einsum('bds,bs->bd', h, c))
            h0 = jnp.zeros((Bb, D_INNER, D_STATE), x.dtype)
            _, ys = jax.lax.scan(step, h0, (jnp.moveaxis(dA, 1, 0), jnp.moveaxis(dBx, 1, 0), jnp.moveaxis(Cm, 1, 0)))
            y = jnp.moveaxis(ys, 0, 1) + xi * Dp
            y = y * jax.nn.silu(z)
            return jnp.einsum('ble,de->bld', y, out_proj)
        xb = x[:, ::-1, :]
        yf = jax.nn.sigmoid(_mamba(x, f_in_proj, f_conv_w, f_conv_b, f_x_proj, f_dt_w, f_dt_b, f_A_log, f_D, f_out_proj))
        yb = jax.nn.sigmoid(_mamba(xb, b_in_proj, b_conv_w, b_conv_b, b_x_proj, b_dt_w, b_dt_b, b_A_log, b_D, b_out_proj))
        d = 0.5 * (yf + yb[:, ::-1, :])
        mu = jnp.mean(d, axis=-1, keepdims=True)
        var = jnp.var(d, axis=-1, keepdims=True)
        d = (d - mu) * jax.lax.rsqrt(var + LN_EPS) * ln_g + ln_b
        return d + x

    def _L1_ffn_ref(x, Wg, We, be):
        import jax, jax.numpy as jnp
        import numpy as np
        B, S, D = (4, 256, 128)
        E = 8
        CF = 1
        b, s, d = x.shape
        n = b * s
        cap = n // E * CF
        h = x.reshape(n, d)
        router_logits = h @ Wg
        probs = jax.nn.softmax(router_logits, axis=1)
        best = jnp.argmax(probs, axis=1)
        mask = jax.nn.one_hot(best, E, dtype=probs.dtype)
        gate = jnp.sum(probs * mask, axis=1)
        locations = jnp.cumsum(mask, axis=0) - 1.0
        mask = mask * (locations < cap).astype(mask.dtype)
        loc_idx = jnp.sum(locations * mask, axis=1).astype(jnp.int32)
        new_gate = gate[:, None] * mask
        loc_oh = jax.nn.one_hot(loc_idx, cap, dtype=new_gate.dtype)
        combine = new_gate[:, :, None] * loc_oh[:, None, :]
        dispatch = (combine != 0).astype(h.dtype)
        dispatched = jnp.einsum('nec,nd->ecd', dispatch, h).reshape(E * cap, d)
        expert_out = dispatched @ We + be
        out = combine.reshape(n, E * cap) @ expert_out
        return out.reshape(b, s, d)

    def _L2_attn_ref(x, Wq, Wkv, Wo):
        import jax, jax.numpy as jnp
        import numpy as np
        HEADS = 16
        EPS = 1e-08

        def _attention(x, Wq, Wkv, Wo, heads=HEADS, causal=True, eps=EPS):
            B, N, D = x.shape
            dh = D // heads
            q = x @ Wq.T
            k, v = jnp.split(x @ Wkv.T, 2, axis=-1)

            def split_heads(t):
                return t.reshape(B, N, heads, dh).transpose(0, 2, 1, 3)
            q, k, v = map(split_heads, (q, k, v))
            q = q * dh ** (-0.5)
            sim = jnp.einsum('bhid,bhjd->bhij', q, k)
            mask_value = -jnp.finfo(sim.dtype).max
            if causal:
                causal_mask = jnp.triu(jnp.ones((N, N), dtype=bool), 1)
                sim = jnp.where(causal_mask, mask_value, sim)
            m = jax.lax.stop_gradient(jnp.max(sim, axis=-1, keepdims=True))
            e = jnp.exp(sim - m)
            num = jnp.einsum('bhij,bhjd->bhid', e, v)
            den = jnp.sum(e, axis=-1, keepdims=True) + eps
            out = num / den
            out = out.transpose(0, 2, 1, 3).reshape(B, N, D)
            return out @ Wo.T
        return _attention(x, Wq, Wkv, Wo)

    def _L2_ffn_ref(x, Wr, Wg, Wu, Wd, Sg, Su, Sd):
        import jax, jax.numpy as jnp
        import numpy as np
        B, S, D = (2, 256, 128)
        E, K, F = (16, 2, 64)
        FS = 128
        b, s, d = x.shape
        T = b * s
        xf = x.reshape(T, d)
        shared = jax.nn.silu(xf @ Sg) * (xf @ Su) @ Sd
        probs = jax.nn.softmax(xf @ Wr, axis=-1)
        topk_p, topk_i = jax.lax.top_k(probs, K)
        n_exp = Wr.shape[1]
        cw = jnp.zeros((T, n_exp), x.dtype).at[jnp.arange(T)[:, None], topk_i].add(topk_p)

        def step(acc, ew):
            wg, wu, wd, c = ew
            y = jax.nn.silu(xf @ wg) * (xf @ wu) @ wd
            return (acc + y * c[:, None], None)
        routed, _ = jax.lax.scan(step, jnp.zeros_like(xf), (Wg, Wu, Wd, cw.T))
        return (routed + shared).reshape(b, s, d)

    def _L3_attn_ref(x, Wqkv, bqkv, Wo, bo, wq, wk):
        import jax, jax.numpy as jnp
        import numpy as np
        D_MODEL = 128
        N_HEADS = 16
        D_HEAD = D_MODEL // N_HEADS

        def _rmsnorm(x, w):
            xf = x.astype(jnp.float32)
            rms = jnp.mean(xf * xf, axis=-1, keepdims=True)
            return (xf / jnp.sqrt(rms + 1e-06) * w.astype(jnp.float32)).astype(x.dtype)
        b, s, d = x.shape
        qkv = x @ Wqkv.T + bqkv
        q, k, v = jnp.split(qkv, 3, axis=-1)
        q = q.reshape(b, s, N_HEADS, D_HEAD)
        k = k.reshape(b, s, N_HEADS, D_HEAD)
        v = v.reshape(b, s, N_HEADS, D_HEAD)
        q = _rmsnorm(q, wq)
        k = _rmsnorm(k, wk)
        qf = q.astype(jnp.float32)
        kf = k.astype(jnp.float32)
        vf = v.astype(jnp.float32)
        attn = jnp.einsum('bqhd,bkhd->bhqk', qf, kf)
        attn = jax.nn.softmax(attn, axis=-1)
        z = jnp.einsum('bhqk,bkhd->bqhd', attn, vf).astype(x.dtype)
        z = z.reshape(b, s, d)
        return z @ Wo.T + bo

    def _L3_ffn_ref(x, gate_W, gate_b, expert_W, expert_b):
        import jax, jax.numpy as jnp
        import numpy as np
        B, S, D, E, K = (4, 256, 128, 8, 2)
        EPS, W_THRES, TEMP = (0.0001, 0.1, 1.0)
        scores = jnp.maximum((x @ gate_W + gate_b) / TEMP, EPS)
        p = jax.nn.softmax(scores, axis=-1)
        _, topk_idx = jax.lax.top_k(p, K)
        topk_mask = jax.nn.one_hot(topk_idx, E, dtype=p.dtype).sum(-2) > 0
        w = jnp.maximum(p, W_THRES)
        w_gather = jnp.take_along_axis(w, topk_idx, axis=-1)
        total = jax.lax.stop_gradient(w_gather.sum(-1, keepdims=True))
        w = w / total
        comb = jnp.where(topk_mask, w, jnp.zeros_like(w))
        y = jnp.einsum('bsd,edf->bsef', x, expert_W) + expert_b
        out = jnp.einsum('bsef,bse->bsf', y, comb) / K
        return out
    x = L0_attn_x
    x = x + 0.5 * _L0_ffn_ref(_layernorm(x, axis=-1), L0_ffn_W_r, L0_ffn_W_k, L0_ffn_W_v, L0_ffn_mu_r, L0_ffn_mu_k)
    x = x + _L0_attn_ref(_layernorm(x, axis=-1), L0_attn_w_norm, L0_attn_W_in, L0_attn_b_in, L0_attn_W_x, L0_attn_b_x, L0_attn_W_dt, L0_attn_b_dt, L0_attn_W_out, L0_attn_b_out)
    x = x + 0.5 * _L0_ffn_ref(_layernorm(x, axis=-1), L0_ffn_W_r, L0_ffn_W_k, L0_ffn_W_v, L0_ffn_mu_r, L0_ffn_mu_k)
    x = x + 0.5 * _L1_ffn_ref(_layernorm(x, axis=-1), L1_ffn_Wg, L1_ffn_We, L1_ffn_be)
    x = x + _L1_attn_ref(_layernorm(x, axis=-1), L1_attn_f_in_proj, L1_attn_f_conv_w, L1_attn_f_conv_b, L1_attn_f_x_proj, L1_attn_f_dt_w, L1_attn_f_dt_b, L1_attn_f_A_log, L1_attn_f_D, L1_attn_f_out_proj, L1_attn_b_in_proj, L1_attn_b_conv_w, L1_attn_b_conv_b, L1_attn_b_x_proj, L1_attn_b_dt_w, L1_attn_b_dt_b, L1_attn_b_A_log, L1_attn_b_D, L1_attn_b_out_proj, L1_attn_ln_g, L1_attn_ln_b)
    x = x + 0.5 * _L1_ffn_ref(_layernorm(x, axis=-1), L1_ffn_Wg, L1_ffn_We, L1_ffn_be)
    x = x + 0.5 * _L2_ffn_ref(_layernorm(x, axis=-1), L2_ffn_Wr, L2_ffn_Wg, L2_ffn_Wu, L2_ffn_Wd, L2_ffn_Sg, L2_ffn_Su, L2_ffn_Sd)
    x = x + _L2_attn_ref(_layernorm(x, axis=-1), L2_attn_Wq, L2_attn_Wkv, L2_attn_Wo)
    x = x + 0.5 * _L2_ffn_ref(_layernorm(x, axis=-1), L2_ffn_Wr, L2_ffn_Wg, L2_ffn_Wu, L2_ffn_Wd, L2_ffn_Sg, L2_ffn_Su, L2_ffn_Sd)
    x = x + 0.5 * _L3_ffn_ref(_layernorm(x, axis=-1), L3_ffn_gate_W, L3_ffn_gate_b, L3_ffn_expert_W, L3_ffn_expert_b)
    x = x + _L3_attn_ref(_layernorm(x, axis=-1), L3_attn_Wqkv, L3_attn_bqkv, L3_attn_Wo, L3_attn_bo, L3_attn_wq, L3_attn_wk)
    x = x + 0.5 * _L3_ffn_ref(_layernorm(x, axis=-1), L3_ffn_gate_W, L3_ffn_gate_b, L3_ffn_expert_W, L3_ffn_expert_b)
    return x

_drawn_inputs = setup_inputs


def setup_inputs(seed=0):
    import zlib

    import numpy as np

    out = dict(_drawn_inputs(seed))
    spreads = {'L0_attn_w_norm': (1.0, 0.2),
     'L0_attn_b_in': (0.0, 0.344),
     'L0_attn_b_x': (0.0, 0.36),
     'L0_attn_b_dt': (0.0, 0.8),
     'L0_attn_b_out': (0.0, 0.1),
     'L1_attn_f_conv_b': (0.0, 0.274),
     'L1_attn_f_dt_b': (-4.599999904632568, 0.6),
     'L1_attn_f_D': (1.0, 0.6),
     'L1_attn_b_conv_b': (0.0, 0.304),
     'L1_attn_b_dt_b': (-4.599999904632568, 0.6),
     'L1_attn_b_D': (1.0, 0.6),
     'L1_attn_ln_g': (1.0, 0.6),
     'L1_attn_ln_b': (0.0, 0.1),
     'L3_attn_wq': (1.0, 0.6),
     'L3_attn_wk': (1.0, 0.581),
     'L3_ffn_gate_b': (0.0, 0.445),
     'L3_ffn_expert_b': (0.0, 0.718)}
    factors = {'L0_ffn_W_r': 3.577,
     'L0_ffn_mu_r': 6.511,
     'L1_attn_f_x_proj': 8.0,
     'L1_attn_f_dt_w': 8.0,
     'L1_attn_f_A_log': 8.0,
     'L1_attn_b_x_proj': 8.0,
     'L1_attn_b_dt_w': 8.0,
     'L1_attn_b_A_log': 8.0,
     'L1_ffn_be': 8.0,
     'L2_attn_Wq': 8.0,
     'L2_attn_Wkv': 8.0,
     'L2_attn_Wo': 8.0,
     'L3_attn_bqkv': 8.0,
     'L3_attn_bo': 8.0}
    for name, (base, spread) in spreads.items():
        noise = np.random.default_rng([zlib.crc32(name.encode()), seed]).standard_normal(out[name].shape)
        drawn = base * np.exp(spread * noise) if base else spread * noise
        out[name] = jnp.asarray(drawn.astype(out[name].dtype))
    for name, factor in factors.items():
        out[name] = (out[name] * factor).astype(out[name].dtype)
    return out
```

```python
from contextlib import ExitStack

import numpy as np

import concourse.bass as bass
from concourse import mybir

F32 = mybir.dt.float32
BF16 = mybir.dt.bfloat16
ALU = mybir.AluOpType
ACT = mybir.ActivationFunctionType
AX = mybir.AxisListType

B, T, D = 8, 512, 128
NT = T // 128
PAD = 3
H, DH = 16, 8
NS, DR = 16, 64
NEG = -1e30


GROUPS = [
    [("cen", 128, 128), ("cenh", 128, 128), ("avg", 128, 128), ("ident", 128, 128), ("ones", 128, 128),
     ("upper", 128, 128), ("rev8", 128, 8), ("rev16", 128, 16),
     ("wr", 128, 128), ("wk", 128, 128), ("wv", 128, 128), ("mur", 128, 1), ("muk", 128, 1)],
    [("win", 128, 96), ("wn", 128, 1), ("bin", 32, 3), ("wx", 32, 32), ("bx", 32, 1), ("wdt", 32, 32),
     ("bdt", 32, 1), ("wout", 32, 128), ("bout", 128, 1),
     ("l1g", 128, 8), ("l1e", 128, 128), ("l1b", 128, 1), ("selbc", 96, 32)],
    [(p + n, r, c) for p in ("mf_", "mb_") for n, r, c in
     (("in", 128, 512), ("cw", 128, 8), ("cb", 128, 2), ("xp", 128, 320), ("dw", 64, 256), ("db", 128, 2),
      ("al", 128, 32), ("dd", 128, 2), ("op", 128, 256))] + [("lng", 128, 1), ("lnb", 128, 1)],
    [("l2r", 128, 16), ("sel16", 48, 16), ("mq", 128, 128), ("mt", 128, 128), ("l2g", 128, 1024), ("l2u", 128, 1024)],
    [("l2d", 128, 1024), ("sg", 128, 128), ("su", 128, 128), ("sd", 128, 128),
     ("a2q", 128, 128), ("a2k", 128, 128), ("a2v", 128, 128), ("a2o", 128, 128)],
    [("bd8", 128, 128), ("a3q", 128, 128), ("a3k", 128, 128), ("a3v", 128, 128), ("a3bq", 128, 1),
     ("a3bk", 128, 1), ("a3bv", 1, 128), ("a3o", 128, 128), ("a3bo", 128, 1), ("a3wq", 128, 1), ("a3wk", 128, 1),
     ("l3g", 128, 8), ("l3gb", 1, 8), ("sel8", 24, 8), ("l3w", 128, 1024), ("l3b", 24, 128)],
]
COLS = {}
EDGE = [0]
for _g in GROUPS:
    _at = EDGE[-1]
    for _n, _r, _c in _g:
        assert _n not in COLS
        COLS[_n] = (_at, _r, _c)
        _at += _c
    EDGE.append(_at)
WIDTH = EDGE[-1]


class Counter:

    def __init__(self, sem):
        self.sem, self.n = sem, 0

    def add(self, k):
        self.n += k
        return self, self.n


class Queue:

    def __init__(self, sem):
        self.mine, self.ops, self.seen = Counter(sem), [], {}

    def wait(self, after):
        need = {}
        for c, v in after:
            need[c] = max(v, need.get(c, 0))
        for c, v in need.items():
            if self.seen.get(c, 0) < v:
                self.seen[c] = v
                self.ops.append((c.sem, v))

    def __call__(self, after, f, *a, **k):
        self.wait(after)
        self.ops.append((f, a, k, self.mine.sem, 1))
        return self.mine.add(1)

    def plain(self, f, *a):
        self.ops.append((f, a, {}, None, 0))

    def dma(self, after, counter, f, out, in_):
        self.wait(after)
        self.ops.append((f, (out, in_), {}, counter.sem, 16))
        return counter.add(16)

    def play(self, eng):
        for op in self.ops:
            if len(op) == 2:
                eng.wait_ge(*op)
            else:
                f, a, k, sem, inc = op
                ins = f(*a, **k)
                if inc:
                    ins.then_inc(sem, inc)


class Slot:

    def __init__(self, ap, pool):
        self.ap, self.free, self.pool = ap, (), pool

    def give(self, *last):
        self.free = last
        self.pool.append(self)


class Pool:
    def __init__(self, aps):
        self.slots = []
        for ap in aps:
            self.slots.append(Slot(ap, self.slots))

    def take(self):
        assert self.slots, "no slot left"
        return self.slots.pop(0)


def build(nc, xin, wts, out):
    ctx = ExitStack()
    with ctx:
        def sb(name, shape, dt=F32):
            return ctx.enter_context(nc.sbuf_tensor(name, shape, dt))

        def sem(name):
            return ctx.enter_context(nc.semaphore(name))

        PE, V, S, G, SP = (Queue(sem("s_" + n)) for n in ("pe", "dve", "act", "pool", "sp"))
        te, ve, se, ge, sy = nc.tensor, nc.vector, nc.scalar, nc.gpsimd, nc.sync
        TT, TS, STT, RED, SCAN = (ve.tensor_tensor, ve.tensor_scalar, ve.scalar_tensor_tensor,
                                  ve.tensor_reduce, ve.tensor_tensor_scan)
        AF = se.activation

        psum = [ctx.enter_context(nc.psum_tensor(f"ps{i}", [128, 512], F32)) for i in range(8)]
        W = sb("W", [128, WIDTH])
        NX = 3
        X = [sb(f"X{b}", [128, T]) for b in range(NX)]
        X = [X[b % NX] for b in range(B)]

        def w(name, lo=0, hi=None):
            at, rows, cols = COLS[name]
            return W[0:rows, at + lo:at + (cols if hi is None else hi)]

        s_w = [Counter(sem(f"s_w{i}")) for i in range(len(GROUPS))]
        s_x = [Counter(sem(f"s_x{b}")) for b in range(B)]
        s_out = Counter(sem("s_out"))
        wl, xl = [], []
        wl.append(SP.dma((), s_w[0], sy.dma_start, W[:, EDGE[0]:EDGE[1]], wts[:, EDGE[0]:EDGE[1]]))
        xl.append(SP.dma((), s_x[0], sy.dma_start, X[0][:, :], xin[0]))
        for i in range(1, len(GROUPS)):
            wl.append(SP.dma((), s_w[i], sy.dma_start, W[:, EDGE[i]:EDGE[i + 1]], wts[:, EDGE[i]:EDGE[i + 1]]))
        for b in range(1, NX):
            xl.append(SP.dma((), s_x[b], sy.dma_start, X[b][:, :], xin[b]))

        def mm(after, o, l, r, start=True, stop=True, skip=False):
            return PE(after, te.matmul, o, l, r, start=start, stop=stop, skip_group_check=skip)

        eps = sb("eps", [128, 4])
        e5, e8, e6, one = (eps[:, i:i + 1] for i in range(4))
        for i, val in enumerate((1e-5, 1e-8, 1e-6, 1.0)):
            t_eps = V((), ve.memset, eps[:, i:i + 1], val)
        wr1, wr2, wk1, wk2 = (sb(n, [128, 128]) for n in ("wr1", "wr2", "wk1", "wk2"))
        om = sb("om", [128, 2])
        t_mu = V((wl[0],), TS, om[:, 0:1], w("mur"), -1.0, 1.0, ALU.mult, ALU.add)
        t_mu = V((wl[0],), TS, om[:, 1:2], w("muk"), -1.0, 1.0, ALU.mult, ALU.add)
        V((wl[0],), TS, wr1[:, :], w("wr"), w("mur"), None, ALU.mult)
        V((wl[0],), TS, wk1[:, :], w("wk"), w("muk"), None, ALU.mult)
        V((t_mu,), TS, wr2[:, :], w("wr"), om[:, 0:1], None, ALU.mult)
        t_l0f = V((t_mu,), TS, wk2[:, :], w("wk"), om[:, 1:2], None, ALU.mult)
        identb, upb, oneb = (sb(n, [128, 128], BF16) for n in ("identb", "upb", "oneb"))
        V((), ve.tensor_copy, identb[:, :], w("ident"))
        V((), ve.tensor_copy, upb[:, :], w("upper"))
        t_cb = V((), ve.tensor_copy, oneb[:, :], w("ones"))
        winS = sb("winS", [128, 96])
        V((wl[1],), TS, winS[:, :], w("win"), w("wn"), None, ALU.mult)
        nbdt = sb("nbdt", [32, 1])
        V((wl[1],), TS, nbdt[:, :], w("bdt"), -1.0, None, ALU.mult)
        selbc = sb("selbc_b", [96, 32], BF16)
        t_l0a = V((wl[1],), ve.tensor_copy, selbc[:, :], w("selbc"))
        Am = sb("Am", [128, 64])
        sel16, sel8 = sb("sel16_b", [48, 16, 64], BF16), sb("sel8_b", [24, 8], BF16)
        mqb, mtb = sb("mqb", [128, 128], BF16), sb("mtb", [128, 128], BF16)

        table = [None]

        def use(name):
            if table[0] != name:
                table[0] = name
                S.plain(se.preload_act_table_set, name)

        LE, SG, SI = "natural_log_exp_and_others", "sigmoid_and_others", "silu_and_others"
        use(LE)
        S((wl[2],), AF, Am[:, 0:32], w("mf_al"), ACT.Exp)
        t_al = S((), AF, Am[:, 32:64], w("mb_al"), ACT.Exp)
        t_am = V((t_al,), TS, Am[:, :], Am[:, :], -1.0, None, ALU.mult)
        V((wl[3],), ve.tensor_copy, sel16[:, :, :], w("sel16").unsqueeze(2).broadcast_to([48, 16, 64]))
        V((), ve.tensor_copy, mqb[:, :], w("mq"))
        t_m3 = V((), ve.tensor_copy, mtb[:, :], w("mt"))
        t_m5 = V((wl[5],), ve.tensor_copy, sel8[:, :], w("sel8"))

        class Half:
            def __init__(self, n, banks, tmps):
                self.banks = Pool([p[:, :] for p in banks])
                self.tmps = Pool([sb(f"tmp{n}_{i}", [128, T])[:, :] for i in range(tmps)])
                hs = [sb(f"h{n}_{i}", [128, PAD + T]) for i in range(2)]
                self.tz = [V((), ve.memset, h[:, 0:PAD], 0.0) for h in hs][-1]
                self.hs = Pool(hs)
                self.small = Pool([sb(f"sm{n}_{i}", [128, 512])[:, :] for i in range(2)])
                self.cb = Pool([sb(f"cb{n}_{i}", [128, 192], BF16)[:, :] for i in range(2)])
                self.cT = Pool([sb(f"cT{n}_{i}", [48, 512], BF16)[:, :] for i in range(2)])

        HA = Half("a", psum[0:4], 6)
        HB = Half("b", psum[4:8], 8)

        def rms(h, x, tx, mat, e, use_center=True):
            if use_center:
                A = h.banks.take()
                t1 = mm((*A.free, *tx), A.ap, w(mat), x)
                src = A.ap
            else:
                A, t1, src = None, None, x
            r = h.tmps.take()
            t2 = S((*(tx if t1 is None else (t1,)), *r.free), AF, r.ap, src, ACT.Square)
            Bk = h.banks.take()
            t3 = mm((t2, *Bk.free), Bk.ap, w("avg"), r.ap)
            use(LE)
            t4 = S((t3, t_eps), AF, r.ap, Bk.ap, ACT.Ln, bias=e)
            Bk.give(t4)
            t5 = S((t4,), AF, r.ap, r.ap, ACT.Exp, scale=-0.5)
            return A, r, t5

        def ln(h, x, tx, mat="cen", e=None):
            A, r, t5 = rms(h, x, tx, mat, e5 if e is None else e)
            o = h.hs.take()
            t6 = V((t5, h.tz, *o.free), TT, o.ap[:, PAD:], A.ap, r.ap, ALU.mult)
            A.give(t6)
            r.give(t6)
            return o, t6

        def l0_ffn(h, b, tx):
            x = X[b][:, :]
            hh, th = ln(h, x, tx)
            yield 1
            hc, hp = hh.ap[:, PAD:], hh.ap[:, PAD - 1:PAD - 1 + T]
            R, K = h.banks.take(), h.banks.take()
            mm((th, t_l0f, *R.free), R.ap, wr1[:, :], hc, stop=False)
            t1 = mm((), R.ap, wr2[:, :], hp, start=False)
            mm(K.free, K.ap, wk1[:, :], hc, stop=False)
            t2 = mm((), K.ap, wk2[:, :], hp, start=False)
            hh.give(t2)
            r, k = h.tmps.take(), h.tmps.take()
            t4 = S((t2, *k.free), AF, k.ap, K.ap, ACT.Relu)
            K.give(t4)
            t4 = S((t4,), AF, k.ap, k.ap, ACT.Square)
            use(SG)
            t3 = S((t1, *r.free), AF, r.ap, R.ap, ACT.Sigmoid)
            R.give(t3)
            yield 1
            Vk = h.banks.take()
            t5 = mm((t4, *Vk.free), Vk.ap, w("wv"), k.ap)
            k.give(t5)
            t6 = V((t5, t3), STT, r.ap, Vk.ap, 0.5, r.ap, ALU.mult, ALU.mult)
            Vk.give(t6)
            t7 = V((t6,), TT, x, x, r.ap, ALU.add)
            r.give(t7)
            yield 1
            return (t7,)

        def l0_attn(h, b, tx):
            x = X[b][:, :]
            hh, th = ln(h, x, tx)
            yield 1
            hc = hh.ap[:, PAD:]
            _, r, t5 = rms(h, hc, (th,), None, e8, use_center=False)
            xn = h.tmps.take()
            t1 = V((t5, *xn.free), TT, xn.ap, hc, r.ap, ALU.mult)
            r.give(t1)
            yield 1
            uzg = []
            for i in range(3):
                bk = h.banks.take()
                t = mm((t1, t_l0a, *bk.free), bk.ap[0:32, :], winS[:, 32 * i:32 * i + 32], xn.ap)
                uzg.append((bk, t))
            xn.give(t)
            u, z, g = h.tmps.take(), h.tmps.take(), h.tmps.take()
            tu = S((uzg[0][1], *u.free), AF, u.ap[0:32, :], uzg[0][0].ap[0:32, :], ACT.Identity, bias=w("bin", 0, 1))
            tz = S((uzg[1][1], *z.free), AF, z.ap[0:32, :], uzg[1][0].ap[0:32, :], ACT.Identity, bias=w("bin", 1, 2))
            uzg[0][0].give(tu)
            uzg[1][0].give(tz)
            use(SG)
            tg = S((uzg[2][1], *g.free), AF, g.ap[0:32, :], uzg[2][0].ap[0:32, :], ACT.Sigmoid, bias=w("bin", 2, 3))
            uzg[2][0].give(tg)
            yield 1
            U, Z = h.banks.take(), h.banks.take()
            t1 = mm((tu, *U.free), U.ap[0:32, :], w("wx"), u.ap[0:32, :])
            t2 = mm((tz, *Z.free), Z.ap[0:32, :], w("wdt"), z.ap[0:32, :])
            tu = S((t1,), AF, u.ap[0:32, :], U.ap[0:32, :], ACT.Tanh, bias=w("bx"))
            U.give(tu)
            a = h.tmps.take()
            tz = S((t2,), AF, z.ap[0:32, :], Z.ap[0:32, :], ACT.Sigmoid, bias=w("bdt"))
            ta = S((*a.free,), AF, a.ap[0:32, :], Z.ap[0:32, :], ACT.Sigmoid, bias=nbdt[:, :], scale=-1.0)
            Z.give(ta)
            t3 = V((tu, tz), TT, u.ap[0:32, :], u.ap[0:32, :], z.ap[0:32, :], ALU.mult)
            t4 = V((t3, ta), SCAN, z.ap[0:32, :], a.ap[0:32, :], u.ap[0:32, :], 0.0, ALU.mult, ALU.add)
            u.give(t4)
            a.give(t4)
            t5 = V((t4, tg), TT, g.ap[0:32, :], g.ap[0:32, :], z.ap[0:32, :], ALU.mult)
            z.give(t5)
            yield 1
            Y = h.banks.take()
            t6 = mm((t5, *Y.free), Y.ap, w("wout"), g.ap[0:32, :])
            g.give(t6)
            y = h.tmps.take()
            t7 = V((t6, *y.free), STT, y.ap, Y.ap, w("bout"), hc, ALU.add, ALU.add)
            Y.give(t7)
            hh.give(t7)
            t8 = V((t7,), TT, x, x, y.ap, ALU.add)
            y.give(t8)
            yield 1
            return (t8,)

        def first_max(sm, e, at, n, rev, after):
            mask = sm[:, at:at + NT * n].rearrange("p (t e) -> p t e", e=n)
            mx = sm[:, at + NT * n:at + NT * n + NT]
            mb = mx.unsqueeze(2).broadcast_to([128, NT, n])
            rb = w(rev).unsqueeze(1).broadcast_to([128, NT, n])
            t = V(after, RED, mx, e, AX.X, ALU.max)
            t = V((t,), TT, mask, e, mb, ALU.is_equal)
            t = V((t,), TT, mask, mask, rb, ALU.mult)
            t = V((t,), RED, mx, mask, AX.X, ALU.max)
            return mask, V((t,), TT, mask, mask, mb, ALU.is_equal)

        def bc(ap, n):
            return ap.unsqueeze(2).broadcast_to([128, NT, n])

        def softmax_rows(h, hc, after, wr, n, sm, bias=None, floor=None):
            L = h.banks.take()
            for j in range(NT):
                o = L.ap[:, j * n:(j + 1) * n]
                t = mm((*after, *L.free), o, hc[:, j * 128:(j + 1) * 128], w(wr), stop=bias is None)
                if bias is not None:
                    t = mm((), o, w("ones")[0:1, :], w(bias), start=False)
            e = sm.ap[:, 0:NT * n].rearrange("p (t e) -> p t e", e=n)
            mx, sums = sm.ap[:, NT * n:NT * n + NT], sm.ap[:, NT * n + NT:NT * n + 2 * NT]
            l3 = L.ap[:, 0:NT * n].rearrange("p (t e) -> p t e", e=n)
            if floor is not None:
                t = V((t, *sm.free), TS, e, l3, floor, None, ALU.max)
                L.give(t)
                t1 = V((t,), RED, mx, e, AX.X, ALU.max)
                t2 = V((t1,), TT, e, e, bc(mx, n), ALU.subtract)
            else:
                t1 = V((t, *sm.free), RED, mx, l3, AX.X, ALU.max)
                t2 = V((t1,), TT, e, l3, bc(mx, n), ALU.subtract)
                L.give(t2)
            use(LE)
            t3 = S((t2,), AF, e, e, ACT.Exp)
            t4 = V((t3,), RED, sums, e, AX.X, ALU.add)
            t5 = V((t4,), ve.reciprocal, mx, sums)
            return e, mx, t5

        def split_T(h, c, n, after):
            cb, cT = h.cb.take(), h.cT.take()
            v = cb.ap[:, 0:NT * 3 * n].rearrange("p (t k e) -> p t k e", k=3, e=n)
            t1 = V((*after, *cb.free), ve.tensor_copy, v[:, :, 0, :], c)
            t2 = V((t1,), TT, c, c, v[:, :, 0, :], ALU.subtract)
            t3 = V((t2,), ve.tensor_copy, v[:, :, 1, :], c)
            t4 = V((t3,), TT, v[:, :, 2, :], c, v[:, :, 1, :], ALU.subtract)
            bk = h.banks.take()
            pT = bk.ap[0:3 * n, 0:256].bitcast(BF16)
            for j in range(NT):
                t5 = PE((t4, t_cb, *bk.free), te.transpose, pT[:, j * 128:(j + 1) * 128],
                        cb.ap[:, j * 3 * n:(j + 1) * 3 * n], identb[:, :])
            cb.give(t5)
            t6 = V((t5, *cT.free), ve.tensor_copy, cT.ap[0:3 * n, :], pT)
            bk.give(t6)
            return cT, t6, t4

        carry = [[sb(f"carry{i}_{k}", [128, 8]) for k in range(2)] for i in range(2)]
        t_carry = [[(V((), ve.memset, carry[i][k][:, :], 0.0),) for k in range(2)] for i in range(2)]

        def l1_ffn(h, b, tx, which):
            x = X[b][:, :]
            hh, th = ln(h, x, tx)
            yield 1
            hc = hh.ap[:, PAD:]
            sm = h.small.take()
            e, rec, t1 = softmax_rows(h, hc, (th, wl[1]), "l1g", 8, sm)
            mask, t2 = first_max(sm.ap, e, 64, 8, "rev8", (t1,))
            mb = h.cb.take()
            mk = mb.ap[:, 0:32]
            t3 = V((t2, *mb.free), ve.tensor_copy, mk, sm.ap[:, 64:96])
            yield 1
            C = h.banks.take()
            for j in range(NT):
                o = C.ap[:, 8 * j:8 * j + 8]
                t4 = mm((t3, t_cb, *C.free), o, upb[:, :], mk[:, 8 * j:8 * j + 8], stop=j == 0)
                for i in range(j):
                    t4 = mm((), o, oneb[:, :], mk[:, 8 * i:8 * i + 8], start=False, stop=i == j - 1)
            for i in range(NT):
                t4 = mm((), C.ap[:, 32:40], oneb[:, :], mk[:, 8 * i:8 * i + 8], start=i == 0, stop=i == NT - 1)
            mb.give(t4)
            old, new = carry[which][b % 2], carry[which][(b + 1) % 2]
            loc = sm.ap[:, 0:32].rearrange("p (t e) -> p t e", e=8)
            t5 = V((t4, *t_carry[which][b % 2]), TT, loc, C.ap[:, 0:32].rearrange("p (t e) -> p t e", e=8),
                   old[:, :].unsqueeze(1).broadcast_to([128, NT, 8]), ALU.add)
            t6 = V((), TT, new[:, :], C.ap[:, 32:40], old[:, :], ALU.add)
            t_carry[which][(b + 1) % 2] = (t6,)
            C.give(t6)
            t7 = V((t5,), STT, loc, loc, 512.0, mask, ALU.is_le, ALU.mult)
            g = sm.ap[:, 128:132]
            t8 = V((t7,), RED, g, loc, AX.X, ALU.add)
            t9 = V((t8,), STT, g, g, 0.5, rec, ALU.mult, ALU.mult)
            yield 1
            Gb, Y = h.banks.take(), h.banks.take()
            for j in range(NT):
                t10 = mm((t9, *Gb.free), Gb.ap[:, j * 128:(j + 1) * 128], g[:, j:j + 1].broadcast_to([128, 128]),
                         w("ident"))
            sm.give(t10)
            t11 = mm(Y.free, Y.ap, w("l1e"), hc)
            hh.give(t11)
            y = h.tmps.take()
            t12 = S((t11, *y.free), AF, y.ap, Y.ap, ACT.Identity, bias=w("l1b"))
            Y.give(t12)
            t13 = V((t12, t10), TT, y.ap, y.ap, Gb.ap, ALU.mult)
            Gb.give(t13)
            t14 = V((t13,), TT, x, x, y.ap, ALU.add)
            y.give(t14)
            yield 1
            return (t14,)

        def two(ap):
            return ap.rearrange("p (g n) -> p g n", g=2)

        def pair(name):
            return sb(name, [128, 2, T])

        xpad = sb("xpad", [128, 2, PAD + T])
        t_xp = V((), ve.memset, xpad[:, :, 0:PAD], 0.0)
        m_xi, m_z, m_dt, m_du, m_c = (Pool([pair(n)]) for n in ("m_xi", "m_z", "m_dt", "m_du", "m_c"))
        m_xp = Pool([xpad])
        m_rev = Pool([sb("m_rev", [128, T])])
        m_bc = Pool([sb("m_bc", [96, T], BF16)])
        m_dtr = Pool([sb("m_dtr", [64, T])])
        m_y = Pool([sb(f"m_y{i}", [128, T]) for i in range(2)])
        ring_a = Pool([sb(f"ra{i}", [128, 2 * T]) for i in range(2)])
        t_a0 = [V((), ve.memset, two(s.ap[:, :])[:, :, 0:1], 0.0) for s in ring_a.slots][-1]
        ring_b = Pool([sb(f"rb{i}", [128, 2 * T]) for i in range(3)])
        ring_h = Pool([sb(f"rh{i}", [128, 2 * T]) for i in range(2)])

        def mamba_dir(h, p, src, tsrc):
            k = 0 if p == "mf_" else 1
            xp, z, c = m_xp.take(), m_z.take(), m_c.take()
            xi, dt, du = m_xi.take(), m_dt.take(), m_du.take()
            txp, tz = [], []
            for m in range(4):
                bk = h.banks.take()
                t = mm((*tsrc, wl[2], *bk.free), bk.ap, w(p + "in", m * 128, m * 128 + 128), src)
                if m < 2:
                    t2 = S((t, t_xp, *xp.free), AF, xp.ap[:, m, PAD:], bk.ap, ACT.Copy)
                    txp.append(t2)
                else:
                    use(SI)
                    t2 = S((t, *z.free), AF, z.ap[:, m - 2, :], bk.ap, ACT.Silu)
                    tz.append(t2)
                bk.give(t2)
                yield 1
            tlast = t
            for g in range(2):
                cw = w(p + "cw")
                t = V((txp[g], *c.free), TS, c.ap[:, g, :], xp.ap[:, g, 0:T], cw[:, 4 * g:4 * g + 1], None, ALU.mult)
                for j in range(1, 4):
                    t = V((t,), STT, c.ap[:, g, :], xp.ap[:, g, j:j + T], cw[:, 4 * g + j:4 * g + j + 1],
                          c.ap[:, g, :], ALU.mult, ALU.add)
                t = S((t, *xi.free), AF, xi.ap[:, g, :], c.ap[:, g, :], ACT.Silu, bias=w(p + "cb", g, g + 1))
                yield 1
            txi = t
            c.give(t)
            xp.give(t)
            Q, R = h.banks.take(), h.banks.take()
            for g in range(2):
                t1 = mm((txi, *Q.free), Q.ap[0:64, :], w(p + "xp", g * 160, g * 160 + 64), xi.ap[:, g, :],
                        start=g == 0, stop=g == 1)
            for g in range(2):
                t2 = mm(R.free, R.ap[0:96, :], w(p + "xp", g * 160 + 64, g * 160 + 160), xi.ap[:, g, :],
                        start=g == 0, stop=g == 1)
            dtr, bcs, r1 = m_dtr.take(), m_bc.take(), h.tmps.take()
            tdr = S((t1, *dtr.free), AF, dtr.ap[:, :], Q.ap[0:64, :], ACT.Copy)
            Q.give(tdr)
            t3 = S((t2, *bcs.free), AF, bcs.ap[:, :], R.ap[0:96, :], ACT.Copy)
            t4 = V((t3, *r1.free), TT, r1.ap[0:96, :], R.ap[0:96, :], bcs.ap[:, :], ALU.subtract)
            R.give(t4)
            t5 = V((t4,), ve.tensor_copy, bcs.ap[32:64, :], r1.ap[32:64, :])
            t6 = V((t4,), ve.tensor_copy, bcs.ap[64:96, :], r1.ap[64:96, :])
            tbc = V((t6,), TT, bcs.ap[64:96, :], r1.ap[64:96, :], bcs.ap[64:96, :], ALU.subtract)
            r1.give(tbc)
            yield 1
            use(LE)
            for g in range(2):
                bk, a = h.banks.take(), h.tmps.take()
                db = w(p + "db", g, g + 1)
                t = mm((tdr, *bk.free), bk.ap, w(p + "dw", g * 128, g * 128 + 128), dtr.ap[:, :])
                t1 = S((t, *a.free), AF, a.ap, bk.ap, ACT.Abs, bias=db)
                t1 = S((t1,), AF, a.ap, a.ap, ACT.Exp, scale=-1.0)
                t1 = S((t1, t_eps), AF, a.ap, a.ap, ACT.Ln, bias=one)
                t2 = V((t, t1, *dt.free), TS, dt.ap[:, g, :], bk.ap, db, 0.0, ALU.add, ALU.max)
                bk.give(t2)
                t2 = V((t2,), TT, dt.ap[:, g, :], dt.ap[:, g, :], a.ap, ALU.add)
                a.give(t2)
                yield 1
            dtr.give(t)
            tdu = V((t2, *du.free), TT, du.ap[:, :, :], dt.ap[:, :, :], xi.ap[:, :, :], ALU.mult)
            Y = [h.banks.take(), h.banks.take()]
            for s in range(NS):
                Bb = h.banks.take()
                t1 = mm((tbc, *Bb.free), Bb.ap, selbc[:, s:s + 1].broadcast_to([96, 128]), bcs.ap[:, :])
                Cb = h.banks.take()
                t2 = mm(Cb.free, Cb.ap, selbc[:, 16 + s:17 + s].broadcast_to([96, 128]), bcs.ap[:, :])
                a, bb, hh = ring_a.take(), ring_b.take(), ring_h.take()
                for g in range(2):
                    ta = S((tdu, t_am, t_a0, *a.free), AF, a.ap[:, g * T + 1:(g + 1) * T], dt.ap[:, g, 1:], ACT.Exp,
                           scale=Am[:, 32 * k + 16 * g + s:32 * k + 16 * g + s + 1])
                tb = V((t1, tdu, *bb.free), TT, two(bb.ap[:, :]), du.ap[:, :, :],
                       Bb.ap.unsqueeze(1).broadcast_to([128, 2, T]), ALU.mult)
                Bb.give(tb)
                th = V((ta, tb, *hh.free), SCAN, hh.ap[:, :], a.ap[:, :], bb.ap[:, :], 0.0, ALU.mult, ALU.add)
                a.give(th)
                tc = V((th, t2), TT, two(bb.ap[:, :]), two(hh.ap[:, :]),
                       Cb.ap.unsqueeze(1).broadcast_to([128, 2, T]), ALU.mult)
                Cb.give(tc)
                hh.give(tc)
                for g in range(2):
                    ty = mm((tc, *Y[g].free), Y[g].ap, w("ident"), bb.ap[:, g * T:(g + 1) * T],
                            start=s == 0, stop=s == NS - 1)
                bb.give(ty)
                yield 3
            bcs.give(t2)
            dt.give(ta)
            for g in range(2):
                t = V((ty, *du.free), STT, du.ap[:, g, :], xi.ap[:, g, :], w(p + "dd", g, g + 1), Y[g].ap,
                      ALU.mult, ALU.add)
                Y[g].give(t)
            xi.give(t)
            t = V((t, *tz), TT, du.ap[:, :, :], du.ap[:, :, :], z.ap[:, :, :], ALU.mult)
            z.give(t)
            O, y = h.banks.take(), m_y.take()
            for g in range(2):
                t1 = mm((t, *O.free), O.ap, w(p + "op", g * 128, g * 128 + 128), du.ap[:, g, :],
                        start=g == 0, stop=g == 1)
            du.give(t1)
            use(SG)
            t2 = S((t1, *y.free), AF, y.ap[:, :], O.ap, ACT.Sigmoid)
            O.give(t2)
            yield 1
            return y, t2, tlast

        def l1_attn(h, b, tx):
            x = X[b][:, :]
            hh, th = ln(h, x, tx)
            yield 1
            hc = hh.ap[:, PAD:]
            rev = m_rev.take()
            tr = S((th, *rev.free), AF, rev.ap[:, :], hc[:, ::-1], ACT.Copy)
            yf, tf, _ = yield from mamba_dir(h, "mf_", hc, (th,))
            yb, tb, t_in = yield from mamba_dir(h, "mb_", rev.ap[:, :], (tr,))
            rev.give(t_in)
            t1 = V((tf, tb), TT, yf.ap[:, :], yf.ap[:, :], yb.ap[:, ::-1], ALU.add)
            yb.give(t1)
            A, r, t2 = rms(h, yf.ap[:, :], (t1,), "cenh", e5)
            t3 = V((t2,), TT, r.ap, A.ap, r.ap, ALU.mult)
            yf.give(t2)
            A.give(t3)
            t4 = V((t3,), STT, r.ap, r.ap, w("lng"), hc, ALU.mult, ALU.add)
            hh.give(t4)
            t5 = V((t4,), STT, x, r.ap, w("lnb"), x, ALU.add, ALU.add)
            r.give(t5)
            yield 1
            return (t5,)

        def l2_ffn(h, b, tx):
            x = X[b][:, :]
            hh, th = ln(h, x, tx)
            yield 1
            hc = hh.ap[:, PAD:]
            sm = h.small.take()
            e, rec, t1 = softmax_rows(h, hc, (th, wl[3]), "l2r", 16, sm)
            m1, t2 = first_max(sm.ap, e, 80, 16, "rev16", (t1,))
            e2 = sm.ap[:, 160:224].rearrange("p (t e) -> p t e", e=16)
            t3 = V((t2,), STT, e2, m1, -2.0, e, ALU.mult, ALU.add)
            m2, t4 = first_max(sm.ap, e2, 240, 16, "rev16", (t3,))
            t5 = V((t4,), TT, m1, m1, m2, ALU.add)
            t6 = V((t5,), STT, e, e, 0.5, m1, ALU.mult, ALU.mult)
            t7 = V((t6,), TT, e, e, bc(rec, 16), ALU.mult)
            cT, tc, ts = split_T(h, e, 16, (t7,))
            sm.give(ts)
            yield 1
            O = h.banks.take()
            use(SI)
            for i in range(9):
                Gt, U = h.banks.take(), h.banks.take()
                wg = w("l2g", 128 * i, 128 * i + 128) if i < 8 else w("sg")
                wu = w("l2u", 128 * i, 128 * i + 128) if i < 8 else w("su")
                t1 = mm((th, wl[4], *Gt.free), Gt.ap, wg, hc)
                t2 = mm(U.free, U.ap, wu, hc)
                g = h.tmps.take()
                t3 = S((t1, *g.free), AF, g.ap, Gt.ap, ACT.Silu)
                Gt.give(t3)
                if i < 8:
                    Cb = h.banks.take()
                    t4 = mm((tc, *Cb.free), Cb.ap, sel16[:, 2 * i:2 * i + 2, :].rearrange("k e f -> k (e f)"),
                            cT.ap[0:48, :])
                    t5 = V((t3, t4), TT, g.ap, g.ap, Cb.ap, ALU.mult)
                    Cb.give(t5)
                    t6 = V((t5, t2), TT, g.ap, g.ap, U.ap, ALU.mult)
                else:
                    cT.give(t4)
                    t6 = V((t3, t2), STT, g.ap, g.ap, 0.5, U.ap, ALU.mult, ALU.mult)
                U.give(t6)
                t7 = mm((t6, *O.free), O.ap, w("l2d", 128 * i, 128 * i + 128) if i < 8 else w("sd"), g.ap,
                        start=i == 0, stop=i == 8)
                g.give(t7)
                yield 1.5
            hh.give(t2)
            t8 = V((t7,), TT, x, x, O.ap, ALU.add)
            O.give(t8)
            return (t8,)

        def l3_ffn(h, b, tx):
            x = X[b][:, :]
            hh, th = ln(h, x, tx)
            yield 1
            hc = hh.ap[:, PAD:]
            sm = h.small.take()
            e, rec, t1 = softmax_rows(h, hc, (th, wl[5]), "l3g", 8, sm, bias="l3gb", floor=1e-4)
            t1 = V((t1,), TT, e, e, bc(rec, 8), ALU.mult)
            m1, t2 = first_max(sm.ap, e, 64, 8, "rev8", (t1,))
            e2 = sm.ap[:, 112:144].rearrange("p (t e) -> p t e", e=8)
            t3 = V((t2,), STT, e2, m1, -2.0, e, ALU.mult, ALU.add)
            m2, t4 = first_max(sm.ap, e2, 160, 8, "rev8", (t3,))
            t5 = V((t4,), TT, m1, m1, m2, ALU.add)
            t6 = V((t5,), STT, e, e, 0.1, m1, ALU.max, ALU.mult)
            t7 = V((t6,), RED, rec, e, AX.X, ALU.add)
            t7 = V((t7,), ve.reciprocal, sm.ap[:, 208:212], rec)
            t8 = V((t7,), STT, e, e, 0.25, bc(sm.ap[:, 208:212], 8), ALU.mult, ALU.mult)
            cT, tc, ts = split_T(h, e, 8, (t8,))
            sm.give(ts)
            cf = h.tmps.take()
            tcf = S((tc, *cf.free), AF, cf.ap[0:24, :], cT.ap[0:24, :], ACT.Copy)
            yield 1
            O = h.banks.take()
            mm((tcf, *O.free), O.ap, w("l3b"), cf.ap[0:24, :], stop=False)
            for i in range(8):
                Cb, xs = h.banks.take(), h.tmps.take()
                t1 = mm((tc, *Cb.free, t_m5), Cb.ap, sel8[:, i:i + 1].broadcast_to([24, 128]), cT.ap[0:24, :])
                t2 = V((t1, *xs.free), TT, xs.ap, hc, Cb.ap, ALU.mult)
                Cb.give(t2)
                t3 = mm((t2,), O.ap, w("l3w", 128 * i, 128 * i + 128), xs.ap, start=False, stop=i == 7)
                xs.give(t3)
                yield 1.2
            cf.give(t3)
            cT.give(t1)
            hh.give(t2)
            t4 = V((t3,), TT, x, x, O.ap, ALU.add)
            O.give(t4)
            return (t4,)

        Qs, Ks = (Pool([sb(f"{n}s{i}", [128, H // 2, T], BF16) for i in range(1)]) for n in "QK")
        t_ks = [V((), ve.memset, s.ap[:, :, :], 1.0) for s in Ks.slots][-1]
        V9 = Pool([sb("V9", [128, NT, H, DH + 1])])
        t_v9 = [V((), ve.memset, s.ap[:, :, :, DH:DH + 1], 1.0) for s in V9.slots][-1]
        SPL = Pool([sb(f"spl{i}", [128, 3, T], BF16) for i in range(2)])
        Pt = Pool([sb(f"pt{i}", [128, NT, T]) for i in range(2)])
        NM = Pool([sb("nmax", [128, NT, H])])
        s_st = [[Counter(sem(f"s_st{q}{i}")) for i in range(2)] for q in range(3)]

        QB, KB = (0, 0, 0, 1, 1, 2), (0, 1, 2, 0, 1, 0)

        def split3(h, q, tq, st, free, parts, counter):
            sp = SPL.take()
            t1 = S((tq, *sp.free), AF, sp.ap[:, 0, :], q.ap, ACT.Copy)
            t2 = V((t1,), TT, q.ap, q.ap, sp.ap[:, 0, :], ALU.subtract)
            t3 = S((t2,), AF, sp.ap[:, 1, :], q.ap, ACT.Copy)
            t4 = V((t3,), TT, sp.ap[:, 2, :], q.ap, sp.ap[:, 1, :], ALU.subtract)
            q.give(t4)
            for a in range(2):
                for j, part in enumerate(parts):
                    for i in range(H // 2):
                        src = sp.ap[16 * i + 8 * a:16 * i + 8 * a + 8, part, :]
                        t5 = SP.dma((t4, *free), counter, sy.dma_start,
                                    st.ap[64 * a + 8 * j:64 * a + 8 * j + 8, i, :], src)
            sp.give(t5)
            return t5

        def attention(h, b, tx, l3):
            x = X[b][:, :]
            n = "a3" if l3 else "a2"
            wt = wl[5] if l3 else wl[4]
            hh, th = ln(h, x, tx)
            yield 1
            hc = hh.ap[:, PAD:]
            qs, ks, v9 = Qs.take(), Ks.take(), V9.take()
            ready = []
            slot = b % 2
            for st, nm, parts, kind in ((qs, "q", QB, 0), (ks, "k", KB, 1)):
                bk, q = h.banks.take(), h.tmps.take()
                t = mm((th, wt, *bk.free), bk.ap, w(n + nm), hc)
                if l3:
                    t = S((t, *q.free), AF, q.ap, bk.ap, ACT.Identity, bias=w("a3b" + nm))
                    bk.give(t)
                    r = h.tmps.take()
                    t2 = S((t, *r.free), AF, r.ap, q.ap, ACT.Square)
                    bk = h.banks.take()
                    t2 = mm((t2, *bk.free), bk.ap, w("bd8"), r.ap)
                    use(LE)
                    t2 = S((t2,), AF, r.ap, bk.ap, ACT.Ln, bias=e6)
                    bk.give(t2)
                    t2 = S((t2,), AF, r.ap, r.ap, ACT.Exp, scale=-0.5)
                    t = V((t2,), STT, q.ap, q.ap, w("a3w" + nm), r.ap, ALU.mult, ALU.mult)
                    r.give(t)
                else:
                    t = S((t, *q.free), AF, q.ap, bk.ap, ACT.Copy, scale=DH ** -0.5 if nm == "q" else 1.0)
                    bk.give(t)
                ready.append(split3(h, q, t, st, (*st.free, t_ks), parts, s_st[kind][slot]))
                yield 1
            bk = h.banks.take()
            for j in range(NT):
                o = bk.ap[:, j * 128:(j + 1) * 128]
                t = mm((*bk.free,), o, hc[:, j * 128:(j + 1) * 128], w(n + "v"), stop=not l3)
                if l3:
                    t = mm((), o, w("ones")[0:1, :], w("a3bv"), start=False)
            hh.give(t)
            tv = S((t, t_v9, *v9.free), AF, v9.ap[:, :, :, 0:DH],
                   bk.ap.rearrange("p (t h d) -> p t h d", t=NT, d=DH), ACT.Copy)
            bk.give(tv)
            yield 1
            nmx = NM.take()
            for hd in range(H):
                i, a = hd // 2, 64 * (hd % 2)
                for qt in range(NT):
                    nk = T if l3 else 128 * (qt + 1)
                    bk = h.banks.take()
                    t = mm((*ready, *bk.free), bk.ap[:, 0:nk], qs.ap[a:a + 48, i, 128 * qt:128 * qt + 128],
                           ks.ap[a:a + 48, i, 0:nk])
                    if not l3:
                        t = mm((t_m3,), bk.ap[:, nk - 128:nk], identb[:, :], mqb[:, :], start=False, skip=True)
                    t1 = V((t, *nmx.free), RED, nmx.ap[:, qt, hd:hd + 1], bk.ap[:, 0:nk], AX.X, ALU.max,
                           negate=True)
                    bk.give(t1)
                    yield 0.7
            cT, t2, t3 = split_T(h, nmx.ap[:, :, :], H, (t1,))
            nmx.give(t3)
            for a in range(2):
                for j in range(3):
                    for i in range(H // 2):
                        r = 64 * a + 48 + j
                        tq = SP.dma((t2, *qs.free), s_st[2][slot], sy.dma_start, qs.ap[r:r + 1, i, :],
                                    cT.ap[16 * j + 2 * i + a:16 * j + 2 * i + a + 1, :])
            cT.give(tq)
            on = h.tmps.take()
            yield 1
            onv = on.ap.rearrange("p (t h d) -> p t h d", t=NT, d=DH)
            for half in range(2):
                O = h.banks.take()
                ov = O.ap[:, 0:NT * 8 * 9].rearrange("p (t h d) -> p t h d", t=NT, d=DH + 1)
                for hl in range(8):
                    hd = 8 * half + hl
                    i, a = hd // 2, 64 * (hd % 2)
                    P = Pt.take()
                    tp = []
                    for kt in range(NT):
                        q0 = 0 if l3 else 128 * kt
                        bk = h.banks.take()
                        t = mm((tq, *bk.free), bk.ap[:, 0:T - q0], ks.ap[a:a + 51, i, 128 * kt:128 * kt + 128],
                               qs.ap[a:a + 51, i, q0:T])
                        if not l3:
                            t = mm((), bk.ap[:, 0:128], identb[:, :], mtb[:, :], start=False, skip=True)
                        use(LE)
                        t = S((t, *P.free), AF, P.ap[:, kt, q0:T], bk.ap[:, 0:T - q0], ACT.Exp)
                        bk.give(t)
                        tp.append(t)
                        yield 0.5
                    for qt in range(NT):
                        ks_ = range(NT) if l3 else range(qt + 1)
                        for kt in ks_:
                            t = mm((tp[kt], tv, *O.free), ov[:, qt, hl, :], P.ap[:, kt, 128 * qt:128 * qt + 128],
                                   v9.ap[:, kt, hd, :], start=kt == 0, stop=kt == ks_[-1])
                    P.give(t)
                    yield 1
                sm = h.small.take()
                rc = sm.ap[:, 0:32].rearrange("p (t h) -> p t h", h=8)
                t1 = V((t, *sm.free), TS, rc, ov[:, :, :, DH], 0.0 if l3 else 1e-8, None, ALU.add)
                t1 = V((t1,), ve.reciprocal, rc, rc)
                t1 = V((t1, *on.free), TT, onv[:, :, 8 * half:8 * half + 8, :], ov[:, :, :, 0:DH],
                       rc.unsqueeze(3).broadcast_to([128, NT, 8, DH]), ALU.mult)
                O.give(t1)
                sm.give(t1)
            qs.give(t)
            ks.give(t)
            v9.give(t)
            bk, oT = h.banks.take(), h.tmps.take()
            for j in range(NT):
                t = PE((t1, *bk.free), te.transpose, bk.ap[:, j * 128:(j + 1) * 128],
                       on.ap[:, j * 128:(j + 1) * 128], w("ident"))
            on.give(t)
            t = S((t, *oT.free), AF, oT.ap, bk.ap, ACT.Copy)
            bk.give(t)
            bk = h.banks.take()
            t = mm((t, *bk.free), bk.ap, w(n + "o"), oT.ap)
            oT.give(t)
            if l3:
                t = V((t,), STT, x, bk.ap, w("a3bo"), x, ALU.add, ALU.add)
            else:
                t = V((t,), TT, x, x, bk.ap, ALU.add)
            bk.give(t)
            yield 1
            return (t,)

        done = {}

        def first(b):
            h, t = HA, (xl[b], wl[0])
            t = yield from l0_ffn(h, b, t)
            t = yield from l0_attn(h, b, t)
            t = yield from l0_ffn(h, b, t)
            t = yield from l1_ffn(h, b, t, 0)
            t = yield from l1_attn(h, b, t)
            t = yield from l1_ffn(h, b, t, 1)
            done[b] = t

        def second(b):
            h, t = HB, done[b]
            t = yield from l2_ffn(h, b, t)
            t = yield from attention(h, b, t, False)
            t = yield from l2_ffn(h, b, t)
            t = yield from l3_ffn(h, b, t)
            t = yield from attention(h, b, t, True)
            t = yield from l3_ffn(h, b, t)
            t = SP.dma(t, s_out, sy.dma_start, out[b], X[b][:, :])
            if b + NX < B:
                xl.append(SP.dma((t,), s_x[b + NX], sy.dma_start, X[b][:, :], xin[b + NX]))

        def weave(a, b, ratio):
            ta = tb = 0.0
            live = [a, b]
            while live[0] or live[1]:
                pick = 0 if live[0] and (not live[1] or ta <= tb) else 1
                try:
                    d = next(live[pick])
                except StopIteration:
                    live[pick] = None
                    continue
                if pick == 0:
                    ta += d / ratio
                else:
                    tb += d

        weave(first(0), None, 1.0)
        for b in range(B):
            weave(first(b + 1) if b + 1 < B else None, second(b), 0.75)
        SP.wait(((s_out, s_out.n),))

        block = ctx.enter_context(nc.Block())

        @block.sync
        def _(eng):
            SP.play(eng)

        @block.tensor
        def _(eng):
            PE.play(eng)

        @block.vector
        def _(eng):
            V.play(eng)

        @block.scalar
        def _(eng):
            S.play(eng)

        @block.gpsimd
        def _(eng):
            G.play(eng)


def layout(i):
    k = np.arange(128)
    c = {}
    eye = np.eye(128, dtype=np.float32)
    c["ident"], c["ones"], c["avg"] = eye, np.ones((128, 128)), np.full((128, 128), 1 / 128)
    c["cen"] = eye - np.float32(1 / 128)
    c["cenh"] = (eye - np.float32(1 / 128)) * np.float32(0.5)
    c["upper"] = k[:, None] <= k[None, :]
    c["rev8"], c["rev16"] = np.tile(8 - np.arange(8), (128, 1)), np.tile(16 - np.arange(16), (128, 1))
    c["mq"] = np.where(k[None, :] > k[:, None], NEG, 0.0)
    c["mt"] = np.where(k[:, None] > k[None, :], NEG, 0.0)
    c["bd8"] = (k[:, None] // 8 == k[None, :] // 8) / 8
    c["selbc"] = np.arange(96)[:, None] % 32 == np.arange(32)[None, :]
    c["sel16"] = np.arange(48)[:, None] % 16 == np.arange(16)[None, :]
    c["sel8"] = np.arange(24)[:, None] % 8 == np.arange(8)[None, :]
    c["wr"], c["wk"], c["wv"] = i["L0_ffn_W_r"].T, i["L0_ffn_W_k"].T, i["L0_ffn_W_v"].T
    c["mur"], c["muk"] = i["L0_ffn_mu_r"][:, None], i["L0_ffn_mu_k"][:, None]
    c["win"], c["wn"] = i["L0_attn_W_in"], i["L0_attn_w_norm"][:, None]
    c["bin"] = i["L0_attn_b_in"].reshape(3, 32).T
    c["wx"], c["bx"] = i["L0_attn_W_x"], i["L0_attn_b_x"][:, None]
    c["wdt"], c["bdt"] = i["L0_attn_W_dt"], i["L0_attn_b_dt"][:, None]
    c["wout"], c["bout"] = i["L0_attn_W_out"], i["L0_attn_b_out"][:, None]
    c["l1g"], c["l1e"], c["l1b"] = i["L1_ffn_Wg"], i["L1_ffn_We"], i["L1_ffn_be"][:, None]

    def halves(a):
        a = a.reshape(2, 128, -1)
        return np.concatenate([a[0], a[1]], axis=1)

    for p in ("mf_", "mb_"):
        q = f"L1_attn_{p[1]}_"
        c[p + "in"] = i[q + "in_proj"].T
        c[p + "cw"], c[p + "cb"] = halves(i[q + "conv_w"]), halves(i[q + "conv_b"])
        xp = i[q + "x_proj"].T
        c[p + "xp"] = halves(np.concatenate([xp[:, 0:64]] + [xp[:, 64:96]] * 3, axis=1))
        c[p + "dw"], c[p + "db"] = i[q + "dt_w"].T, halves(i[q + "dt_b"])
        c[p + "al"], c[p + "dd"], c[p + "op"] = halves(i[q + "A_log"]), halves(i[q + "D"]), halves(i[q + "out_proj"].T)
    c["lng"], c["lnb"] = i["L1_attn_ln_g"][:, None], i["L1_attn_ln_b"][:, None]
    c["l2r"] = i["L2_ffn_Wr"]
    c["l2g"] = i["L2_ffn_Wg"].transpose(1, 0, 2).reshape(128, 1024)
    c["l2u"] = i["L2_ffn_Wu"].transpose(1, 0, 2).reshape(128, 1024)
    c["l2d"] = i["L2_ffn_Wd"].reshape(8, 128, 128).transpose(1, 0, 2).reshape(128, 1024)
    c["sg"], c["su"], c["sd"] = i["L2_ffn_Sg"], i["L2_ffn_Su"], i["L2_ffn_Sd"]
    c["a2q"], c["a2k"], c["a2v"] = i["L2_attn_Wq"].T, i["L2_attn_Wkv"][0:128].T, i["L2_attn_Wkv"][128:256].T
    c["a2o"] = i["L2_attn_Wo"].T
    for j, n in enumerate("qkv"):
        c["a3" + n] = i["L3_attn_Wqkv"][128 * j:128 * j + 128].T
    bq = i["L3_attn_bqkv"]
    c["a3bq"], c["a3bk"], c["a3bv"] = bq[0:128, None], bq[128:256, None], bq[None, 256:384]
    c["a3o"], c["a3bo"] = i["L3_attn_Wo"].T, i["L3_attn_bo"][:, None]
    c["a3wq"], c["a3wk"] = np.tile(i["L3_attn_wq"], 16)[:, None], np.tile(i["L3_attn_wk"], 16)[:, None]
    c["l3g"], c["l3gb"] = i["L3_ffn_gate_W"], i["L3_ffn_gate_b"][None, :]
    c["l3w"] = i["L3_ffn_expert_W"].transpose(1, 0, 2).reshape(128, 1024)
    c["l3b"] = np.tile(i["L3_ffn_expert_b"], (3, 1))
    table = np.zeros((128, WIDTH), np.float32)
    for n, (at, rows, cols) in COLS.items():
        table[0:rows, at:at + cols] = c[n]
    return table


def kernel(**inputs):
    import concourse.bacc as _bacc
    from concourse.bass_utils import run_bass_kernel_spmd as _run

    i = {n: np.asarray(a) for n, a in inputs.items()}
    arrays = {"xin": np.ascontiguousarray(i["L0_attn_x"].transpose(0, 2, 1)), "wts": layout(i)}
    nc = _bacc.Bacc("TRN2", target_bir_lowering=False, num_devices=1)
    xin = nc.dram_tensor("xin", (B, D, T), F32, kind="ExternalInput").ap()
    wts = nc.dram_tensor("wts", (128, WIDTH), F32, kind="ExternalInput").ap()
    out = nc.dram_tensor("out", (B, D, T), F32, kind="ExternalOutput").ap()
    build(nc, xin, wts, out)
    r = _run(nc, [arrays], core_ids=[0])
    return np.ascontiguousarray(r.results[0]["out"].transpose(0, 2, 1))
```

```python
from contextlib import ExitStack

import numpy as np

import concourse.bass as bass
from concourse import mybir

F32 = mybir.dt.float32
BF16 = mybir.dt.bfloat16
ALU = mybir.AluOpType
ACT = mybir.ActivationFunctionType
AX = mybir.AxisListType

B, T, D = 8, 512, 128
NT = T // 128
PAD = 3
H, DH = 16, 8
NS, DR = 16, 64
NEG = -1e30


GROUPS = [
    [("cen", 128, 128), ("cenh", 128, 128), ("avg", 128, 128), ("ident", 128, 128), ("rev8", 128, 8), ("rev16", 128, 16),
     ("wr", 128, 128), ("wk", 128, 128), ("wv", 128, 128), ("mur", 128, 1), ("muk", 128, 1)],
    [("win", 128, 96), ("wn", 128, 1), ("bin", 32, 3), ("wx", 32, 32), ("bx", 32, 1), ("wdt", 32, 32),
     ("bdt", 32, 1), ("wout", 32, 128), ("bout", 128, 1),
     ("l1g", 128, 8), ("l1e", 128, 128), ("l1b", 128, 1), ("selbc", 96, 32)],
    [(p + n, r, c) for p in ("mf_", "mb_") for n, r, c in
     (("in", 128, 512), ("cw", 128, 8), ("cb", 128, 2), ("xp", 128, 320), ("dw", 64, 256), ("db", 128, 2),
      ("al", 128, 32), ("dd", 128, 2), ("op", 128, 256))] + [("lng", 128, 1), ("lnb", 128, 1)],
    [("l2r", 128, 16), ("sel16", 48, 16), ("l2g", 128, 1024), ("l2u", 128, 1024)],
    [("l2d", 128, 1024), ("sg", 128, 128), ("su", 128, 128), ("sd", 128, 128),
     ("a2q", 128, 128), ("a2k", 128, 128), ("a2v", 128, 128), ("a2o", 128, 128)],
    [("bd8", 128, 128), ("a3q", 128, 128), ("a3k", 128, 128), ("a3v", 128, 128), ("a3bq", 128, 1),
     ("a3bk", 128, 1), ("a3bv", 1, 128), ("a3o", 128, 128), ("a3bo", 128, 1), ("a3wq", 128, 1), ("a3wk", 128, 1),
     ("l3g", 128, 8), ("l3gb", 1, 8), ("sel8", 24, 8), ("l3w", 128, 1024), ("l3b", 24, 128)],
]
PASSING = ["ones", "upper", "mq", "mt"]
COLS = {}
EDGE = [0]
for _g in GROUPS:
    _at = EDGE[-1]
    for _n, _r, _c in _g:
        assert _n not in COLS
        COLS[_n] = (_at, _r, _c)
        _at += _c
    EDGE.append(_at)
WIDTH = EDGE[-1]


NOW = [0.0]
SWITCH = 1.3
BIAS = (0.0, 0.0, 0.0, 0.0)


def cells(ap):
    n = 1
    for k in ap.shape[1:]:
        n *= k
    return n


def price_pe(a):
    return max(cells(a[0]), 64) * (4 if a[1].dtype == F32 else 1) / 2400


def price_dve(a):
    return 0.07 + cells(a[1]) * 1.04e-3 if len(a) > 2 else 0.1 + cells(a[0]) * 0.8e-3


def price_act(a):
    return 0.1 + cells(a[0]) * 0.84e-3


def price_pool(a):
    return 0.1 + cells(a[0]) * 2.3e-3


class Counter:

    def __init__(self, sem):
        self.sem, self.n, self.at = sem, 0, {}

    def add(self, k):
        self.n += k
        return self, self.n


class Queue:

    def __init__(self, sem, price):
        self.mine, self.ops, self.seen = Counter(sem), [], {}
        self.before = None
        self.price, self.clock, self.busy = price, 0.0, 0.0

    def wait(self, after):
        need = {}
        for c, v in after:
            need[c] = max(v, need.get(c, 0))
        for c, v in need.items():
            if self.seen.get(c, 0) < v:
                self.seen[c] = v
                self.ops.append((c.sem, v))

    def guess(self, after, cost):
        NOW[0] = max([self.clock] + [c.at[v] for c, v in after if v in c.at])
        self.clock = NOW[0] + cost
        self.busy += cost
        return self.clock

    def __call__(self, after, f, *a, **k):
        if self.before:
            self.before(a)
        self.wait(after)
        self.mine.at[self.mine.n + 1] = self.guess(after, self.price(a)) + 0.15
        self.ops.append((f, a, k, self.mine.sem, 1))
        return self.mine.add(1)

    def op(self, after, f, *a, **k):
        return self, after, self.price(a), lambda: self(after, f, *a, **k), a

    def op_dma(self, after, counter, f, out, in_):
        return self, after, 0.6, lambda: self.dma(after, counter, f, out, in_), ()

    def plain(self, f, *a):
        self.ops.append((f, a, {}, None, 0))

    def dma(self, after, counter, f, out, in_):
        self.wait(after)
        counter.at[counter.n + 16] = self.guess(after, 0.6) + 2.0
        self.ops.append((f, (out, in_), {}, counter.sem, 16))
        return counter.add(16)

    def play(self, eng):
        for op in self.ops:
            if len(op) == 2:
                eng.wait_ge(*op)
            else:
                f, a, k, sem, inc = op
                ins = f(*a, **k)
                if inc:
                    ins.then_inc(sem, inc)


class Slot:

    def __init__(self, ap, pool):
        self.ap, self.free, self.pool = ap, (), pool

    def give(self, *last):
        self.free = last
        self.pool.append(self)


class Pool:
    def __init__(self, aps):
        self.slots = []
        for ap in aps:
            self.slots.append(Slot(ap, self.slots))

    def take(self):
        assert self.slots, "no slot left"
        return self.slots.pop(0)


def build(nc, xin, wts, cst, out):
    ctx = ExitStack()
    with ctx:
        def sb(name, shape, dt=F32):
            return ctx.enter_context(nc.sbuf_tensor(name, shape, dt))

        def sem(name):
            return ctx.enter_context(nc.semaphore(name))

        PE, V, S, G, SP = (Queue(sem("s_" + n), price) for n, price in
                           (("pe", price_pe), ("dve", price_dve), ("act", price_act), ("pool", price_pool),
                            ("sp", None)))
        te, ve, se, ge, sy = nc.tensor, nc.vector, nc.scalar, nc.gpsimd, nc.sync
        TT, TS, STT, RED, SCAN = (ve.tensor_tensor, ve.tensor_scalar, ve.scalar_tensor_tensor,
                                  ve.tensor_reduce, ve.tensor_tensor_scan)
        AF = se.activation

        psum = [ctx.enter_context(nc.psum_tensor(f"ps{i}", [128, 512], F32)) for i in range(8)]
        W = sb("W", [128, WIDTH])
        NX = 5
        X = [sb(f"X{b}", [128, T]) for b in range(NX)]
        X = [X[b % NX] for b in range(B)]

        def w(name, lo=0, hi=None):
            at, rows, cols = COLS[name]
            return W[0:rows, at + lo:at + (cols if hi is None else hi)]

        s_w = [Counter(sem(f"s_w{i}")) for i in range(len(GROUPS))]
        s_x = [Counter(sem(f"s_x{b}")) for b in range(B)]
        s_out = Counter(sem("s_out"))
        wl, xl = [], []
        wl.append(SP.dma((), s_w[0], sy.dma_start, W[:, EDGE[0]:EDGE[1]], wts[:, EDGE[0]:EDGE[1]]))
        xl.append(SP.dma((), s_x[0], sy.dma_start, X[0][:, :], xin[0]))
        for i in range(1, len(GROUPS)):
            wl.append(SP.dma((), s_w[i], sy.dma_start, W[:, EDGE[i]:EDGE[i + 1]], wts[:, EDGE[i]:EDGE[i + 1]]))
        for b in range(1, NX):
            xl.append(SP.dma((), s_x[b], sy.dma_start, X[b][:, :], xin[b]))

        def mm(after, o, l, r, start=True, stop=True, skip=False):
            return PE.op(after, te.matmul, o, l, r, start=start, stop=stop, skip_group_check=skip)

        eps = sb("eps", [128, 4])
        e5, e8, e6, one = (eps[:, i:i + 1] for i in range(4))
        for i, val in enumerate((1e-5, 1e-8, 1e-6, 1.0)):
            t_eps = V((), ve.memset, eps[:, i:i + 1], val)
        tiles = [sb(f"tmp{i}", [128, T]) for i in range(12)]
        t_c = SP.dma((), Counter(sem("s_c")), sy.dma_start, tiles[0][:, :], cst[:, :])
        wr2, wk2 = sb("wr2", [128, 128]), sb("wk2", [128, 128])
        wr1, wk1, winS = w("wr"), w("wk"), w("win")
        om = sb("om", [128, 2])
        t_mu = V((wl[0],), TS, om[:, 0:1], w("mur"), -1.0, 1.0, ALU.mult, ALU.add)
        t_mu = V((wl[0],), TS, om[:, 1:2], w("muk"), -1.0, 1.0, ALU.mult, ALU.add)
        V((t_mu,), TS, wr2[:, :], wr1, om[:, 0:1], None, ALU.mult)
        t = V((), TS, wk2[:, :], wk1, om[:, 1:2], None, ALU.mult)
        V((t,), TS, wr1, wr1, w("mur"), None, ALU.mult)
        t_l0f = V((t,), TS, wk1, wk1, w("muk"), None, ALU.mult)
        identb, upb, oneb = (sb(n, [128, 128], BF16) for n in ("identb", "upb", "oneb"))
        V((), ve.tensor_copy, identb[:, :], w("ident"))
        ones = sb("ones", [1, 128])
        V((), ve.memset, ones[:, :], 1.0)
        mqb, mtb = sb("mqb", [128, 128], BF16), sb("mtb", [128, 128], BF16)
        for i, to in enumerate((oneb, upb, mqb, mtb)):
            t_cb = V((t_c,), ve.tensor_copy, to[:, :], tiles[0][:, 128 * i:128 * i + 128])
        V((wl[1],), TS, winS[:, :], w("win"), w("wn"), None, ALU.mult)
        nbdt = sb("nbdt", [32, 1])
        V((wl[1],), TS, nbdt[:, :], w("bdt"), -1.0, None, ALU.mult)
        selbc = sb("selbc_b", [96, 32], BF16)
        t_l0a = V((wl[1],), ve.tensor_copy, selbc[:, :], w("selbc"))
        Am = sb("Am", [128, 64])
        sel16, sel8 = sb("sel16_b", [48, 16, 64], BF16), sb("sel8_b", [24, 8], BF16)

        table, switches = [None], []

        def table_of(a):
            f = a[2] if len(a) > 2 else None
            return LE if f in (ACT.Exp, ACT.Ln) else SG if f in (ACT.Sigmoid, ACT.Tanh) else SI if f == ACT.Silu else None

        def use(name):
            if table[0] != name:
                table[0] = name
                switches.append(name)
                S.clock += 1.3
                S.plain(se.preload_act_table_set, name)

        LE, SG, SI = "natural_log_exp_and_others", "sigmoid_and_others", "silu_and_others"
        S.before = lambda a: use(table_of(a)) if table_of(a) else None
        S((wl[2],), AF, Am[:, 0:32], w("mf_al"), ACT.Exp)
        t_al = S((), AF, Am[:, 32:64], w("mb_al"), ACT.Exp)
        t_am = V((t_al,), TS, Am[:, :], Am[:, :], -1.0, None, ALU.mult)
        V((wl[3],), ve.tensor_copy, sel16[:, :, :], w("sel16").unsqueeze(2).broadcast_to([48, 16, 64]))
        t_m3 = t_cb
        t_m5 = V((wl[5],), ve.tensor_copy, sel8[:, :], w("sel8"))

        class Shared:
            banks = Pool([p[:, :] for p in psum[2:8]])
            tmps = Pool([t[:, :] for t in tiles])
            tmps.slots[0].free = (t_cb,)
            hs = Pool([sb(f"h{i}", [128, PAD + T]) for i in range(5)])
            tz = [V((), ve.memset, s.ap[:, 0:PAD], 0.0) for s in hs.slots][-1]
            small = Pool([sb(f"sm{i}", [128, 308])[:, :] for i in range(3)])
            cb = Pool([sb(f"cb{i}", [128, 192], BF16)[:, :] for i in range(4)])
            cT = Pool([sb(f"cT{i}", [48, 512], BF16)[:, :] for i in range(4)])

        h = Shared

        def rms(h, x, tx, mat, e, use_center=True):
            if use_center:
                A = (yield h.banks)
                t1 = yield mm((*A.free, *tx), A.ap, w(mat), x)
                src = A.ap
            else:
                A, t1, src = None, None, x
            r = (yield h.tmps)
            t2 = yield S.op((*(tx if t1 is None else (t1,)), *r.free), AF, r.ap, src, ACT.Square)
            Bk = (yield h.banks)
            t3 = yield mm((t2, *Bk.free), Bk.ap, w("avg"), r.ap)
            t4 = yield S.op((t3, t_eps), AF, r.ap, Bk.ap, ACT.Ln, bias=e)
            Bk.give(t4)
            t5 = yield S.op((t4,), AF, r.ap, r.ap, ACT.Exp, scale=-0.5)
            return A, r, t5

        def ln(h, x, tx, mat="cen", e=None):
            A, r, t5 = (yield from rms(h, x, tx, mat, e5 if e is None else e))
            o = (yield h.hs)
            t6 = yield V.op((t5, h.tz, *o.free), TT, o.ap[:, PAD:], A.ap, r.ap, ALU.mult)
            A.give(t6)
            r.give(t6)
            return o, t6

        def l0_ffn(h, b, tx):
            x = X[b][:, :]
            hh, th = (yield from ln(h, x, tx))
            hc, hp = hh.ap[:, PAD:], hh.ap[:, PAD - 1:PAD - 1 + T]
            R, K = (yield h.banks), (yield h.banks)
            yield mm((th, t_l0f, *R.free), R.ap, wr1[:, :], hc, stop=False)
            t1 = yield mm((), R.ap, wr2[:, :], hp, start=False)
            yield mm(K.free, K.ap, wk1[:, :], hc, stop=False)
            t2 = yield mm((), K.ap, wk2[:, :], hp, start=False)
            hh.give(t2)
            r, k = (yield h.tmps), (yield h.tmps)
            t4 = yield S.op((t2, *k.free), AF, k.ap, K.ap, ACT.Relu)
            K.give(t4)
            t4 = yield S.op((t4,), AF, k.ap, k.ap, ACT.Square)
            t3 = yield S.op((t1, *r.free), AF, r.ap, R.ap, ACT.Sigmoid)
            R.give(t3)
            Vk = (yield h.banks)
            t5 = yield mm((t4, *Vk.free), Vk.ap, w("wv"), k.ap)
            k.give(t5)
            t6 = yield V.op((t5, t3), STT, r.ap, Vk.ap, 0.5, r.ap, ALU.mult, ALU.mult)
            Vk.give(t6)
            t7 = yield V.op((t6,), TT, x, x, r.ap, ALU.add)
            r.give(t7)
            return (t7,)

        def l0_attn(h, b, tx):
            x = X[b][:, :]
            hh, th = (yield from ln(h, x, tx))
            hc = hh.ap[:, PAD:]
            _, r, t5 = (yield from rms(h, hc, (th,), None, e8, use_center=False))
            xn = (yield h.tmps)
            t1 = yield V.op((t5, *xn.free), TT, xn.ap, hc, r.ap, ALU.mult)
            r.give(t1)
            uzg = []
            for i in range(3):
                bk = (yield h.banks)
                t = yield mm((t1, t_l0a, *bk.free), bk.ap[0:32, :], winS[:, 32 * i:32 * i + 32], xn.ap)
                uzg.append((bk, t))
            xn.give(t)
            u, z, g = (yield h.tmps), (yield h.tmps), (yield h.tmps)
            tu = yield S.op((uzg[0][1], *u.free), AF, u.ap[0:32, :], uzg[0][0].ap[0:32, :], ACT.Identity, bias=w("bin", 0, 1))
            tz = yield S.op((uzg[1][1], *z.free), AF, z.ap[0:32, :], uzg[1][0].ap[0:32, :], ACT.Identity, bias=w("bin", 1, 2))
            uzg[0][0].give(tu)
            uzg[1][0].give(tz)
            tg = yield S.op((uzg[2][1], *g.free), AF, g.ap[0:32, :], uzg[2][0].ap[0:32, :], ACT.Sigmoid, bias=w("bin", 2, 3))
            uzg[2][0].give(tg)
            U, Z = (yield h.banks), (yield h.banks)
            t1 = yield mm((tu, *U.free), U.ap[0:32, :], w("wx"), u.ap[0:32, :])
            t2 = yield mm((tz, *Z.free), Z.ap[0:32, :], w("wdt"), z.ap[0:32, :])
            tu = yield S.op((t1,), AF, u.ap[0:32, :], U.ap[0:32, :], ACT.Tanh, bias=w("bx"))
            U.give(tu)
            a = (yield h.tmps)
            tz = yield S.op((t2,), AF, z.ap[0:32, :], Z.ap[0:32, :], ACT.Sigmoid, bias=w("bdt"))
            ta = yield S.op((*a.free,), AF, a.ap[0:32, :], Z.ap[0:32, :], ACT.Sigmoid, bias=nbdt[:, :], scale=-1.0)
            Z.give(ta)
            t3 = yield V.op((tu, tz), TT, u.ap[0:32, :], u.ap[0:32, :], z.ap[0:32, :], ALU.mult)
            t4 = yield V.op((t3, ta), SCAN, z.ap[0:32, :], a.ap[0:32, :], u.ap[0:32, :], 0.0, ALU.mult, ALU.add)
            u.give(t4)
            a.give(t4)
            t5 = yield V.op((t4, tg), TT, g.ap[0:32, :], g.ap[0:32, :], z.ap[0:32, :], ALU.mult)
            z.give(t5)
            Y = (yield h.banks)
            t6 = yield mm((t5, *Y.free), Y.ap, w("wout"), g.ap[0:32, :])
            g.give(t6)
            y = (yield h.tmps)
            t7 = yield V.op((t6, *y.free), STT, y.ap, Y.ap, w("bout"), hc, ALU.add, ALU.add)
            Y.give(t7)
            hh.give(t7)
            t8 = yield V.op((t7,), TT, x, x, y.ap, ALU.add)
            y.give(t8)
            return (t8,)

        def first_max(sm, e, at, n, rev, after):
            mask = sm[:, at:at + NT * n].rearrange("p (t e) -> p t e", e=n)
            mx = sm[:, at + NT * n:at + NT * n + NT]
            mb = mx.unsqueeze(2).broadcast_to([128, NT, n])
            rb = w(rev).unsqueeze(1).broadcast_to([128, NT, n])
            t = yield V.op(after, RED, mx, e, AX.X, ALU.max)
            t = yield V.op((t,), TT, mask, e, mb, ALU.is_equal)
            t = yield V.op((t,), TT, mask, mask, rb, ALU.mult)
            t = yield V.op((t,), RED, mx, mask, AX.X, ALU.max)
            return mask, (yield V.op((t,), TT, mask, mask, mb, ALU.is_equal))

        def bc(ap, n):
            return ap.unsqueeze(2).broadcast_to([128, NT, n])

        def softmax_rows(h, hc, after, wr, n, sm, bias=None, floor=None):
            L = (yield h.banks)
            for j in range(NT):
                o = L.ap[:, j * n:(j + 1) * n]
                t = yield mm((*after, *L.free), o, hc[:, j * 128:(j + 1) * 128], w(wr), stop=bias is None)
                if bias is not None:
                    t = yield mm((), o, ones[:, :], w(bias), start=False)
            e = sm.ap[:, 0:NT * n].rearrange("p (t e) -> p t e", e=n)
            mx, sums = sm.ap[:, NT * n:NT * n + NT], sm.ap[:, NT * n + NT:NT * n + 2 * NT]
            l3 = L.ap[:, 0:NT * n].rearrange("p (t e) -> p t e", e=n)
            if floor is not None:
                t = yield V.op((t, *sm.free), TS, e, l3, floor, None, ALU.max)
                L.give(t)
                t1 = yield V.op((t,), RED, mx, e, AX.X, ALU.max)
                t2 = yield V.op((t1,), TT, e, e, bc(mx, n), ALU.subtract)
            else:
                t1 = yield V.op((t, *sm.free), RED, mx, l3, AX.X, ALU.max)
                t2 = yield V.op((t1,), TT, e, l3, bc(mx, n), ALU.subtract)
                L.give(t2)
            t3 = yield S.op((t2,), AF, e, e, ACT.Exp)
            t4 = yield V.op((t3,), RED, sums, e, AX.X, ALU.add)
            t5 = yield V.op((t4,), ve.reciprocal, mx, sums)
            return e, mx, t5

        def split_T(h, c, n, after):
            cb, cT = (yield h.cb), (yield h.cT)
            v = cb.ap[:, 0:NT * 3 * n].rearrange("p (t k e) -> p t k e", k=3, e=n)
            t1 = yield V.op((*after, *cb.free), ve.tensor_copy, v[:, :, 0, :], c)
            t2 = yield V.op((t1,), TT, c, c, v[:, :, 0, :], ALU.subtract)
            t3 = yield V.op((t2,), ve.tensor_copy, v[:, :, 1, :], c)
            t4 = yield V.op((t3,), TT, v[:, :, 2, :], c, v[:, :, 1, :], ALU.subtract)
            bk = (yield h.banks)
            pT = bk.ap[0:3 * n, 0:256].bitcast(BF16)
            for j in range(NT):
                t5 = yield PE.op((t4, t_cb, *bk.free), te.transpose, pT[:, j * 128:(j + 1) * 128],
                        cb.ap[:, j * 3 * n:(j + 1) * 3 * n], identb[:, :])
            cb.give(t5)
            t6 = yield V.op((t5, *cT.free), ve.tensor_copy, cT.ap[0:3 * n, :], pT)
            bk.give(t6)
            return cT, t6, t4

        carry = [[sb(f"carry{i}_{k}", [128, 8]) for k in range(2)] for i in range(2)]
        t_carry = [[(V((), ve.memset, carry[i][k][:, :], 0.0),) for k in range(2)] for i in range(2)]

        def l1_ffn(h, b, tx, which):
            x = X[b][:, :]
            hh, th = (yield from ln(h, x, tx))
            hc = hh.ap[:, PAD:]
            sm = (yield h.small)
            e, rec, t1 = (yield from softmax_rows(h, hc, (th, wl[1]), "l1g", 8, sm))
            mask, t2 = (yield from first_max(sm.ap, e, 64, 8, "rev8", (t1,)))
            mb = (yield h.cb)
            mk = mb.ap[:, 0:32]
            t3 = yield V.op((t2, *mb.free), ve.tensor_copy, mk, sm.ap[:, 64:96])
            C = (yield h.banks)
            for j in range(NT):
                o = C.ap[:, 8 * j:8 * j + 8]
                t4 = yield mm((t3, t_cb, *C.free), o, upb[:, :], mk[:, 8 * j:8 * j + 8], stop=j == 0)
                for i in range(j):
                    t4 = yield mm((), o, oneb[:, :], mk[:, 8 * i:8 * i + 8], start=False, stop=i == j - 1)
            for i in range(NT):
                t4 = yield mm((), C.ap[:, 32:40], oneb[:, :], mk[:, 8 * i:8 * i + 8], start=i == 0, stop=i == NT - 1)
            mb.give(t4)
            old, new = carry[which][b % 2], carry[which][(b + 1) % 2]
            loc = sm.ap[:, 0:32].rearrange("p (t e) -> p t e", e=8)
            t5 = yield V.op((t4, *t_carry[which][b % 2]), TT, loc, C.ap[:, 0:32].rearrange("p (t e) -> p t e", e=8),
                   old[:, :].unsqueeze(1).broadcast_to([128, NT, 8]), ALU.add)
            t6 = yield V.op((), TT, new[:, :], C.ap[:, 32:40], old[:, :], ALU.add)
            t_carry[which][(b + 1) % 2] = (t6,)
            C.give(t6)
            t7 = yield V.op((t5,), STT, loc, loc, 512.0, mask, ALU.is_le, ALU.mult)
            g = sm.ap[:, 128:132]
            t8 = yield V.op((t7,), RED, g, loc, AX.X, ALU.add)
            t9 = yield V.op((t8,), STT, g, g, 0.5, rec, ALU.mult, ALU.mult)
            Gb, Y = (yield h.banks), (yield h.banks)
            for j in range(NT):
                t10 = yield mm((t9, *Gb.free), Gb.ap[:, j * 128:(j + 1) * 128], g[:, j:j + 1].broadcast_to([128, 128]),
                         w("ident"))
            sm.give(t10)
            t11 = yield mm(Y.free, Y.ap, w("l1e"), hc)
            hh.give(t11)
            y = (yield h.tmps)
            t12 = yield S.op((t11, *y.free), AF, y.ap, Y.ap, ACT.Identity, bias=w("l1b"))
            Y.give(t12)
            t13 = yield V.op((t12, t10), TT, y.ap, y.ap, Gb.ap, ALU.mult)
            Gb.give(t13)
            t14 = yield V.op((t13,), TT, x, x, y.ap, ALU.add)
            y.give(t14)
            return (t14,)

        def two(ap):
            return ap.rearrange("p (g n) -> p g n", g=2)

        def pair(name):
            return sb(name, [128, 2, T])

        xpad = sb("xpad", [128, 2, PAD + T])
        t_xp = V((), ve.memset, xpad[:, :, 0:PAD], 0.0)
        m_xi, m_z, m_dt, m_du = (Pool([pair(n)]) for n in ("m_xi", "m_z", "m_dt", "m_du"))
        m_xp = Pool([xpad])
        m_bc = Pool([sb("m_bc", [96, T], BF16)])
        m_Y = Pool([p[:, :] for p in psum[0:2]])
        ring_a = Pool([sb(f"ra{i}", [128, 2 * T]) for i in range(2)])
        t_a0 = [V((), ve.memset, two(s.ap[:, :])[:, :, 0:1], 0.0) for s in ring_a.slots][-1]
        ring_b = Pool([sb(f"rb{i}", [128, 2 * T]) for i in range(3)])
        ring_h = Pool([sb(f"rh{i}", [128, 2 * T]) for i in range(2)])

        def mamba_dir(h, p, src, tsrc):
            k = 0 if p == "mf_" else 1
            xp, z = (yield m_xp), (yield m_z)
            xi, dt, du = (yield m_xi), (yield m_dt), (yield m_du)
            c = du
            txp, tz = [], []
            for m in range(4):
                bk = (yield h.banks)
                t = yield mm((*tsrc, wl[2], *bk.free), bk.ap, w(p + "in", m * 128, m * 128 + 128), src)
                if m < 2:
                    t2 = yield S.op((t, t_xp, *xp.free), AF, xp.ap[:, m, PAD:], bk.ap, ACT.Copy)
                    txp.append(t2)
                else:
                    t2 = yield S.op((t, *z.free), AF, z.ap[:, m - 2, :], bk.ap, ACT.Silu)
                    tz.append(t2)
                bk.give(t2)
            tlast = t
            for g in range(2):
                cw = w(p + "cw")
                t = yield V.op((txp[g], *c.free), TS, c.ap[:, g, :], xp.ap[:, g, 0:T], cw[:, 4 * g:4 * g + 1], None, ALU.mult)
                for j in range(1, 4):
                    t = yield V.op((t,), STT, c.ap[:, g, :], xp.ap[:, g, j:j + T], cw[:, 4 * g + j:4 * g + j + 1],
                          c.ap[:, g, :], ALU.mult, ALU.add)
                t = yield S.op((t, *xi.free), AF, xi.ap[:, g, :], c.ap[:, g, :], ACT.Silu, bias=w(p + "cb", g, g + 1))
            txi = t
            xp.give(t)
            Q, R = (yield h.banks), (yield h.banks)
            for g in range(2):
                t1 = yield mm((txi, *Q.free), Q.ap[0:64, :], w(p + "xp", g * 160, g * 160 + 64), xi.ap[:, g, :],
                        start=g == 0, stop=g == 1)
            for g in range(2):
                t2 = yield mm(R.free, R.ap[0:96, :], w(p + "xp", g * 160 + 64, g * 160 + 160), xi.ap[:, g, :],
                        start=g == 0, stop=g == 1)
            dtr, bcs, r1 = (yield h.tmps), (yield m_bc), (yield h.tmps)
            tdr = yield S.op((t1, *dtr.free), AF, dtr.ap[0:64, :], Q.ap[0:64, :], ACT.Copy)
            Q.give(tdr)
            t3 = yield S.op((t2, *bcs.free), AF, bcs.ap[:, :], R.ap[0:96, :], ACT.Copy)
            t4 = yield V.op((t3, *r1.free), TT, r1.ap[0:96, :], R.ap[0:96, :], bcs.ap[:, :], ALU.subtract)
            R.give(t4)
            t5 = yield V.op((t4,), ve.tensor_copy, bcs.ap[32:64, :], r1.ap[32:64, :])
            t6 = yield V.op((t4,), ve.tensor_copy, bcs.ap[64:96, :], r1.ap[64:96, :])
            tbc = yield V.op((t6,), TT, bcs.ap[64:96, :], r1.ap[64:96, :], bcs.ap[64:96, :], ALU.subtract)
            r1.give(tbc)
            for g in range(2):
                bk, a = (yield h.banks), (yield h.tmps)
                db = w(p + "db", g, g + 1)
                t = yield mm((tdr, *bk.free), bk.ap, w(p + "dw", g * 128, g * 128 + 128), dtr.ap[0:64, :])
                t1 = yield S.op((t, *a.free), AF, a.ap, bk.ap, ACT.Abs, bias=db)
                t1 = yield S.op((t1,), AF, a.ap, a.ap, ACT.Exp, scale=-1.0)
                t1 = yield S.op((t1, t_eps), AF, a.ap, a.ap, ACT.Ln, bias=one)
                t2 = yield V.op((t, t1, *dt.free), TS, dt.ap[:, g, :], bk.ap, db, 0.0, ALU.add, ALU.max)
                bk.give(t2)
                t2 = yield V.op((t2,), TT, dt.ap[:, g, :], dt.ap[:, g, :], a.ap, ALU.add)
                a.give(t2)
            dtr.give(t)
            tdu = yield V.op((t2, txi), TT, du.ap[:, :, :], dt.ap[:, :, :], xi.ap[:, :, :], ALU.mult)
            Y = [(yield m_Y), (yield m_Y)]
            for s in range(NS):
                Bb = (yield h.banks)
                t1 = yield mm((tbc, *Bb.free), Bb.ap, selbc[:, s:s + 1].broadcast_to([96, 128]), bcs.ap[:, :])
                Cb = (yield h.banks)
                t2 = yield mm(Cb.free, Cb.ap, selbc[:, 16 + s:17 + s].broadcast_to([96, 128]), bcs.ap[:, :])
                a, bb, hh = (yield ring_a), (yield ring_b), (yield ring_h)
                for g in range(2):
                    ta = yield S.op((tdu, t_am, t_a0, *a.free), AF, a.ap[:, g * T + 1:(g + 1) * T], dt.ap[:, g, 1:], ACT.Exp,
                           scale=Am[:, 32 * k + 16 * g + s:32 * k + 16 * g + s + 1])
                tb = yield V.op((t1, tdu, *bb.free), TT, two(bb.ap[:, :]), du.ap[:, :, :],
                       Bb.ap.unsqueeze(1).broadcast_to([128, 2, T]), ALU.mult)
                Bb.give(tb)
                th = yield V.op((ta, tb, *hh.free), SCAN, hh.ap[:, :], a.ap[:, :], bb.ap[:, :], 0.0, ALU.mult, ALU.add)
                a.give(th)
                tc = yield V.op((th, t2), TT, two(bb.ap[:, :]), two(hh.ap[:, :]),
                       Cb.ap.unsqueeze(1).broadcast_to([128, 2, T]), ALU.mult)
                Cb.give(tc)
                hh.give(tc)
                for g in range(2):
                    ty = yield mm((tc, *Y[g].free), Y[g].ap, w("ident"), bb.ap[:, g * T:(g + 1) * T],
                            start=s == 0, stop=s == NS - 1)
                bb.give(ty)
            bcs.give(t2)
            dt.give(ta)
            for g in range(2):
                t = yield V.op((ty,), STT, du.ap[:, g, :], xi.ap[:, g, :], w(p + "dd", g, g + 1), Y[g].ap,
                      ALU.mult, ALU.add)
                Y[g].give(t)
            xi.give(t)
            t = yield V.op((t, *tz), TT, du.ap[:, :, :], du.ap[:, :, :], z.ap[:, :, :], ALU.mult)
            z.give(t)
            O, y = (yield h.banks), (yield h.tmps)
            for g in range(2):
                t1 = yield mm((t, *O.free), O.ap, w(p + "op", g * 128, g * 128 + 128), du.ap[:, g, :],
                        start=g == 0, stop=g == 1)
            du.give(t1)
            t2 = yield S.op((t1, *y.free), AF, y.ap, O.ap, ACT.Sigmoid)
            O.give(t2)
            return y, t2, tlast

        def l1_attn(h, b, tx):
            x = X[b][:, :]
            hh, th = (yield from ln(h, x, tx))
            hc = hh.ap[:, PAD:]
            rev = (yield h.tmps)
            tr = yield S.op((th, *rev.free), AF, rev.ap[:, :], hc[:, ::-1], ACT.Copy)
            yf, tf, _ = yield from mamba_dir(h, "mf_", hc, (th,))
            yb, tb, t_in = yield from mamba_dir(h, "mb_", rev.ap[:, :], (tr,))
            rev.give(t_in)
            t1 = yield V.op((tf, tb), TT, yf.ap[:, :], yf.ap[:, :], yb.ap[:, ::-1], ALU.add)
            yb.give(t1)
            A, r, t2 = (yield from rms(h, yf.ap[:, :], (t1,), "cenh", e5))
            t3 = yield V.op((t2,), TT, r.ap, A.ap, r.ap, ALU.mult)
            yf.give(t2)
            A.give(t3)
            t4 = yield V.op((t3,), STT, r.ap, r.ap, w("lng"), hc, ALU.mult, ALU.add)
            hh.give(t4)
            t5 = yield V.op((t4,), STT, x, r.ap, w("lnb"), x, ALU.add, ALU.add)
            r.give(t5)
            return (t5,)

        def l2_ffn(h, b, tx):
            x = X[b][:, :]
            hh, th = (yield from ln(h, x, tx))
            hc = hh.ap[:, PAD:]
            sm = (yield h.small)
            e, rec, t1 = (yield from softmax_rows(h, hc, (th, wl[3]), "l2r", 16, sm))
            m1, t2 = (yield from first_max(sm.ap, e, 80, 16, "rev16", (t1,)))
            e2 = sm.ap[:, 160:224].rearrange("p (t e) -> p t e", e=16)
            t3 = yield V.op((t2,), STT, e2, m1, -2.0, e, ALU.mult, ALU.add)
            m2, t4 = (yield from first_max(sm.ap, e2, 240, 16, "rev16", (t3,)))
            t5 = yield V.op((t4,), TT, m1, m1, m2, ALU.add)
            t6 = yield V.op((t5,), STT, e, e, 0.5, m1, ALU.mult, ALU.mult)
            t7 = yield V.op((t6,), TT, e, e, bc(rec, 16), ALU.mult)
            cT, tc, ts = (yield from split_T(h, e, 16, (t7,)))
            sm.give(ts)
            O = (yield h.banks)
            for i in range(9):
                Gt, U = (yield h.banks), (yield h.banks)
                wg = w("l2g", 128 * i, 128 * i + 128) if i < 8 else w("sg")
                wu = w("l2u", 128 * i, 128 * i + 128) if i < 8 else w("su")
                t1 = yield mm((th, wl[4], *Gt.free), Gt.ap, wg, hc)
                t2 = yield mm(U.free, U.ap, wu, hc)
                g = (yield h.tmps)
                t3 = yield S.op((t1, *g.free), AF, g.ap, Gt.ap, ACT.Silu)
                Gt.give(t3)
                if i < 8:
                    Cb = (yield h.banks)
                    t4 = yield mm((tc, *Cb.free), Cb.ap, sel16[:, 2 * i:2 * i + 2, :].rearrange("k e f -> k (e f)"),
                            cT.ap[0:48, :])
                    t5 = yield V.op((t3, t4), TT, g.ap, g.ap, Cb.ap, ALU.mult)
                    Cb.give(t5)
                    t6 = yield V.op((t5, t2), TT, g.ap, g.ap, U.ap, ALU.mult)
                else:
                    cT.give(t4)
                    t6 = yield V.op((t3, t2), STT, g.ap, g.ap, 0.5, U.ap, ALU.mult, ALU.mult)
                U.give(t6)
                t7 = yield mm((t6, *O.free), O.ap, w("l2d", 128 * i, 128 * i + 128) if i < 8 else w("sd"), g.ap,
                        start=i == 0, stop=i == 8)
                g.give(t7)
            hh.give(t2)
            t8 = yield V.op((t7,), TT, x, x, O.ap, ALU.add)
            O.give(t8)
            return (t8,)

        def l3_ffn(h, b, tx):
            x = X[b][:, :]
            hh, th = (yield from ln(h, x, tx))
            hc = hh.ap[:, PAD:]
            sm = (yield h.small)
            e, rec, t1 = (yield from softmax_rows(h, hc, (th, wl[5]), "l3g", 8, sm, bias="l3gb", floor=1e-4))
            t1 = yield V.op((t1,), TT, e, e, bc(rec, 8), ALU.mult)
            m1, t2 = (yield from first_max(sm.ap, e, 64, 8, "rev8", (t1,)))
            e2 = sm.ap[:, 112:144].rearrange("p (t e) -> p t e", e=8)
            t3 = yield V.op((t2,), STT, e2, m1, -2.0, e, ALU.mult, ALU.add)
            m2, t4 = (yield from first_max(sm.ap, e2, 160, 8, "rev8", (t3,)))
            t5 = yield V.op((t4,), TT, m1, m1, m2, ALU.add)
            t6 = yield V.op((t5,), STT, e, e, 0.1, m1, ALU.max, ALU.mult)
            t7 = yield V.op((t6,), RED, rec, e, AX.X, ALU.add)
            t7 = yield V.op((t7,), ve.reciprocal, sm.ap[:, 208:212], rec)
            t8 = yield V.op((t7,), STT, e, e, 0.25, bc(sm.ap[:, 208:212], 8), ALU.mult, ALU.mult)
            cT, tc, ts = (yield from split_T(h, e, 8, (t8,)))
            sm.give(ts)
            cf = (yield h.tmps)
            tcf = yield S.op((tc, *cf.free), AF, cf.ap[0:24, :], cT.ap[0:24, :], ACT.Copy)
            O = (yield h.banks)
            yield mm((tcf, *O.free), O.ap, w("l3b"), cf.ap[0:24, :], stop=False)
            for i in range(8):
                Cb, xs = (yield h.banks), (yield h.tmps)
                t1 = yield mm((tc, *Cb.free, t_m5), Cb.ap, sel8[:, i:i + 1].broadcast_to([24, 128]), cT.ap[0:24, :])
                t2 = yield V.op((t1, *xs.free), TT, xs.ap, hc, Cb.ap, ALU.mult)
                Cb.give(t2)
                t3 = yield mm((t2,), O.ap, w("l3w", 128 * i, 128 * i + 128), xs.ap, start=False, stop=i == 7)
                xs.give(t3)
            cf.give(t3)
            cT.give(t1)
            hh.give(t2)
            t4 = yield V.op((t3,), TT, x, x, O.ap, ALU.add)
            O.give(t4)
            return (t4,)

        Qs, Ks = (Pool([sb(f"{n}s{i}", [128, H // 2, T], BF16) for i in range(2)]) for n in "QK")
        t_ks = [V((), ve.memset, s.ap[:, :, :], 1.0) for s in Ks.slots][-1]
        V9 = Pool([sb(f"V9{i}", [128, NT, H, DH + 1]) for i in range(2)])
        t_v9 = [V((), ve.memset, s.ap[:, :, :, DH:DH + 1], 1.0) for s in V9.slots][-1]
        SPL = Pool([sb(f"spl{i}", [128, 3, T], BF16) for i in range(2)])
        Pt = Pool([sb(f"pt{i}", [128, T]) for i in range(8)])
        NM = Pool([sb(f"nmax{i}", [128, NT, H]) for i in range(2)])
        s_st = [[Counter(sem(f"s_st{q}{i}")) for i in range(4)] for q in range(3)]

        DR = Pool([nc.dram_tensor(f"parts{i}", (3, 128, T), BF16, kind="Internal").ap() for i in range(4)])
        for i, slot in enumerate(DR.slots):
            slot.n = i
        s_dr = [Counter(sem(f"s_dr{i}")) for i in range(4)]

        QB, KB = (0, 0, 0, 1, 1, 2), (0, 1, 2, 0, 1, 0)

        def split3(h, q, tq, st, free, parts, counter):
            sp = (yield SPL)
            t1 = yield S.op((tq, *sp.free), AF, sp.ap[:, 0, :], q.ap, ACT.Copy)
            t2 = yield V.op((t1,), TT, q.ap, q.ap, sp.ap[:, 0, :], ALU.subtract)
            t3 = yield S.op((t2,), AF, sp.ap[:, 1, :], q.ap, ACT.Copy)
            t4 = yield V.op((t3,), TT, sp.ap[:, 2, :], q.ap, sp.ap[:, 1, :], ALU.subtract)
            q.give(t4)
            dr = (yield DR)
            t = yield SP.op_dma((t4, *dr.free), s_dr[dr.n], sy.dma_start, dr.ap.rearrange("k p n -> p k n"), sp.ap[:, :, :])
            sp.give(t)
            for a in range(2):
                for j, part in enumerate(parts):
                    src = dr.ap[part, 64 * a:64 * a + 64, :].rearrange("(i d) n -> d i n", d=DH)
                    t5 = yield SP.op_dma((t, *free), counter, sy.dma_start,
                                st.ap[64 * a + 8 * j:64 * a + 8 * j + 8, :, :], src)
            dr.give(t5)
            return t5

        def attention(h, b, tx, l3):
            x = X[b][:, :]
            n = "a3" if l3 else "a2"
            wt = wl[5] if l3 else wl[4]
            hh, th = (yield from ln(h, x, tx))
            hc = hh.ap[:, PAD:]
            qs, ks, v9 = (yield Qs), (yield Ks), (yield V9)
            ready = []
            slot = b % 2 + 2 * l3
            for st, nm, parts, kind in ((qs, "q", QB, 0), (ks, "k", KB, 1)):
                bk, q = (yield h.banks), (yield h.tmps)
                t = yield mm((th, wt, *bk.free), bk.ap, w(n + nm), hc)
                if l3:
                    t = yield S.op((t, *q.free), AF, q.ap, bk.ap, ACT.Identity, bias=w("a3b" + nm))
                    bk.give(t)
                    r = (yield h.tmps)
                    t2 = yield S.op((t, *r.free), AF, r.ap, q.ap, ACT.Square)
                    bk = (yield h.banks)
                    t2 = yield mm((t2, *bk.free), bk.ap, w("bd8"), r.ap)
                    t2 = yield S.op((t2,), AF, r.ap, bk.ap, ACT.Ln, bias=e6)
                    bk.give(t2)
                    t2 = yield S.op((t2,), AF, r.ap, r.ap, ACT.Exp, scale=-0.5)
                    t = yield V.op((t2,), STT, q.ap, q.ap, w("a3w" + nm), r.ap, ALU.mult, ALU.mult)
                    r.give(t)
                else:
                    t = yield S.op((t, *q.free), AF, q.ap, bk.ap, ACT.Copy, scale=DH ** -0.5 if nm == "q" else 1.0)
                    bk.give(t)
                ready.append((yield from split3(h, q, t, st, (*st.free, t_ks), parts, s_st[kind][slot])))
            bk = (yield h.banks)
            for j in range(NT):
                o = bk.ap[:, j * 128:(j + 1) * 128]
                t = yield mm((*bk.free,), o, hc[:, j * 128:(j + 1) * 128], w(n + "v"), stop=not l3)
                if l3:
                    t = yield mm((), o, ones[:, :], w("a3bv"), start=False)
            hh.give(t)
            tv = yield S.op((t, t_v9, *v9.free), AF, v9.ap[:, :, :, 0:DH],
                   bk.ap.rearrange("p (t h d) -> p t h d", t=NT, d=DH), ACT.Copy)
            bk.give(tv)
            nmx = (yield NM)
            for hd in range(H):
                i, a = hd % 8, 64 * (hd // 8)
                for qt in range(NT):
                    nk = T if l3 else 128 * (qt + 1)
                    bk = (yield h.banks)
                    t = yield mm((*ready, *bk.free), bk.ap[:, 0:nk], qs.ap[a:a + 48, i, 128 * qt:128 * qt + 128],
                           ks.ap[a:a + 48, i, 0:nk])
                    if not l3:
                        t = yield mm((t_m3,), bk.ap[:, nk - 128:nk], identb[:, :], mqb[:, :], start=False, skip=True)
                    t1 = yield V.op((t, *nmx.free), RED, nmx.ap[:, qt, hd:hd + 1], bk.ap[:, 0:nk], AX.X, ALU.max,
                           negate=True)
                    bk.give(t1)
            cT, t2, t3 = (yield from split_T(h, nmx.ap[:, :, :], H, (t1,)))
            nmx.give(t3)
            for a in range(2):
                for j in range(3):
                    r = 64 * a + 48 + j
                    tq = yield SP.op_dma((t2, *qs.free), s_st[2][slot], sy.dma_start, qs.ap[r:r + 1, :, :],
                                cT.ap[16 * j + 8 * a:16 * j + 8 * a + 8, :])
            cT.give(tq)
            on = (yield h.tmps)
            onv = on.ap.rearrange("p (t h d) -> p t h d", t=NT, d=DH)
            for half in range(2):
                O = (yield h.banks)
                ov = O.ap[:, 0:NT * 8 * 9].rearrange("p (t h d) -> p t h d", t=NT, d=DH + 1)
                for hl in range(8):
                    hd = 8 * half + hl
                    i, a = hd % 8, 64 * (hd // 8)
                    P, tp = [], []
                    for kt in range(NT):
                        P.append((yield Pt))
                    for kt in range(NT):
                        q0 = 0 if l3 else 128 * kt
                        bk = (yield h.banks)
                        t = yield mm((tq, *bk.free), bk.ap[:, 0:T - q0], ks.ap[a:a + 51, i, 128 * kt:128 * kt + 128],
                               qs.ap[a:a + 51, i, q0:T])
                        if not l3:
                            t = yield mm((), bk.ap[:, 0:128], identb[:, :], mtb[:, :], start=False, skip=True)
                        t = yield S.op((t, *P[kt].free), AF, P[kt].ap[:, q0:T], bk.ap[:, 0:T - q0], ACT.Exp)
                        bk.give(t)
                        tp.append(t)
                    for qt in range(NT):
                        ks_ = range(NT) if l3 else range(qt + 1)
                        for kt in ks_:
                            t = yield mm((tp[kt], tv, *O.free), ov[:, qt, hl, :], P[kt].ap[:, 128 * qt:128 * qt + 128],
                                   v9.ap[:, kt, hd, :], start=kt == 0, stop=kt == ks_[-1])
                    for kt in range(NT):
                        P[kt].give(t)
                sm = (yield h.small)
                rc = sm.ap[:, 0:32].rearrange("p (t h) -> p t h", h=8)
                t1 = yield V.op((t, *sm.free), TS, rc, ov[:, :, :, DH], 0.0 if l3 else 1e-8, None, ALU.add)
                t1 = yield V.op((t1,), ve.reciprocal, rc, rc)
                t1 = yield V.op((t1, *on.free), TT, onv[:, :, 8 * half:8 * half + 8, :], ov[:, :, :, 0:DH],
                       rc.unsqueeze(3).broadcast_to([128, NT, 8, DH]), ALU.mult)
                O.give(t1)
                sm.give(t1)
            qs.give(t)
            ks.give(t)
            v9.give(t)
            bk, oT = (yield h.banks), (yield h.tmps)
            for j in range(NT):
                t = yield PE.op((t1, *bk.free), te.transpose, bk.ap[:, j * 128:(j + 1) * 128],
                       on.ap[:, j * 128:(j + 1) * 128], w("ident"))
            on.give(t)
            t = yield S.op((t, *oT.free), AF, oT.ap, bk.ap, ACT.Copy)
            bk.give(t)
            bk = (yield h.banks)
            t = yield mm((t, *bk.free), bk.ap, w(n + "o"), oT.ap)
            oT.give(t)
            if l3:
                t = yield V.op((t,), STT, x, bk.ap, w("a3bo"), x, ALU.add, ALU.add)
            else:
                t = yield V.op((t,), TT, x, x, bk.ap, ALU.add)
            bk.give(t)
            return (t,)

        def part1(b, t):
            t = yield from l0_ffn(h, b, (xl[b], wl[0]))
            t = yield from l0_attn(h, b, t)
            t = yield from l0_ffn(h, b, t)
            return (yield from l1_ffn(h, b, t, 0))

        def part2(b, t):
            t = yield from l1_attn(h, b, t)
            return (yield from l1_ffn(h, b, t, 1))

        def part3(b, t):
            t = yield from l2_ffn(h, b, t)
            t = yield from attention(h, b, t, False)
            return (yield from l2_ffn(h, b, t))

        def part4(b, t):
            t = yield from l3_ffn(h, b, t)
            t = yield from attention(h, b, t, True)
            t = yield from l3_ffn(h, b, t)
            t = SP.dma(t, s_out, sy.dma_start, out[b], X[b][:, :])
            if b + NX < B:
                xl.append(SP.dma((t,), s_x[b + NX], sy.dma_start, X[b][:, :], xin[b + NX]))
            return t

        parts = [part1, part2, part3, part4]
        claims = [{h.banks: 3, h.tmps: 4}, {h.banks: 2, h.tmps: 4}, {h.banks: 4, h.tmps: 3}, {h.banks: 4, h.tmps: 3}]
        size = {h.banks: len(h.banks.slots), h.tmps: len(h.tmps.slots)}
        held = [{h.banks: [], h.tmps: []} for _ in parts]

        def safe(pool, p):
            have = [len(x[pool]) for x in held]
            have[p] += 1
            left, todo = size[pool] - sum(have), set(range(len(parts)))
            if left < 0:
                return False
            while todo:
                ends = [q for q in todo if claims[q][pool] - have[q] <= left]
                if not ends:
                    return False
                for q in ends:
                    left += have[q]
                    todo.remove(q)
            return True

        live, at, result = [None] * 4, [0] * 4, {}
        wish = [None] * 4

        def step(p, value):
            try:
                wish[p] = live[p].send(value)
            except StopIteration as stop:
                result[p, at[p]] = stop.value
                live[p], wish[p] = None, None
                at[p] += 1

        def start_of(o):
            q, after, cost, _, a = o
            t = max([q.clock] + [c.at[v] for c, v in after if v in c.at])
            if q is S and table_of(a) not in (None, table[0]):
                t += SWITCH
            return t

        while any(n < B for n in at):
            for p in range(4):
                if live[p] is None and at[p] < B:
                    b = at[p]
                    if p == 0 and b < len(xl) and b < at[3] + NX and b <= at[1] + 1:
                        live[p] = part1(b, None)
                        step(p, None)
                    elif p > 0 and (p - 1, b) in result:
                        live[p] = parts[p](b, result[p - 1, b])
                        step(p, None)
                while isinstance(wish[p], Pool):
                    pool = wish[p]
                    if not pool.slots:
                        break
                    if pool in size:
                        for x in held:
                            x[pool] = [s for s in x[pool] if s not in pool.slots]
                        if not safe(pool, p):
                            break
                        slot = pool.take()
                        held[p][pool].append(slot)
                    else:
                        slot = pool.take()
                    step(p, slot)
            can = [q for q in range(4) if isinstance(wish[q], tuple)]
            if not can:
                assert not any(live), "the parts block each other"
                continue
            p = min(can, key=lambda q: (start_of(wish[q]) - BIAS[q], -q))
            step(p, wish[p][3]())
        print("estimate", [(round(q.clock), round(q.busy)) for q in (PE, V, S, G, SP)], "switches", len(switches))
        SP.wait(((s_out, s_out.n), *((c, c.n) for c in s_dr)))

        block = ctx.enter_context(nc.Block())

        @block.sync
        def _(eng):
            SP.play(eng)

        @block.tensor
        def _(eng):
            PE.play(eng)

        @block.vector
        def _(eng):
            V.play(eng)

        @block.scalar
        def _(eng):
            S.play(eng)

        @block.gpsimd
        def _(eng):
            G.play(eng)


def layout(i):
    k = np.arange(128)
    c = {}
    eye = np.eye(128, dtype=np.float32)
    c["ident"], c["ones"], c["avg"] = eye, np.ones((128, 128)), np.full((128, 128), 1 / 128)
    c["cen"] = eye - np.float32(1 / 128)
    c["cenh"] = (eye - np.float32(1 / 128)) * np.float32(0.5)
    c["upper"] = k[:, None] <= k[None, :]
    c["rev8"], c["rev16"] = np.tile(8 - np.arange(8), (128, 1)), np.tile(16 - np.arange(16), (128, 1))
    c["mq"] = np.where(k[None, :] > k[:, None], NEG, 0.0)
    c["mt"] = np.where(k[:, None] > k[None, :], NEG, 0.0)
    c["bd8"] = (k[:, None] // 8 == k[None, :] // 8) / 8
    c["selbc"] = np.arange(96)[:, None] % 32 == np.arange(32)[None, :]
    c["sel16"] = np.arange(48)[:, None] % 16 == np.arange(16)[None, :]
    c["sel8"] = np.arange(24)[:, None] % 8 == np.arange(8)[None, :]
    c["wr"], c["wk"], c["wv"] = i["L0_ffn_W_r"].T, i["L0_ffn_W_k"].T, i["L0_ffn_W_v"].T
    c["mur"], c["muk"] = i["L0_ffn_mu_r"][:, None], i["L0_ffn_mu_k"][:, None]
    c["win"], c["wn"] = i["L0_attn_W_in"], i["L0_attn_w_norm"][:, None]
    c["bin"] = i["L0_attn_b_in"].reshape(3, 32).T
    c["wx"], c["bx"] = i["L0_attn_W_x"], i["L0_attn_b_x"][:, None]
    c["wdt"], c["bdt"] = i["L0_attn_W_dt"], i["L0_attn_b_dt"][:, None]
    c["wout"], c["bout"] = i["L0_attn_W_out"], i["L0_attn_b_out"][:, None]
    c["l1g"], c["l1e"], c["l1b"] = i["L1_ffn_Wg"], i["L1_ffn_We"], i["L1_ffn_be"][:, None]

    def halves(a):
        a = a.reshape(2, 128, -1)
        return np.concatenate([a[0], a[1]], axis=1)

    for p in ("mf_", "mb_"):
        q = f"L1_attn_{p[1]}_"
        c[p + "in"] = i[q + "in_proj"].T
        c[p + "cw"], c[p + "cb"] = halves(i[q + "conv_w"]), halves(i[q + "conv_b"])
        xp = i[q + "x_proj"].T
        c[p + "xp"] = halves(np.concatenate([xp[:, 0:64]] + [xp[:, 64:96]] * 3, axis=1))
        c[p + "dw"], c[p + "db"] = i[q + "dt_w"].T, halves(i[q + "dt_b"])
        c[p + "al"], c[p + "dd"], c[p + "op"] = halves(i[q + "A_log"]), halves(i[q + "D"]), halves(i[q + "out_proj"].T)
    c["lng"], c["lnb"] = i["L1_attn_ln_g"][:, None], i["L1_attn_ln_b"][:, None]
    c["l2r"] = i["L2_ffn_Wr"]
    c["l2g"] = i["L2_ffn_Wg"].transpose(1, 0, 2).reshape(128, 1024)
    c["l2u"] = i["L2_ffn_Wu"].transpose(1, 0, 2).reshape(128, 1024)
    c["l2d"] = i["L2_ffn_Wd"].reshape(8, 128, 128).transpose(1, 0, 2).reshape(128, 1024)
    c["sg"], c["su"], c["sd"] = i["L2_ffn_Sg"], i["L2_ffn_Su"], i["L2_ffn_Sd"]
    c["a2q"], c["a2k"], c["a2v"] = i["L2_attn_Wq"].T, i["L2_attn_Wkv"][0:128].T, i["L2_attn_Wkv"][128:256].T
    c["a2o"] = i["L2_attn_Wo"].T
    for j, n in enumerate("qkv"):
        c["a3" + n] = i["L3_attn_Wqkv"][128 * j:128 * j + 128].T
    bq = i["L3_attn_bqkv"]
    c["a3bq"], c["a3bk"], c["a3bv"] = bq[0:128, None], bq[128:256, None], bq[None, 256:384]
    c["a3o"], c["a3bo"] = i["L3_attn_Wo"].T, i["L3_attn_bo"][:, None]
    c["a3wq"], c["a3wk"] = np.tile(i["L3_attn_wq"], 16)[:, None], np.tile(i["L3_attn_wk"], 16)[:, None]
    c["l3g"], c["l3gb"] = i["L3_ffn_gate_W"], i["L3_ffn_gate_b"][None, :]
    c["l3w"] = i["L3_ffn_expert_W"].transpose(1, 0, 2).reshape(128, 1024)
    c["l3b"] = np.tile(i["L3_ffn_expert_b"], (3, 1))
    table = np.zeros((128, WIDTH), np.float32)
    for n, (at, rows, cols) in COLS.items():
        table[0:rows, at:at + cols] = c[n]
    return table, np.concatenate([c[n] for n in PASSING], axis=1).astype(np.float32)


def kernel(**inputs):
    import concourse.bacc as _bacc
    from concourse.bass_utils import run_bass_kernel_spmd as _run

    i = {n: np.asarray(a) for n, a in inputs.items()}
    table, passing = layout(i)
    arrays = {"xin": np.ascontiguousarray(i["L0_attn_x"].transpose(0, 2, 1)), "wts": table, "cst": passing}
    nc = _bacc.Bacc("TRN2", target_bir_lowering=False, num_devices=1)
    xin = nc.dram_tensor("xin", (B, D, T), F32, kind="ExternalInput").ap()
    wts = nc.dram_tensor("wts", (128, WIDTH), F32, kind="ExternalInput").ap()
    cst = nc.dram_tensor("cst", (128, 512), F32, kind="ExternalInput").ap()
    out = nc.dram_tensor("out", (B, D, T), F32, kind="ExternalOutput").ap()
    build(nc, xin, wts, cst, out)
    r = _run(nc, [arrays], core_ids=[0])
    return np.ascontiguousarray(r.results[0]["out"].transpose(0, 2, 1))
```

```python
from contextlib import ExitStack

import numpy as np

import concourse.bass as bass
from concourse import mybir

F32 = mybir.dt.float32
BF16 = mybir.dt.bfloat16
ALU = mybir.AluOpType
ACT = mybir.ActivationFunctionType
AX = mybir.AxisListType

B, T, D = 8, 512, 128
NT = T // 128
PAD = 3
H, DH = 16, 8
NS, DR = 16, 64
NEG = -1e30


GROUPS = [
    [("cen", 128, 128), ("cenh", 128, 128), ("avg", 128, 128), ("ident", 128, 128), ("rev8", 128, 8), ("rev16", 128, 16),
     ("wr", 128, 128), ("wk", 128, 128), ("wv", 128, 128), ("mur", 128, 1), ("muk", 128, 1)],
    [("win", 128, 96), ("wn", 128, 1), ("bin", 32, 3), ("wx", 32, 32), ("bx", 32, 1), ("wdt", 32, 32),
     ("bdt", 32, 1), ("wout", 32, 128), ("bout", 128, 1),
     ("l1g", 128, 8), ("l1e", 128, 128), ("l1b", 128, 1)],
    [(p + n, r, c) for p in ("mf_", "mb_") for n, r, c in
     (("in", 128, 512), ("cw", 128, 8), ("cb", 128, 2), ("xp", 128, 192), ("dw", 64, 256), ("db", 128, 2),
      ("al", 128, 32), ("dd", 128, 2), ("op", 128, 256))] + [("lng", 128, 1), ("lnb", 128, 1)],
    [("l2r", 128, 16), ("sel16", 48, 16), ("l2g", 128, 1024), ("l2u", 128, 1024)],
    [("l2d", 128, 1024), ("sg", 128, 128), ("su", 128, 128), ("sd", 128, 128),
     ("a2q", 128, 128), ("a2k", 128, 128), ("a2v", 128, 128), ("a2o", 128, 128)],
    [("bd8", 128, 128), ("a3q", 128, 128), ("a3k", 128, 128), ("a3v", 128, 128), ("a3bq", 128, 1),
     ("a3bk", 128, 1), ("a3bv", 1, 128), ("a3o", 128, 128), ("a3bo", 128, 1), ("a3wq", 128, 1), ("a3wk", 128, 1),
     ("l3g", 128, 8), ("l3gb", 1, 8), ("sel8", 24, 8), ("l3w", 128, 1024), ("l3b", 24, 128)],
]
PASSING = ["ones", "upper", "mq", "mt"]
COLS = {}
EDGE = [0]
for _g in GROUPS:
    _at = EDGE[-1]
    for _n, _r, _c in _g:
        assert _n not in COLS
        COLS[_n] = (_at, _r, _c)
        _at += _c
    EDGE.append(_at)
WIDTH = EDGE[-1]


NOW = [0.0]
SWITCH = 1.3
PRIO = (3, 2, 0, 1)
EPS = 0.05
CLAIMS = ((3, 4), (2, 3), (2, 2), (2, 2))
CLAIM_D = (2, 3)
N_T, N_H, N_S, N_P, N_RA, N_RB, N_RH = 12, 4, 3, 3, 2, 2, 3
W_M, W_2, W_3, W_S, W_T = 2, 3, 4, 2, 3
GAP, LEFT, LAT = 0.8, 0.4, 0.17
PEN = [0.5, 0.5, 0.0]


def cells(ap):
    n = 1
    for k in ap.shape[1:]:
        n *= k
    return n


def price_pe(a):
    return max(cells(a[0]), 64) * (4 if a[1].dtype == F32 else 1) / 2400


def price_dve(a):
    if len(a) == 2:
        return 0.07 + cells(a[0]) * 1.04e-3
    return 0.07 + cells(a[1]) * 1.04e-3 if len(a) > 2 else 0.1 + cells(a[0]) * 0.8e-3


def price_act(a):
    return 0.1 + cells(a[0]) * 0.84e-3


def price_pool(a):
    return 0.1 + cells(a[0]) * 2.3e-3


class Counter:

    def __init__(self, sem):
        self.sem, self.n, self.at = sem, 0, {}

    def add(self, k):
        self.n += k
        return self, self.n


class Queue:

    def __init__(self, sem, price):
        self.mine, self.ops, self.seen = Counter(sem), [], {}
        self.before = None
        self.price, self.clock, self.busy = price, 0.0, 0.0

    def wait(self, after):
        need = {}
        for c, v in after:
            need[c] = max(v, need.get(c, 0))
        for c, v in need.items():
            if self.seen.get(c, 0) < v:
                self.seen[c] = v
                self.ops.append((c.sem, v))

    def guess(self, after, cost):
        NOW[0] = max([self.clock] + [c.at[v] for c, v in after if v in c.at])
        self.clock = NOW[0] + cost
        self.busy += cost
        return self.clock

    def __call__(self, after, f, *a, **k):
        if self.before:
            self.before(a)
        self.wait(after)
        self.mine.at[self.mine.n + 1] = self.guess(after, self.price(a)) + LAT
        self.ops.append((f, a, k, self.mine.sem, 1))
        return self.mine.add(1)

    def op(self, after, f, *a, **k):
        return self, after, self.price(a), lambda: self(after, f, *a, **k), a

    def op_dma(self, after, counter, f, out, in_):
        return self, after, 0.6, lambda: self.dma(after, counter, f, out, in_), ()

    def plain(self, f, *a):
        self.ops.append((f, a, {}, None, 0))

    def dma(self, after, counter, f, out, in_):
        self.wait(after)
        counter.at[counter.n + 16] = self.guess(after, 0.6) + 2.0
        self.ops.append((f, (out, in_), {}, counter.sem, 16))
        return counter.add(16)

    def play(self, eng):
        for op in self.ops:
            if len(op) == 2:
                eng.wait_ge(*op)
            else:
                f, a, k, sem, inc = op
                ins = f(*a, **k)
                if inc:
                    ins.then_inc(sem, inc)


class Fork:

    def __init__(self, units, width, banks=1, tmps=1):
        self.units, self.width, self.claim = list(units), width, (banks, tmps)


class Slot:

    def __init__(self, ap, pool):
        self.ap, self.free, self.pool = ap, (), pool

    def give(self, *last):
        self.free = last
        self.pool.append(self)


class Pool:
    def __init__(self, aps):
        self.slots = []
        for ap in aps:
            self.slots.append(Slot(ap, self.slots))

    def take(self):
        assert self.slots, "no slot left"
        return self.slots.pop(0)


def build(nc, xin, wts, cst, out):
    ctx = ExitStack()
    with ctx:
        def sb(name, shape, dt=F32):
            return ctx.enter_context(nc.sbuf_tensor(name, shape, dt))

        def sem(name):
            return ctx.enter_context(nc.semaphore(name))

        PE, V, S, G, SP = (Queue(sem("s_" + n), price) for n, price in
                           (("pe", price_pe), ("dve", price_dve), ("act", price_act), ("pool", price_pool),
                            ("sp", None)))
        te, ve, se, ge, sy = nc.tensor, nc.vector, nc.scalar, nc.gpsimd, nc.sync
        TT, TS, STT, RED, SCAN = (ve.tensor_tensor, ve.tensor_scalar, ve.scalar_tensor_tensor,
                                  ve.tensor_reduce, ve.tensor_tensor_scan)
        AF, GT = se.activation, ge.tensor_tensor

        psum = [ctx.enter_context(nc.psum_tensor(f"ps{i}", [128, 512], F32)) for i in range(8)]
        W = sb("W", [128, WIDTH])
        NX = 5
        X = [sb(f"X{b}", [128, T]) for b in range(NX)]
        X = [X[b % NX] for b in range(B)]

        def w(name, lo=0, hi=None):
            at, rows, cols = COLS[name]
            return W[0:rows, at + lo:at + (cols if hi is None else hi)]

        s_w = [Counter(sem(f"s_w{i}")) for i in range(len(GROUPS))]
        s_x = [Counter(sem(f"s_x{b}")) for b in range(B)]
        s_out = Counter(sem("s_out"))
        wl, xl = [], []
        wl.append(SP.dma((), s_w[0], sy.dma_start, W[:, EDGE[0]:EDGE[1]], wts[:, EDGE[0]:EDGE[1]]))
        xl.append(SP.dma((), s_x[0], sy.dma_start, X[0][:, :], xin[0]))
        for i in range(1, len(GROUPS)):
            wl.append(SP.dma((), s_w[i], sy.dma_start, W[:, EDGE[i]:EDGE[i + 1]], wts[:, EDGE[i]:EDGE[i + 1]]))
        for b in range(1, NX):
            xl.append(SP.dma((), s_x[b], sy.dma_start, X[b][:, :], xin[b]))

        def mm(after, o, l, r, start=True, stop=True, skip=False, group=None):
            if group is None:
                return PE.op(after, te.matmul, o, l, r, start=start, stop=stop, skip_group_check=skip)

            def go():
                group[0] += 1
                return PE(after, te.matmul, o, l, r, start=group[0] == 1, stop=group[0] == group[1],
                          skip_group_check=skip)

            return PE, after, PE.price((o, l, r)), go, (o, l, r)

        def tt(after, o, a, b, op):
            return [V.op(after, TT, o, a, b, op), G.op(after, GT, o, a, b, op)]

        def cp(after, o, a):
            return [S.op(after, AF, o, a, ACT.Copy), V.op(after, ve.tensor_copy, o, a)]

        eps = sb("eps", [128, 4])
        e5, e8, e6, one = (eps[:, i:i + 1] for i in range(4))
        for i, val in enumerate((1e-5, 1e-8, 1e-6, 1.0)):
            t_eps = V((), ve.memset, eps[:, i:i + 1], val)
        tiles = [sb(f"tmp{i}", [128, T]) for i in range(N_T)]
        t_c = SP.dma((), Counter(sem("s_c")), sy.dma_start, tiles[0][:, :], cst[:, :])
        wr2, wk2 = sb("wr2", [128, 128]), sb("wk2", [128, 128])
        wr1, wk1, winS = w("wr"), w("wk"), w("win")
        om = sb("om", [128, 2])
        t_mu = V((wl[0],), TS, om[:, 0:1], w("mur"), -1.0, 1.0, ALU.mult, ALU.add)
        t_mu = V((wl[0],), TS, om[:, 1:2], w("muk"), -1.0, 1.0, ALU.mult, ALU.add)
        V((t_mu,), TS, wr2[:, :], wr1, om[:, 0:1], None, ALU.mult)
        t = V((), TS, wk2[:, :], wk1, om[:, 1:2], None, ALU.mult)
        V((t,), TS, wr1, wr1, w("mur"), None, ALU.mult)
        t_l0f = V((t,), TS, wk1, wk1, w("muk"), None, ALU.mult)
        identb, upb, oneb = (sb(n, [128, 128], BF16) for n in ("identb", "upb", "oneb"))
        V((), ve.tensor_copy, identb[:, :], w("ident"))
        ones = sb("ones", [1, 128])
        V((), ve.memset, ones[:, :], 1.0)
        mqb, mtb = sb("mqb", [128, 128], BF16), sb("mtb", [128, 128], BF16)
        for i, to in enumerate((oneb, upb, mqb, mtb)):
            t_cb = V((t_c,), ve.tensor_copy, to[:, :], tiles[0][:, 128 * i:128 * i + 128])
        V((wl[1],), TS, winS[:, :], w("win"), w("wn"), None, ALU.mult)
        nbdt = sb("nbdt", [32, 1])
        t_l0a = V((wl[1],), TS, nbdt[:, :], w("bdt"), -1.0, None, ALU.mult)
        Am = sb("Am", [128, 64])
        sel16, sel8 = sb("sel16_b", [48, 16, 64], BF16), sb("sel8_b", [24, 8], BF16)

        table = [None]

        def table_of(a):
            f = a[2] if len(a) > 2 else None
            return LE if f in (ACT.Exp, ACT.Ln) else SG if f in (ACT.Sigmoid, ACT.Tanh) else SI if f == ACT.Silu else None

        def use(name):
            if table[0] != name:
                table[0] = name
                S.clock += 1.3
                S.plain(se.preload_act_table_set, name)

        LE, SG, SI = "natural_log_exp_and_others", "sigmoid_and_others", "silu_and_others"
        S.before = lambda a: use(table_of(a)) if table_of(a) else None
        S((wl[2],), AF, Am[:, 0:32], w("mf_al"), ACT.Exp)
        t_al = S((), AF, Am[:, 32:64], w("mb_al"), ACT.Exp)
        t_am = V((t_al,), TS, Am[:, :], Am[:, :], -1.0, None, ALU.mult)
        V((wl[3],), ve.tensor_copy, sel16[:, :, :], w("sel16").unsqueeze(2).broadcast_to([48, 16, 64]))
        t_m3 = t_cb
        t_m5 = V((wl[5],), ve.tensor_copy, sel8[:, :], w("sel8"))

        class Shared:
            banks = Pool([p[:, :] for p in psum])
            tmps = Pool([t[:, :] for t in tiles])
            tmps.slots[0].free = (t_cb,)
            for i, slot in enumerate(tmps.slots):
                slot.dma = Counter(sem(f"s_tmp{i}"))
            hs = Pool([sb(f"h{i}", [128, PAD + T]) for i in range(N_H)])
            tz = [V((), ve.memset, s.ap[:, 0:PAD], 0.0) for s in hs.slots][-1]
            small = Pool([sb(f"sm{i}", [128, 308])[:, :] for i in range(3)])
            cb = Pool([sb(f"cb{i}", [128, 192], BF16)[:, :] for i in range(4)])
            cT = Pool([sb(f"cT{i}", [48, 512], BF16)[:, :] for i in range(4)])

        h = Shared

        def rms(h, x, tx, mat, e, use_center=True):
            if use_center:
                A = (yield h.banks)
                t1 = yield mm((*A.free, *tx), A.ap, w(mat), x)
                src = A.ap
            else:
                A, t1, src = None, None, x
            r = (yield h.tmps)
            t2 = yield S.op((*(tx if t1 is None else (t1,)), *r.free), AF, r.ap, src, ACT.Square)
            Bk = (yield h.banks)
            t3 = yield mm((t2, *Bk.free), Bk.ap, w("avg"), r.ap)
            t4 = yield S.op((t3, t_eps), AF, r.ap, Bk.ap, ACT.Ln, bias=e)
            Bk.give(t4)
            t5 = yield S.op((t4,), AF, r.ap, r.ap, ACT.Exp, scale=-0.5)
            return A, r, t5

        def ln(h, x, tx, mat="cen", e=None):
            A, r, t5 = (yield from rms(h, x, tx, mat, e5 if e is None else e))
            o = (yield h.hs)
            t6 = yield V.op((t5, h.tz, *o.free), TT, o.ap[:, PAD:], A.ap, r.ap, ALU.mult)
            A.give(t6)
            r.give(t6)
            return o, t6

        def l0_ffn(h, b, tx):
            x = X[b][:, :]
            hh, th = (yield from ln(h, x, tx))
            hc, hp = hh.ap[:, PAD:], hh.ap[:, PAD - 1:PAD - 1 + T]
            R, K = (yield h.banks), (yield h.banks)
            yield mm((th, t_l0f, *R.free), R.ap, wr1[:, :], hc, stop=False)
            t1 = yield mm((), R.ap, wr2[:, :], hp, start=False)
            yield mm(K.free, K.ap, wk1[:, :], hc, stop=False)
            t2 = yield mm((), K.ap, wk2[:, :], hp, start=False)
            hh.give(t2)
            r, k = (yield h.tmps), (yield h.tmps)
            t4 = yield S.op((t2, *k.free), AF, k.ap, K.ap, ACT.Relu)
            K.give(t4)
            t4 = yield S.op((t4,), AF, k.ap, k.ap, ACT.Square)
            t3 = yield S.op((t1, *r.free), AF, r.ap, R.ap, ACT.Sigmoid)
            R.give(t3)
            Vk = (yield h.banks)
            t5 = yield mm((t4, *Vk.free), Vk.ap, w("wv"), k.ap)
            k.give(t5)
            t6 = yield V.op((t5, t3), STT, r.ap, Vk.ap, 0.5, r.ap, ALU.mult, ALU.mult)
            Vk.give(t6)
            t7 = yield tt((t6,), x, x, r.ap, ALU.add)
            r.give(t7)
            return (t7,)

        def l0_attn(h, b, tx):
            x = X[b][:, :]
            hh, th = (yield from ln(h, x, tx))
            hc = hh.ap[:, PAD:]
            _, r, t5 = (yield from rms(h, hc, (th,), None, e8, use_center=False))
            xn = (yield h.tmps)
            t1 = yield V.op((t5, *xn.free), TT, xn.ap, hc, r.ap, ALU.mult)
            r.give(t1)
            bk = (yield h.banks)
            t = yield mm((t1, t_l0a, *bk.free), bk.ap[0:96, :], winS[:, :], xn.ap)
            xn.give(t)
            u, z, g = (yield h.tmps), (yield h.tmps), (yield h.tmps)
            tu = yield S.op((t, *u.free), AF, u.ap[0:32, :], bk.ap[0:32, :], ACT.Identity, bias=w("bin", 0, 1))
            tz = yield S.op((t, *z.free), AF, z.ap[0:32, :], bk.ap[32:64, :], ACT.Identity, bias=w("bin", 1, 2))
            tg = yield S.op((t, *g.free), AF, g.ap[0:32, :], bk.ap[64:96, :], ACT.Sigmoid, bias=w("bin", 2, 3))
            bk.give(tg)
            U, Z = (yield h.banks), (yield h.banks)
            t1 = yield mm((tu, *U.free), U.ap[0:32, :], w("wx"), u.ap[0:32, :])
            t2 = yield mm((tz, *Z.free), Z.ap[0:32, :], w("wdt"), z.ap[0:32, :])
            tu = yield S.op((t1,), AF, u.ap[0:32, :], U.ap[0:32, :], ACT.Tanh, bias=w("bx"))
            U.give(tu)
            a = (yield h.tmps)
            tz = yield S.op((t2,), AF, z.ap[0:32, :], Z.ap[0:32, :], ACT.Sigmoid, bias=w("bdt"))
            ta = yield S.op((*a.free,), AF, a.ap[0:32, :], Z.ap[0:32, :], ACT.Sigmoid, bias=nbdt[:, :], scale=-1.0)
            Z.give(ta)
            t3 = yield V.op((tu, tz), TT, u.ap[0:32, :], u.ap[0:32, :], z.ap[0:32, :], ALU.mult)
            t4 = yield V.op((t3, ta), SCAN, z.ap[0:32, :], a.ap[0:32, :], u.ap[0:32, :], 0.0, ALU.mult, ALU.add)
            u.give(t4)
            a.give(t4)
            t5 = yield V.op((t4, tg), TT, g.ap[0:32, :], g.ap[0:32, :], z.ap[0:32, :], ALU.mult)
            z.give(t5)
            Y = (yield h.banks)
            t6 = yield mm((t5, *Y.free), Y.ap, w("wout"), g.ap[0:32, :])
            g.give(t6)
            y = (yield h.tmps)
            t7 = yield V.op((t6, *y.free), STT, y.ap, Y.ap, w("bout"), hc, ALU.add, ALU.add)
            Y.give(t7)
            hh.give(t7)
            t8 = yield tt((t7,), x, x, y.ap, ALU.add)
            y.give(t8)
            return (t8,)

        def first_max(sm, e, at, n, rev, after):
            mask = sm[:, at:at + NT * n].rearrange("p (t e) -> p t e", e=n)
            mx = sm[:, at + NT * n:at + NT * n + NT]
            mb = mx.unsqueeze(2).broadcast_to([128, NT, n])
            rb = w(rev).unsqueeze(1).broadcast_to([128, NT, n])
            t = yield V.op(after, RED, mx, e, AX.X, ALU.max)
            t = yield V.op((t,), TT, mask, e, mb, ALU.is_equal)
            t = yield V.op((t,), TT, mask, mask, rb, ALU.mult)
            t = yield V.op((t,), RED, mx, mask, AX.X, ALU.max)
            return mask, (yield V.op((t,), TT, mask, mask, mb, ALU.is_equal))

        def bc(ap, n):
            return ap.unsqueeze(2).broadcast_to([128, NT, n])

        def softmax_rows(h, hc, after, wr, n, sm, bias=None, floor=None):
            L = (yield h.banks)
            for j in range(NT):
                o = L.ap[:, j * n:(j + 1) * n]
                t = yield mm((*after, *L.free), o, hc[:, j * 128:(j + 1) * 128], w(wr), stop=bias is None)
                if bias is not None:
                    t = yield mm((), o, ones[:, :], w(bias), start=False)
            e = sm.ap[:, 0:NT * n].rearrange("p (t e) -> p t e", e=n)
            mx, sums = sm.ap[:, NT * n:NT * n + NT], sm.ap[:, NT * n + NT:NT * n + 2 * NT]
            l3 = L.ap[:, 0:NT * n].rearrange("p (t e) -> p t e", e=n)
            if floor is not None:
                t = yield V.op((t, *sm.free), TS, e, l3, floor, None, ALU.max)
                L.give(t)
                t1 = yield V.op((t,), RED, mx, e, AX.X, ALU.max)
                t2 = yield V.op((t1,), TT, e, e, bc(mx, n), ALU.subtract)
            else:
                t1 = yield V.op((t, *sm.free), RED, mx, l3, AX.X, ALU.max)
                t2 = yield V.op((t1,), TT, e, l3, bc(mx, n), ALU.subtract)
                L.give(t2)
            t3 = yield S.op((t2,), AF, e, e, ACT.Exp)
            t4 = yield V.op((t3,), RED, sums, e, AX.X, ALU.add)
            t5 = yield V.op((t4,), ve.reciprocal, mx, sums)
            return e, mx, t5

        def split_T(h, c, n, after):
            cb, cT = (yield h.cb), (yield h.cT)
            v = cb.ap[:, 0:NT * 3 * n].rearrange("p (t k e) -> p t k e", k=3, e=n)
            t1 = yield V.op((*after, *cb.free), ve.tensor_copy, v[:, :, 0, :], c)
            t2 = yield V.op((t1,), TT, c, c, v[:, :, 0, :], ALU.subtract)
            t3 = yield V.op((t2,), ve.tensor_copy, v[:, :, 1, :], c)
            t4 = yield V.op((t3,), TT, v[:, :, 2, :], c, v[:, :, 1, :], ALU.subtract)
            bk = (yield h.banks)
            pT = bk.ap[0:3 * n, 0:256].bitcast(BF16)
            for j in range(NT):
                t5 = yield PE.op((t4, t_cb, *bk.free), te.transpose, pT[:, j * 128:(j + 1) * 128],
                        cb.ap[:, j * 3 * n:(j + 1) * 3 * n], identb[:, :])
            cb.give(t5)
            t6 = yield V.op((t5, *cT.free), ve.tensor_copy, cT.ap[0:3 * n, :], pT)
            bk.give(t6)
            return cT, t6, t4

        carry = [[sb(f"carry{i}_{k}", [128, 8]) for k in range(2)] for i in range(2)]
        t_carry = [[(V((), ve.memset, carry[i][k][:, :], 0.0),) for k in range(2)] for i in range(2)]

        def l1_ffn(h, b, tx, which):
            x = X[b][:, :]
            hh, th = (yield from ln(h, x, tx))
            hc = hh.ap[:, PAD:]
            sm = (yield h.small)
            Y, y = (yield h.banks), (yield h.tmps)
            t11 = yield mm((th, wl[1], *Y.free), Y.ap, w("l1e"), hc)
            t12 = yield S.op((t11, *y.free), AF, y.ap, Y.ap, ACT.Identity, bias=w("l1b"))
            Y.give(t12)
            e, rec, t1 = (yield from softmax_rows(h, hc, (th, wl[1]), "l1g", 8, sm))
            hh.give(t1)
            mask, t2 = (yield from first_max(sm.ap, e, 64, 8, "rev8", (t1,)))
            mb = (yield h.cb)
            mk = mb.ap[:, 0:32]
            t3 = yield V.op((t2, *mb.free), ve.tensor_copy, mk, sm.ap[:, 64:96])
            C = (yield h.banks)
            for j in range(NT):
                o = C.ap[:, 8 * j:8 * j + 8]
                t4 = yield mm((t3, t_cb, *C.free), o, upb[:, :], mk[:, 8 * j:8 * j + 8], stop=j == 0)
                for i in range(j):
                    t4 = yield mm((), o, oneb[:, :], mk[:, 8 * i:8 * i + 8], start=False, stop=i == j - 1)
            for i in range(NT):
                t4 = yield mm((), C.ap[:, 32:40], oneb[:, :], mk[:, 8 * i:8 * i + 8], start=i == 0, stop=i == NT - 1)
            mb.give(t4)
            old, new = carry[which][b % 2], carry[which][(b + 1) % 2]
            loc = sm.ap[:, 0:32].rearrange("p (t e) -> p t e", e=8)
            t5 = yield V.op((t4, *t_carry[which][b % 2]), TT, loc, C.ap[:, 0:32].rearrange("p (t e) -> p t e", e=8),
                   old[:, :].unsqueeze(1).broadcast_to([128, NT, 8]), ALU.add)
            t6 = yield V.op((), TT, new[:, :], C.ap[:, 32:40], old[:, :], ALU.add)
            t_carry[which][(b + 1) % 2] = (t6,)
            C.give(t6)
            t7 = yield V.op((t5,), STT, loc, loc, 512.0, mask, ALU.is_le, ALU.mult)
            g = sm.ap[:, 128:132]
            t8 = yield V.op((t7,), RED, g, loc, AX.X, ALU.add)
            t9 = yield V.op((t8,), STT, g, g, 0.5, rec, ALU.mult, ALU.mult)
            Gb = (yield h.banks)
            for j in range(NT):
                t10 = yield mm((t9, *Gb.free), Gb.ap[:, j * 128:(j + 1) * 128], g[:, j:j + 1].broadcast_to([128, 128]),
                         w("ident"))
            sm.give(t10)
            t13 = yield V.op((t12, t10), TT, y.ap, y.ap, Gb.ap, ALU.mult)
            Gb.give(t13)
            t14 = yield V.op((t13,), TT, x, x, y.ap, ALU.add)
            y.give(t14)
            return (t14,)

        def two(ap):
            return ap.rearrange("p (g n) -> p g n", g=2)

        def pair(name):
            return sb(name, [128, 2, T])

        m_xi, m_dt, m_du = (Pool([pair(n + "f"), pair(n + "b")]) for n in ("m_xi", "m_dt", "m_du"))
        m_rows = Pool([nc.dram_tensor(f"rows{i}", (32, T), F32, kind="Internal").ap() for i in range(2)])
        for i, slot in enumerate(m_rows.slots):
            slot.dma = Counter(sem(f"s_rows{i}"))
        ring_a = Pool([sb(f"ra{i}", [128, 2 * T]) for i in range(N_RA)])
        t_a0 = [V((), ve.memset, two(s.ap[:, :])[:, :, 0:1], 0.0) for s in ring_a.slots][-1]
        ring_b = Pool([sb(f"rb{i}", [128, 2 * T]) for i in range(N_RB)])
        ring_h = Pool([sb(f"rh{i}", [128, 2 * T]) for i in range(N_RH)])

        def mamba_dir(h, p, src, tsrc):
            k = 0 if p == "mf_" else 1
            xp = (yield ring_b)
            xv = two(xp.ap[:, :])
            xi, dt, du = (yield m_xi), (yield m_dt), (yield m_du)
            c = du
            txp = []
            for m in range(2):
                bk = (yield h.banks)
                t = yield mm((*tsrc, wl[2], *bk.free), bk.ap, w(p + "in", m * 128, m * 128 + 128), src)
                t2 = yield cp((t, *xp.free), xv[:, m, :], bk.ap)
                txp.append(t2)
                bk.give(t2)
            for g in range(2):
                cw = w(p + "cw")
                t = yield V.op((txp[g], *c.free), TS, c.ap[:, g, :], xv[:, g, :], cw[:, 4 * g + 3:4 * g + 4], None,
                               ALU.mult)
                for d in range(1, 4):
                    t = yield V.op((t,), STT, c.ap[:, g, d:], xv[:, g, 0:T - d], cw[:, 4 * g + 3 - d:4 * g + 4 - d],
                                   c.ap[:, g, d:], ALU.mult, ALU.add)
                t = yield S.op((t, *xi.free), AF, xi.ap[:, g, :], c.ap[:, g, :], ACT.Silu, bias=w(p + "cb", g, g + 1))
            txi = t
            xp.give(t)
            Q = (yield h.banks)
            for g in range(2):
                t1 = yield mm((txi, *Q.free), Q.ap[0:96, :], w(p + "xp", g * 96, g * 96 + 96), xi.ap[:, g, :],
                              start=g == 0, stop=g == 1)
            dtr, bc2 = (yield h.tmps), (yield h.tmps)
            tdr = yield cp((t1, *dtr.free), dtr.ap[0:64, :], Q.ap[0:64, :])
            t3 = yield cp((t1, *bc2.free), bc2.ap[64:96, :], Q.ap[64:96, :])
            Q.give(tdr, t3)
            rows = (yield m_rows)
            tbc = yield SP.op_dma((t3, *rows.free), rows.dma, sy.dma_start, rows.ap, bc2.ap[64:96, :])
            bc2.give(tbc)
            for g in range(2):
                bk, a = (yield h.banks), (yield h.tmps)
                db = w(p + "db", g, g + 1)
                t = yield mm((tdr, *bk.free), bk.ap, w(p + "dw", g * 128, g * 128 + 128), dtr.ap[0:64, :])
                t1 = yield S.op((t, *a.free), AF, a.ap, bk.ap, ACT.Abs, bias=db)
                t1 = yield S.op((t1,), AF, a.ap, a.ap, ACT.Exp, scale=-1.0)
                t1 = yield S.op((t1, t_eps), AF, a.ap, a.ap, ACT.Ln, bias=one)
                t2 = yield V.op((t, t1, *dt.free), TS, dt.ap[:, g, :], bk.ap, db, 0.0, ALU.add, ALU.max)
                bk.give(t2)
                t2 = yield V.op((t2,), TT, dt.ap[:, g, :], dt.ap[:, g, :], a.ap, ALU.add)
                a.give(t2)
            dtr.give(t)
            tdu = yield tt((t2, txi), du.ap[:, :, :], dt.ap[:, :, :], xi.ap[:, :, :], ALU.mult)
            for g in range(2):
                ty = yield V.op((tdu,), TS, xi.ap[:, g, :], xi.ap[:, g, :], w(p + "dd", g, g + 1), None, ALU.mult)
            y = [ty]

            def add_up(after, y, hh):
                o, a = xi.ap[:, :, :], two(hh.ap[:, :])

                def go(q, f):
                    y[0] = q((*after, *y), f, o, o, a, ALU.add)
                    return y[0]

                return [(q, (*after, *y), q.price((o, o, a)), lambda q=q, f=f: go(q, f), (o,)) for q, f in ((V, TT), (G, GT))]

            def state(s):
                bs, cs = (yield h.tmps), (yield h.tmps)
                t1 = yield SP.op_dma((tbc, *bs.free), bs.dma, sy.dma_start, bs.ap,
                                     rows.ap[s:s + 1, :].broadcast_to([128, T]))
                t2 = yield SP.op_dma((tbc, *cs.free), cs.dma, sy.dma_start, cs.ap,
                                     rows.ap[16 + s:17 + s, :].broadcast_to([128, T]))
                bb = (yield ring_b)
                tb = yield tt((t1, tdu, *bb.free), two(bb.ap[:, :]), du.ap[:, :, :],
                                bs.ap.unsqueeze(1).broadcast_to([128, 2, T]), ALU.mult)
                bs.give(tb)
                a = (yield ring_a)
                for g in range(2):
                    ta = yield S.op((tdu, t_am, t_a0, *a.free), AF, a.ap[:, g * T + 1:(g + 1) * T], dt.ap[:, g, 1:],
                                    ACT.Exp, scale=Am[:, 32 * k + 16 * g + s:32 * k + 16 * g + s + 1])
                hh = (yield ring_h)
                th = yield V.op((ta, tb, *hh.free), SCAN, hh.ap[:, :], a.ap[:, :], bb.ap[:, :], 0.0, ALU.mult, ALU.add)
                a.give(th)
                bb.give(th)
                tc = yield tt((th, t2), two(hh.ap[:, :]), two(hh.ap[:, :]),
                              cs.ap.unsqueeze(1).broadcast_to([128, 2, T]), ALU.mult)
                cs.give(tc)
                ty = yield add_up((tc,), y, hh)
                hh.give(ty)
                return t1, t2, ta

            ends = yield Fork((state(s) for s in range(NS)), W_M, 1, 2)
            ta = max((e[2] for e in ends), key=lambda x: x[1])
            rows.give(*(t for e in ends for t in e[0:2]))
            du.give(*y)
            for m in range(2):
                bk = (yield h.banks)
                tlast = yield mm((*tsrc, *bk.free), bk.ap, w(p + "in", m * 128 + 256, m * 128 + 384), src)
                tz = yield S.op((tlast, ta), AF, dt.ap[:, m, :], bk.ap, ACT.Silu)
                bk.give(tz)
            t = yield tt((*y, tz), xi.ap[:, :, :], xi.ap[:, :, :], dt.ap[:, :, :], ALU.mult)
            dt.give(t)
            O, s = (yield h.banks), (yield h.tmps)
            for g in range(2):
                t1 = yield mm((t, *O.free), O.ap, w(p + "op", g * 128, g * 128 + 128), xi.ap[:, g, :],
                        start=g == 0, stop=g == 1)
            xi.give(t1)
            t2 = yield S.op((t1, *s.free), AF, s.ap, O.ap, ACT.Sigmoid)
            O.give(t2)
            return p, s, t2, tlast

        def l1_attn(h, b, tx):
            x = X[b][:, :]
            hh, th = (yield from ln(h, x, tx))
            hc = hh.ap[:, PAD:]
            rev = (yield h.tmps)
            tr = yield cp((th, *rev.free), rev.ap[:, :], hc[:, ::-1])
            ends = yield Fork((mamba_dir(h, "mf_", hc, (th,)), mamba_dir(h, "mb_", rev.ap[:, :], (tr,))), 2, *CLAIM_D)
            (_, yb, tb, t_in), (_, yf, tf, _) = sorted(ends, key=lambda e: e[0])
            rev.give(t_in)
            t1 = yield V.op((tf, tb), TT, yf.ap[:, :], yf.ap[:, :], yb.ap[:, ::-1], ALU.add)
            yb.give(t1)
            A, r, t2 = (yield from rms(h, yf.ap[:, :], (t1,), "cenh", e5))
            t3 = yield V.op((t2,), TT, r.ap, A.ap, r.ap, ALU.mult)
            yf.give(t2)
            A.give(t3)
            t4 = yield V.op((t3,), STT, r.ap, r.ap, w("lng"), hc, ALU.mult, ALU.add)
            hh.give(t4)
            t5 = yield V.op((t4,), STT, x, r.ap, w("lnb"), x, ALU.add, ALU.add)
            r.give(t5)
            return (t5,)

        def l2_ffn(h, b, tx):
            x = X[b][:, :]
            hh, th = (yield from ln(h, x, tx))
            hc = hh.ap[:, PAD:]
            sm = (yield h.small)
            def router():
                e, rec, t1 = (yield from softmax_rows(h, hc, (th, wl[3]), "l2r", 16, sm))
                m1, t2 = (yield from first_max(sm.ap, e, 80, 16, "rev16", (t1,)))
                e2 = sm.ap[:, 160:224].rearrange("p (t e) -> p t e", e=16)
                t3 = yield V.op((t2,), STT, e2, m1, -2.0, e, ALU.mult, ALU.add)
                m2, t4 = (yield from first_max(sm.ap, e2, 240, 16, "rev16", (t3,)))
                t5 = yield V.op((t4,), TT, m1, m1, m2, ALU.add)
                t6 = yield V.op((t5,), STT, e, e, 0.5, m1, ALU.mult, ALU.mult)
                t7 = yield V.op((t6,), TT, e, e, bc(rec, 16), ALU.mult)
                cT, tc, ts = (yield from split_T(h, e, 16, (t7,)))
                sm.give(ts)
                for _ in range(8):
                    chosen.slots.append((cT, tc))
                return 0, ts, ts, ts

            chosen = Pool(())
            O = (yield h.banks)
            total = [0, 9]

            def unit(i):
                wg = w("l2g", 128 * i, 128 * i + 128) if i < 8 else w("sg")
                wu = w("l2u", 128 * i, 128 * i + 128) if i < 8 else w("su")
                Gt, g, t4 = (yield h.banks), (yield h.tmps), None
                t1 = yield mm((th, wl[4], *Gt.free), Gt.ap, wg, hc)
                t3 = yield S.op((t1, *g.free), AF, g.ap, Gt.ap, ACT.Silu)
                Gt.give(t3)
                if i < 8:
                    cT, tc = (yield chosen)
                    Cb = (yield h.banks)
                    t4 = yield mm((tc, *Cb.free), Cb.ap, sel16[:, 2 * i:2 * i + 2, :].rearrange("k e f -> k (e f)"),
                                  cT.ap[0:48, :])
                    t3 = yield V.op((t3, t4), TT, g.ap, g.ap, Cb.ap, ALU.mult)
                    Cb.give(t3)
                U = (yield h.banks)
                t2 = yield mm(U.free, U.ap, wu, hc)
                if i < 8:
                    t6 = yield V.op((t3, t2), TT, g.ap, g.ap, U.ap, ALU.mult)
                else:
                    t6 = yield V.op((t3, t2), STT, g.ap, g.ap, 0.5, U.ap, ALU.mult, ALU.mult)
                U.give(t6)
                t7 = yield mm((t6, *O.free), O.ap, w("l2d", 128 * i, 128 * i + 128) if i < 8 else w("sd"), g.ap,
                              group=total)
                g.give(t7)
                return 1, t2, t7, t4 or t2, cT if i < 8 else None

            ends = yield Fork((router(), unit(8), *(unit(i) for i in range(8))), W_2 + 1, 2, 1)
            cT = next(e[4] for e in ends if e[0] and e[4])
            t2, t7, t4 = (max((e[i] for e in ends if e[0]), key=lambda x: x[1]) for i in (1, 2, 3))
            cT.give(t4)
            hh.give(t2)
            t8 = yield V.op((t7,), TT, x, x, O.ap, ALU.add)
            O.give(t8)
            return (t8,)

        def l3_ffn(h, b, tx):
            x = X[b][:, :]
            hh, th = (yield from ln(h, x, tx))
            hc = hh.ap[:, PAD:]
            sm = (yield h.small)
            e, rec, t1 = (yield from softmax_rows(h, hc, (th, wl[5]), "l3g", 8, sm, bias="l3gb", floor=1e-4))
            t1 = yield V.op((t1,), TT, e, e, bc(rec, 8), ALU.mult)
            m1, t2 = (yield from first_max(sm.ap, e, 64, 8, "rev8", (t1,)))
            e2 = sm.ap[:, 112:144].rearrange("p (t e) -> p t e", e=8)
            t3 = yield V.op((t2,), STT, e2, m1, -2.0, e, ALU.mult, ALU.add)
            m2, t4 = (yield from first_max(sm.ap, e2, 160, 8, "rev8", (t3,)))
            t5 = yield V.op((t4,), TT, m1, m1, m2, ALU.add)
            t6 = yield V.op((t5,), STT, e, e, 0.1, m1, ALU.max, ALU.mult)
            t7 = yield V.op((t6,), RED, rec, e, AX.X, ALU.add)
            t7 = yield V.op((t7,), ve.reciprocal, sm.ap[:, 208:212], rec)
            t8 = yield V.op((t7,), STT, e, e, 0.25, bc(sm.ap[:, 208:212], 8), ALU.mult, ALU.mult)
            cT, tc, ts = (yield from split_T(h, e, 8, (t8,)))
            sm.give(ts)
            cf = (yield h.tmps)
            tcf = yield cp((tc, *cf.free), cf.ap[0:24, :], cT.ap[0:24, :])
            O = (yield h.banks)
            total = [0, 9]
            tcf = yield mm((tcf, *O.free), O.ap, w("l3b"), cf.ap[0:24, :], group=total)

            def unit(i):
                Cb, xs = (yield h.banks), (yield h.tmps)
                t1 = yield mm((tc, *Cb.free, t_m5), Cb.ap, sel8[:, i:i + 1].broadcast_to([24, 128]), cT.ap[0:24, :])
                t2 = yield V.op((t1, *xs.free), TT, xs.ap, hc, Cb.ap, ALU.mult)
                Cb.give(t2)
                t3 = yield mm((t2, *O.free), O.ap, w("l3w", 128 * i, 128 * i + 128), xs.ap, group=total)
                xs.give(t3)
                return t1, t2, t3

            ends = yield Fork((unit(i) for i in range(8)), W_3)
            t1, t2, t3 = (max((e[i] for e in ends), key=lambda x: x[1]) for i in range(3))
            cf.give(t3)
            cT.give(t1)
            hh.give(t2)
            t4 = yield V.op((t3,), TT, x, x, O.ap, ALU.add)
            O.give(t4)
            return (t4,)

        Qs, Ks = (Pool([sb(f"{n}s{i}", [128, H // 2, T], BF16) for i in range(2)]) for n in "QK")
        t_ks = [G((), ge.memset, s.ap[:, :, :], 1.0) for s in Ks.slots][-1]
        V9 = Pool([sb(f"V9{i}", [128, NT, H, DH]) for i in range(2)])
        strips = Pool([sb(f"strip{i}", [128, NT, 184]) for i in range(N_S)])
        for slot in strips.slots:
            t = G((), ge.memset, slot.ap[:, :, :], 0.0)
            t_strip = G((t,), ge.memset, slot.ap[:, :, 120:128], 1.0)
        SPL = Pool([sb(f"spl{i}", [128, 3, T], BF16) for i in range(2)])
        Pt = Pool([sb(f"pt{i}", [128, T]) for i in range(N_P)])
        NM = Pool([sb(f"nmax{i}", [128, NT, 8]) for i in range(4)])
        s_st = [[Counter(sem(f"s_st{q}{i}")) for i in range(4 if q < 2 else 8)] for q in range(3)]

        DR = Pool([nc.dram_tensor(f"parts{i}", (3, 128, T), BF16, kind="Internal").ap() for i in range(4)])
        for i, slot in enumerate(DR.slots):
            slot.n = i
        s_dr = [Counter(sem(f"s_dr{i}")) for i in range(4)]

        QB, KB = (0, 0, 0, 1, 1, 2), (0, 1, 2, 0, 1, 0)

        def split3(h, q, tq, st, free, parts, counter):
            sp = (yield SPL)
            t1 = yield cp((tq, *sp.free), sp.ap[:, 0, :], q.ap)
            t2 = yield V.op((t1,), TT, q.ap, q.ap, sp.ap[:, 0, :], ALU.subtract)
            t3 = yield cp((t2,), sp.ap[:, 1, :], q.ap)
            t4 = yield V.op((t3,), TT, sp.ap[:, 2, :], q.ap, sp.ap[:, 1, :], ALU.subtract)
            q.give(t4)
            dr = (yield DR)
            t = yield SP.op_dma((t4, *dr.free), s_dr[dr.n], sy.dma_start, dr.ap.rearrange("k p n -> p k n"), sp.ap[:, :, :])
            sp.give(t)
            for a in range(2):
                for j, part in enumerate(parts):
                    src = dr.ap[part, 64 * a:64 * a + 64, :].rearrange("(i d) n -> d i n", d=DH)
                    t5 = yield SP.op_dma((t, *free), counter, sy.dma_start,
                                st.ap[64 * a + 8 * j:64 * a + 8 * j + 8, :, :], src)
            dr.give(t5)
            return t5

        def attention(h, b, tx, l3):
            x = X[b][:, :]
            n = "a3" if l3 else "a2"
            wt = wl[5] if l3 else wl[4]
            hh, th = (yield from ln(h, x, tx))
            hc = hh.ap[:, PAD:]
            qs, ks, v9 = (yield Qs), (yield Ks), (yield V9)
            slot = b % 2 + 2 * l3

            def queries_or_keys(st, nm, parts, kind):
                bk, q = (yield h.banks), (yield h.tmps)
                t0 = t = yield mm((th, wt, *bk.free), bk.ap, w(n + nm), hc)
                if l3:
                    t = yield S.op((t, *q.free), AF, q.ap, bk.ap, ACT.Identity, bias=w("a3b" + nm))
                    bk.give(t)
                    r = (yield h.tmps)
                    t2 = yield S.op((t, *r.free), AF, r.ap, q.ap, ACT.Square)
                    bk = (yield h.banks)
                    t2 = yield mm((t2, *bk.free), bk.ap, w("bd8"), r.ap)
                    t2 = yield S.op((t2,), AF, r.ap, bk.ap, ACT.Ln, bias=e6)
                    bk.give(t2)
                    t2 = yield S.op((t2,), AF, r.ap, r.ap, ACT.Exp, scale=-0.5)
                    t = yield V.op((t2,), STT, q.ap, q.ap, w("a3w" + nm), r.ap, ALU.mult, ALU.mult)
                    r.give(t)
                else:
                    t = yield S.op((t, *q.free), AF, q.ap, bk.ap, ACT.Copy, scale=DH ** -0.5 if nm == "q" else 1.0)
                    bk.give(t)
                t = yield from split3(h, q, t, st, (*st.free, t_ks), parts, s_st[kind][slot])
                return kind, t0, t

            def values():
                bk = (yield h.banks)
                for j in range(NT):
                    o = bk.ap[:, j * 128:(j + 1) * 128]
                    t = yield mm((th, wt, *bk.free), o, hc[:, j * 128:(j + 1) * 128], w(n + "v"), stop=not l3)
                    if l3:
                        t = yield mm((), o, ones[:, :], w("a3bv"), start=False)
                tv = yield S.op((t, *v9.free), AF, v9.ap[:, :, :, :],
                                bk.ap.rearrange("p (t h d) -> p t h d", t=NT, d=DH), ACT.Copy)
                bk.give(tv)
                return 2, t, tv

            ends = yield Fork((queries_or_keys(qs, "q", QB, 0), queries_or_keys(ks, "k", KB, 1), values()), 3, 1, 2)
            (_, _, tq), (_, _, tk), (_, _, tv) = sorted(ends, key=lambda e: e[0])
            ready = [tq, tk]
            hh.give(max((e[1] for e in ends), key=lambda x: x[1]))
            on = (yield h.tmps)

            def highest(a, i, nmx):
                for qt in range(NT):
                    nk = T if l3 else 128 * (qt + 1)
                    bk = (yield h.banks)
                    t = yield mm((*ready, *bk.free), bk.ap[:, 0:nk], qs.ap[a:a + 48, i, 128 * qt:128 * qt + 128],
                                 ks.ap[a:a + 48, i, 0:nk])
                    if not l3:
                        t = yield mm((t_m3,), bk.ap[:, nk - 128:nk], identb[:, :], mqb[:, :], start=False, skip=True)
                    t1 = yield V.op((t, *nmx.free), RED, nmx.ap[:, qt, i:i + 1], bk.ap[:, 0:nk], AX.X, ALU.max,
                                    negate=True)
                    bk.give(t1)
                return t1

            def head(a, i, tq, O, total):
                st = (yield strips)
                ts = yield G.op((tv, t_strip, *st.free), ge.tensor_copy, st.ap[:, :, 56:64],
                                v9.ap[:, :, a // 8 + i, :])
                for kt in range(NT):
                    q0 = 0 if l3 else 128 * kt
                    bk, P = (yield h.banks), (yield Pt)
                    t = yield mm((*tq, *bk.free), bk.ap[:, 0:T - q0], ks.ap[a:a + 51, i, 128 * kt:128 * kt + 128],
                                 qs.ap[a:a + 51, i, q0:T])
                    if not l3:
                        t = yield mm((), bk.ap[:, 0:128], identb[:, :], mtb[:, :], start=False, skip=True)
                    t1 = yield S.op((t, *P.free), AF, P.ap[:, q0:T], bk.ap[:, 0:T - q0], ACT.Exp)
                    bk.give(t1)
                    t2 = yield mm((t1, ts, *O.free), O.ap[:, q0:T], st.ap[:, kt, 56 - 8 * i:184 - 8 * i],
                                  P.ap[:, q0:T], group=total, skip=True)
                    P.give(t2)
                st.give(t2)
                return ts, t, t2

            def half(a):
                nmx = (yield NM)
                ends = yield Fork((highest(a, i, nmx) for i in range(8)), W_S, tmps=0)
                t1 = max(ends, key=lambda x: x[1])
                cT, t2, t3 = (yield from split_T(h, nmx.ap[:, :, :], 8, (t1,)))
                nmx.give(t3)
                for j in range(3):
                    r = a + 48 + j
                    tq = yield SP.op_dma((t2, *qs.free), s_st[2][2 * slot + a // 64], sy.dma_start,
                                         qs.ap[r:r + 1, :, :], cT.ap[8 * j:8 * j + 8, :])
                cT.give(tq)
                O = (yield h.banks)
                total = [0, 8 * NT]
                ends = yield Fork((head(a, i, (tq, *ready), O, total) for i in range(8)), W_T, tmps=0)
                ts, t, t2 = (max((e[i] for e in ends), key=lambda x: x[1]) for i in range(3))
                rd = (yield h.tmps)
                t1 = yield S.op((t2, *rd.free), AF, rd.ap[0:64, :], O.ap[64:128, :], ACT.Ln,
                                bias=0.0 if l3 else eps[64:128, 1:2])
                t1 = yield S.op((t1,), AF, rd.ap[0:64, :], rd.ap[0:64, :], ACT.Exp, scale=-1.0)
                t1 = yield V.op((t1, *on.free), TT, on.ap[a:a + 64, :], O.ap[0:64, :], rd.ap[0:64, :], ALU.mult)
                O.give(t1)
                rd.give(t1)
                return ts, t, t1

            ends = yield Fork((half(0), half(64)), 2, 2, 1)
            ts, t, t1 = (max((e[i] for e in ends), key=lambda x: x[1]) for i in range(3))
            qs.give(t)
            ks.give(t)
            v9.give(ts)
            bk = (yield h.banks)
            t = yield mm((t1, *bk.free), bk.ap, w(n + "o"), on.ap)
            on.give(t)
            if l3:
                t = yield V.op((t,), STT, x, bk.ap, w("a3bo"), x, ALU.add, ALU.add)
            else:
                t = yield V.op((t,), TT, x, x, bk.ap, ALU.add)
            bk.give(t)
            return (t,)

        def part1(b, t):
            t = yield from l0_ffn(h, b, (xl[b], wl[0]))
            t = yield from l0_attn(h, b, t)
            t = yield from l0_ffn(h, b, t)
            return (yield from l1_ffn(h, b, t, 0))

        def part2(b, t):
            t = yield from l1_attn(h, b, t)
            return (yield from l1_ffn(h, b, t, 1))

        def part3(b, t):
            t = yield from l2_ffn(h, b, t)
            t = yield from attention(h, b, t, False)
            return (yield from l2_ffn(h, b, t))

        def part4(b, t):
            t = yield from l3_ffn(h, b, t)
            t = yield from attention(h, b, t, True)
            t = yield from l3_ffn(h, b, t)
            t = SP.dma(t, s_out, sy.dma_start, out[b], X[b][:, :])
            if b + NX < B:
                xl.append(SP.dma((t,), s_x[b + NX], sy.dma_start, X[b][:, :], xin[b + NX]))
            return t

        parts = [part1, part2, part3, part4]
        row_a, row_b = (slot.dma for slot in m_rows.slots)
        pools = (h.banks, h.tmps)
        size = [len(pool.slots) for pool in pools]
        strands = []

        class Strand:

            def __init__(self, gen, claim, rank, parent=None):
                self.gen, self.claim, self.rank, self.parent = gen, claim, rank, parent
                self.wish, self.branch, self.kids, self.value = None, None, 0, None
                self.held = ([], [])
                strands.append(self)
                self.step(None)

            def step(self, value):
                try:
                    self.wish = self.gen.send(value)
                except StopIteration as stop:
                    strands.remove(self)
                    self.wish, self.value = None, stop.value
                    self.rank[1](stop.value)
                    return
                if isinstance(self.wish, Fork):
                    self.branch, self.ends, self.todo = self.wish, [], list(self.wish.units)
                    self.left = len(self.todo)

            def more(self):
                while self.kids < self.branch.width and self.todo:
                    self.kids += 1
                    Strand(self.todo.pop(0), self.branch.claim, (self.rank[0], self.ended), self)

            def ended(self, value):
                self.kids -= 1
                self.left -= 1
                self.ends.append(value)

        def safe(n, s):
            for x in strands:
                x.have = len(x.held[n]) + (x is s)
            left, todo = size[n] - sum(x.have for x in strands), list(strands)
            while todo:
                ends = [x for x in todo if not any(y.parent is x for y in todo)
                        and max(x.claim[n] - x.have, x.branch.claim[n] if x.branch else 0) <= left]
                if left < 0 or not ends:
                    return False
                for x in ends:
                    left += x.have
                    todo.remove(x)
            return True

        lean = {V: PEN[0], S: PEN[1], G: PEN[2]}
        at, on_way, result = [0] * 4, [False] * 4, {}

        def start_of(o):
            q, after, cost, _, a = o
            t = max([q.clock] + [c.at[v] for c, v in after if v in c.at])
            if q is S and table_of(a) not in (None, table[0]):
                t += SWITCH
            return t

        def keep_warm(gap):
            def free_at(bank):
                return max([PE.clock] + [c.at[v] for c, v in bank.free if v in c.at])

            if gap > GAP and h.banks.slots:
                bank = min(h.banks.slots, key=free_at)
                for _ in range(int((gap + PE.clock - free_at(bank) - LEFT) * 2400 / T)):
                    PE((*bank.free, t_cb), te.matmul, bank.ap, identb[:, :],
                       oneb[:, :].unsqueeze(1).broadcast_to([128, NT, 128]), start=True, stop=True)

        def finish(p):
            def end(value):
                result[p, at[p]] = value
                at[p] += 1
                on_way[p] = False
            return end

        while any(n < B for n in at):
            busy = True
            while busy:
                busy = False
                for p in range(4):
                    b = at[p]
                    if not on_way[p] and b < B and (b < len(xl) and b < at[3] + NX and b <= at[1] + 1 if p == 0
                                                    else (p - 1, b) in result):
                        on_way[p] = busy = True
                        Strand(parts[p](b, result.get((p - 1, b))), CLAIMS[p], (p, finish(p)))
                for s in list(strands):
                    if isinstance(s.wish, Fork):
                        if s.left == 0:
                            s.branch = None
                            busy = True
                            s.step(s.ends)
                        elif s.kids < s.branch.width and s.todo:
                            busy = True
                            s.more()
                    elif isinstance(s.wish, Pool) and s.wish.slots:
                        pool = s.wish
                        if pool in pools:
                            n = pools.index(pool)
                            for x in strands:
                                x.held[n][:] = [y for y in x.held[n] if y not in pool.slots]
                            if not safe(n, s):
                                continue
                            slot = pool.take()
                            s.held[n].append(slot)
                        else:
                            slot = pool.take()
                        busy = True
                        s.step(slot)
            can = [s for s in strands if isinstance(s.wish, (tuple, list))]
            if not can and all(n == B for n in at):
                break
            assert can, ("the strands block each other", [(s.rank[0], type(s.wish)) for s in strands])
            first = {}
            for s in can:
                s.pick = s.wish if isinstance(s.wish, tuple) else min(s.wish, key=lambda o: start_of(o) + o[2] + lean[o[0]])
                s.at = start_of(s.pick)
                q = s.pick[0]
                first[q] = min(first.get(q, s.at), s.at)
            s = min(can, key=lambda s: (first[s.pick[0]], s.at > first[s.pick[0]] + EPS, PRIO[s.rank[0]], s.at))
            if s.pick[0] is PE:
                keep_warm(s.at - PE.clock)
            s.step(s.pick[3]())
        SP.wait(((s_out, s_out.n), *((c, c.n) for c in s_dr), (row_a, row_a.n), (row_b, row_b.n)))

        block = ctx.enter_context(nc.Block())

        @block.sync
        def _(eng):
            SP.play(eng)

        @block.tensor
        def _(eng):
            PE.play(eng)

        @block.vector
        def _(eng):
            V.play(eng)

        @block.scalar
        def _(eng):
            S.play(eng)

        @block.gpsimd
        def _(eng):
            G.play(eng)


def layout(i):
    k = np.arange(128)
    c = {}
    eye = np.eye(128, dtype=np.float32)
    c["ident"], c["ones"], c["avg"] = eye, np.ones((128, 128)), np.full((128, 128), 1 / 128)
    c["cen"] = eye - np.float32(1 / 128)
    c["cenh"] = (eye - np.float32(1 / 128)) * np.float32(0.5)
    c["upper"] = k[:, None] <= k[None, :]
    c["rev8"], c["rev16"] = np.tile(8 - np.arange(8), (128, 1)), np.tile(16 - np.arange(16), (128, 1))
    c["mq"] = np.where(k[None, :] > k[:, None], NEG, 0.0)
    c["mt"] = np.where(k[:, None] > k[None, :], NEG, 0.0)
    c["bd8"] = (k[:, None] // 8 == k[None, :] // 8) / 8
    c["sel16"] = np.arange(48)[:, None] % 16 == np.arange(16)[None, :]
    c["sel8"] = np.arange(24)[:, None] % 8 == np.arange(8)[None, :]
    c["wr"], c["wk"], c["wv"] = i["L0_ffn_W_r"].T, i["L0_ffn_W_k"].T, i["L0_ffn_W_v"].T
    c["mur"], c["muk"] = i["L0_ffn_mu_r"][:, None], i["L0_ffn_mu_k"][:, None]
    c["win"], c["wn"] = i["L0_attn_W_in"], i["L0_attn_w_norm"][:, None]
    c["bin"] = i["L0_attn_b_in"].reshape(3, 32).T
    c["wx"], c["bx"] = i["L0_attn_W_x"], i["L0_attn_b_x"][:, None]
    c["wdt"], c["bdt"] = i["L0_attn_W_dt"], i["L0_attn_b_dt"][:, None]
    c["wout"], c["bout"] = i["L0_attn_W_out"], i["L0_attn_b_out"][:, None]
    c["l1g"], c["l1e"], c["l1b"] = i["L1_ffn_Wg"], i["L1_ffn_We"], i["L1_ffn_be"][:, None]

    def halves(a):
        a = a.reshape(2, 128, -1)
        return np.concatenate([a[0], a[1]], axis=1)

    for p in ("mf_", "mb_"):
        q = f"L1_attn_{p[1]}_"
        c[p + "in"] = i[q + "in_proj"].T
        c[p + "cw"], c[p + "cb"] = halves(i[q + "conv_w"]), halves(i[q + "conv_b"])
        c[p + "xp"] = halves(i[q + "x_proj"].T)
        c[p + "dw"], c[p + "db"] = i[q + "dt_w"].T, halves(i[q + "dt_b"])
        c[p + "al"], c[p + "dd"], c[p + "op"] = halves(i[q + "A_log"]), halves(i[q + "D"]), halves(i[q + "out_proj"].T)
    c["lng"], c["lnb"] = i["L1_attn_ln_g"][:, None], i["L1_attn_ln_b"][:, None]
    c["l2r"] = i["L2_ffn_Wr"]
    c["l2g"] = i["L2_ffn_Wg"].transpose(1, 0, 2).reshape(128, 1024)
    c["l2u"] = i["L2_ffn_Wu"].transpose(1, 0, 2).reshape(128, 1024)
    c["l2d"] = i["L2_ffn_Wd"].reshape(8, 128, 128).transpose(1, 0, 2).reshape(128, 1024)
    c["sg"], c["su"], c["sd"] = i["L2_ffn_Sg"], i["L2_ffn_Su"], i["L2_ffn_Sd"]
    c["a2q"], c["a2k"], c["a2v"] = i["L2_attn_Wq"].T, i["L2_attn_Wkv"][0:128].T, i["L2_attn_Wkv"][128:256].T
    c["a2o"] = i["L2_attn_Wo"].T
    for j, n in enumerate("qkv"):
        c["a3" + n] = i["L3_attn_Wqkv"][128 * j:128 * j + 128].T
    bq = i["L3_attn_bqkv"]
    c["a3bq"], c["a3bk"], c["a3bv"] = bq[0:128, None], bq[128:256, None], bq[None, 256:384]
    c["a3o"], c["a3bo"] = i["L3_attn_Wo"].T, i["L3_attn_bo"][:, None]
    c["a3wq"], c["a3wk"] = np.tile(i["L3_attn_wq"], 16)[:, None], np.tile(i["L3_attn_wk"], 16)[:, None]
    c["l3g"], c["l3gb"] = i["L3_ffn_gate_W"], i["L3_ffn_gate_b"][None, :]
    c["l3w"] = i["L3_ffn_expert_W"].transpose(1, 0, 2).reshape(128, 1024)
    c["l3b"] = np.tile(i["L3_ffn_expert_b"], (3, 1))
    table = np.zeros((128, WIDTH), np.float32)
    for n, (at, rows, cols) in COLS.items():
        table[0:rows, at:at + cols] = c[n]
    return table, np.concatenate([c[n] for n in PASSING], axis=1).astype(np.float32)


def kernel(**inputs):
    import concourse.bacc as _bacc
    from concourse.bass_utils import run_bass_kernel_spmd as _run

    i = {n: np.asarray(a) for n, a in inputs.items()}
    table, passing = layout(i)
    arrays = {"xin": np.ascontiguousarray(i["L0_attn_x"].transpose(0, 2, 1)), "wts": table, "cst": passing}
    nc = _bacc.Bacc("TRN2", target_bir_lowering=False, num_devices=1)
    xin = nc.dram_tensor("xin", (B, D, T), F32, kind="ExternalInput").ap()
    wts = nc.dram_tensor("wts", (128, WIDTH), F32, kind="ExternalInput").ap()
    cst = nc.dram_tensor("cst", (128, 512), F32, kind="ExternalInput").ap()
    out = nc.dram_tensor("out", (B, D, T), F32, kind="ExternalOutput").ap()
    build(nc, xin, wts, cst, out)
    r = _run(nc, [arrays], core_ids=[0])
    return np.ascontiguousarray(r.results[0]["out"].transpose(0, 2, 1))
```
